# Optimizing a Trainium2 kernel written in Bass

```python
import numpy as np
import jax
import jax.numpy as jnp

def _softmax(x, axis=-1):
    return jax.nn.softmax(x, axis=axis)

def _gelu(x):
    return jax.nn.gelu(x, approximate=True)

def _silu(x):
    return jax.nn.silu(x)

def _sigmoid(x):
    return jax.nn.sigmoid(x)

def _layernorm(x, axis=-1, eps=1e-05):
    m = jnp.mean(x, axis=axis, keepdims=True)
    v = jnp.var(x, axis=axis, keepdims=True)
    return (x - m) / jnp.sqrt(v + eps)

def _scatter_add(tgt, idx, src, axis=0):
    return tgt.at[idx].add(src)

def _segment_sum(src, seg, n):
    return jax.ops.segment_sum(src, seg, n)
kernel_name = 'mk_hybrid_d4_jaxref_r8_a80473'

def setup_inputs(seed: int=0):
    np.random.seed(seed)
    _w = jnp.asarray

    def _L0_attn_a_setup():
        import jax, jax.numpy as jnp
        import numpy as np
        DT_MIN, DT_MAX = (0.001, 0.1)
        DT_RANK, D_STATE = (64, 16)

        def _selective_scan(xp, delta, A, Bm, Cm):
            batch, L, d_inner = xp.shape
            d_state = A.shape[1]

            def step(h, inp):
                x_t, dt_t, B_t, C_t = inp
                A_bar = 1.0 + A[None] * dt_t[..., None]
                B_bar = B_t[:, None, :] * dt_t[..., None]
                h = A_bar * h + B_bar * x_t[..., None]
                y_t = jnp.sum(C_t[:, None, :] * h, axis=-1)
                return (h, y_t)
            h0 = jnp.zeros((batch, d_inner, d_state), xp.dtype)
            xs = (jnp.swapaxes(xp, 0, 1), jnp.swapaxes(delta, 0, 1), jnp.swapaxes(Bm, 0, 1), jnp.swapaxes(Cm, 0, 1))
            _, ys = jax.lax.scan(step, h0, xs)
            return jnp.swapaxes(ys, 0, 1)
        key = jax.random.key(seed)
        ks = jax.random.split(key, 8)
        B, L, D_MODEL, D_INNER = (2, 512, 128, 256)
        s = 0.02
        return {'x': jax.random.normal(ks[0], (B, L, D_MODEL), jnp.float32), 'W_in': jax.random.normal(ks[1], (D_MODEL, 2 * D_INNER), jnp.float32) * s, 'W_xproj': jax.random.normal(ks[2], (D_INNER, DT_RANK + 2 * D_STATE), jnp.float32) * s, 'W_dt': jax.random.normal(ks[3], (DT_RANK, D_INNER), jnp.float32) * s, 'b_dt': jax.random.normal(ks[4], (D_INNER,), jnp.float32) * s, 'A_log': jnp.log(jax.random.uniform(ks[5], (D_INNER, D_STATE), jnp.float32) + 0.5), 'D': jnp.ones((D_INNER,), jnp.float32), 'W_out': jax.random.normal(ks[6], (D_INNER, D_MODEL), jnp.float32) * s}
    _L0_attn_a_in = _L0_attn_a_setup()

    def _L0_attn_b_setup():
        import jax, jax.numpy as jnp
        import numpy as np
        import math
        KSIZE = 4
        EPS_NORM = 1e-12
        EPS_LN = 1e-05

        def short_conv(x, w):
            b, l, c = x.shape
            K = w.shape[1]
            xp = jnp.pad(x, ((0, 0), (K - 1, 0), (0, 0)))
            y = x
            for j in range(K):
                y = y + xp[:, j:j + l, :] * w[:, j]
            return y

        def l2norm(x):
            return x * jax.lax.rsqrt(jnp.sum(x * x, axis=-1, keepdims=True) + EPS_NORM)

        def titans_forward(hidden_states, Wq, Wk, Wv, conv_q, conv_k, conv_v, W_init, ln_gamma, ln_beta, Wg, Wo, num_heads=16, chunk_size=16):
            b, l, dim = hidden_states.shape
            h = num_heads
            dk = dim // h
            cs = chunk_size
            nc = l // cs
            q = l2norm(jax.nn.silu(short_conv(hidden_states @ Wq.T, conv_q)).reshape(b, l, h, dk))
            k = l2norm(jax.nn.silu(short_conv(hidden_states @ Wk.T, conv_k)).reshape(b, l, h, dk))
            v = jax.nn.silu(short_conv(hidden_states @ Wv.T, conv_v)).reshape(b, l, h, dk)
            qc = q.reshape(b, nc, cs, h, dk).transpose(1, 0, 2, 3, 4)
            kc = k.reshape(b, nc, cs, h, dk).transpose(1, 0, 2, 3, 4)
            vc = v.reshape(b, nc, cs, h, dk).transpose(1, 0, 2, 3, 4)
            mask = jnp.tril(jnp.ones((cs, cs), q.dtype))
            W0 = jnp.broadcast_to(W_init, (b, h, dk, dk))

            def step(W, chunk):
                q_c, k_c, v_c = chunk
                inter = jnp.einsum('bqhk,bhkv->bqhv', q_c, W)
                qk = jnp.einsum('bqhd,bkhd->bhqk', q_c, k_c) * mask
                intra = jnp.einsum('bhqk,bkhv->bqhv', qk, v_c)
                W_new = W + jnp.einsum('bchk,bchv->bhkv', k_c, v_c)
                return (W_new, inter + intra)
            _, o = jax.lax.scan(step, W0, (qc, kc, vc))
            o = o.transpose(1, 0, 2, 3, 4).reshape(b, l, h, dk)
            mu = jnp.mean(o, axis=-1, keepdims=True)
            var = jnp.mean((o - mu) ** 2, axis=-1, keepdims=True)
            o = (o - mu) * jax.lax.rsqrt(var + EPS_LN) * ln_gamma + ln_beta
            o = o.reshape(b, l, dim)
            gate = hidden_states @ Wg.T
            return o * gate @ Wo.T
        key = jax.random.key(seed)
        ks = jax.random.split(key, 12)
        b, l, dim = (4, 256, 128)
        h = 16
        dk = dim // h
        s = 1.0 / math.sqrt(dim)
        inp = {'hidden_states': jax.random.normal(ks[0], (b, l, dim), jnp.float32), 'Wq': jax.random.normal(ks[1], (dim, dim), jnp.float32) * s, 'Wk': jax.random.normal(ks[2], (dim, dim), jnp.float32) * s, 'Wv': jax.random.normal(ks[3], (dim, dim), jnp.float32) * s, 'conv_q': jax.random.normal(ks[4], (dim, KSIZE), jnp.float32) * 0.1, 'conv_k': jax.random.normal(ks[5], (dim, KSIZE), jnp.float32) * 0.1, 'conv_v': jax.random.normal(ks[6], (dim, KSIZE), jnp.float32) * 0.1, 'W_init': jax.random.normal(ks[7], (1, h, dk, dk), jnp.float32) / math.sqrt(dk), 'ln_gamma': jnp.ones((dk,), jnp.float32), 'ln_beta': jnp.zeros((dk,), jnp.float32), 'Wg': jax.random.normal(ks[8], (dim, dim), jnp.float32) * s, 'Wo': jax.random.normal(ks[9], (dim, dim), jnp.float32) * s}
        return inp
    _L0_attn_b_in = _L0_attn_b_setup()

    def _L0_ffn_setup():
        import jax, jax.numpy as jnp
        import numpy as np
        NUM_EXPERTS = 8
        NUM_LANGS = 4
        TOP_K = 2
        D_MODEL = 128
        EXPERT_SIZE = 512
        B, S = (2, 256)
        key = jax.random.key(seed)
        ks = jax.random.split(key, 6)

        def xavier(k, shape, fan_in, fan_out):
            a = float(np.sqrt(6.0 / (fan_in + fan_out)))
            return jax.random.uniform(k, shape, jnp.float32, -a, a)
        return {'x': jax.random.normal(ks[0], (B, S, D_MODEL), jnp.float32), 'router_w': xavier(ks[1], (NUM_EXPERTS, D_MODEL), D_MODEL, NUM_EXPERTS), 'router_b': jnp.zeros((NUM_EXPERTS,), jnp.float32), 'lang_w': xavier(ks[2], (NUM_LANGS, D_MODEL), D_MODEL, NUM_LANGS), 'lang_b': jnp.zeros((NUM_LANGS,), jnp.float32), 'w1': xavier(ks[3], (NUM_EXPERTS, D_MODEL, EXPERT_SIZE), D_MODEL, EXPERT_SIZE), 'b1': jnp.zeros((NUM_EXPERTS, EXPERT_SIZE), jnp.float32), 'w2': xavier(ks[4], (NUM_EXPERTS, EXPERT_SIZE, D_MODEL), EXPERT_SIZE, D_MODEL), 'b2': jnp.zeros((NUM_EXPERTS, D_MODEL), jnp.float32)}
    _L0_ffn_in = _L0_ffn_setup()

    def _L1_attn_a_setup():
        import jax, jax.numpy as jnp
        import numpy as np

        def _gla_forward(hidden_state, Wq, bq, Wk, bk, Wv, bv, Wg, bg, Wo, bo):
            q = hidden_state @ Wq + bq
            k = jax.nn.sigmoid(hidden_state @ Wk + bk)
            g = jax.nn.sigmoid(hidden_state @ Wg + bg)
            v = hidden_state @ Wv + bv
            B = hidden_state.shape[0]
            K = Wq.shape[1]
            V = Wv.shape[1]
            state0 = jnp.zeros((B, K, V), dtype=hidden_state.dtype)

            def step(state, inp):
                q_t, k_t, g_t, v_t = inp
                state = state * g_t[:, :, None] + k_t[:, :, None] * v_t[:, None, :]
                out_t = jnp.einsum('bkv,bk->bv', state, q_t)
                return (state, out_t)
            xs = (jnp.swapaxes(q, 0, 1), jnp.swapaxes(k, 0, 1), jnp.swapaxes(g, 0, 1), jnp.swapaxes(v, 0, 1))
            final_state, outs = jax.lax.scan(step, state0, xs)
            out = jnp.swapaxes(outs, 0, 1)
            out = out @ Wo + bo
            return (out, final_state)

        def _reference_tuple_inner(hidden_state, Wq, bq, Wk, bk, Wv, bv, Wg, bg, Wo, bo):
            return _gla_forward(hidden_state, Wq, bq, Wk, bk, Wv, bv, Wg, bg, Wo, bo)
        key = jax.random.key(seed)
        ks = jax.random.split(key, 12)
        B, T, H, K, V, O = (8, 256, 128, 32, 32, 128)
        s = 0.02
        return {'hidden_state': jax.random.normal(ks[0], (B, T, H), dtype=jnp.float32), 'Wq': jax.random.normal(ks[1], (H, K), dtype=jnp.float32) * s, 'bq': jax.random.normal(ks[2], (K,), dtype=jnp.float32) * s, 'Wk': jax.random.normal(ks[3], (H, K), dtype=jnp.float32) * s, 'bk': jax.random.normal(ks[4], (K,), dtype=jnp.float32) * s, 'Wv': jax.random.normal(ks[5], (H, V), dtype=jnp.float32) * s, 'bv': jax.random.normal(ks[6], (V,), dtype=jnp.float32) * s, 'Wg': jax.random.normal(ks[7], (H, K), dtype=jnp.float32) * s, 'bg': jax.random.normal(ks[8], (K,), dtype=jnp.float32) * s, 'Wo': jax.random.normal(ks[9], (V, O), dtype=jnp.float32) * s, 'bo': jax.random.normal(ks[10], (O,), dtype=jnp.float32) * s}
    _L1_attn_a_in = _L1_attn_a_setup()

    def _L1_attn_b_setup():
        import jax, jax.numpy as jnp
        import numpy as np
        DIM = 128
        HEADS = 16
        DIM_HEAD = DIM // HEADS
        LATENT = DIM // 4
        SCALE = DIM_HEAD ** (-0.5)
        key = jax.random.key(seed)
        ks = jax.random.split(key, 8)
        B, S = (2, 256)
        init = lambda k, shape, fan_in: jax.random.normal(k, shape, jnp.float32) * fan_in ** (-0.5)
        return {'x': jax.random.normal(ks[0], (B, S, DIM), jnp.float32), 'Wq': init(ks[1], (DIM, DIM), DIM), 'bq': jnp.zeros((DIM,), jnp.float32), 'Wl': init(ks[2], (DIM, LATENT), DIM), 'bl': jnp.zeros((LATENT,), jnp.float32), 'Wk': init(ks[3], (LATENT, DIM), LATENT), 'bk': jnp.zeros((DIM,), jnp.float32), 'Wv': init(ks[4], (LATENT, DIM), LATENT), 'bv': jnp.zeros((DIM,), jnp.float32), 'Wo': init(ks[5], (DIM, DIM), DIM), 'bo': jnp.zeros((DIM,), jnp.float32)}
    _L1_attn_b_in = _L1_attn_b_setup()

    def _L1_ffn_setup():
        import jax, jax.numpy as jnp
        import numpy as np
        DIM = 128
        DEPTH = 2
        HEADS = 8
        DIM_HEAD = 64
        WINDOW = 64
        INNER = HEADS * DIM_HEAD
        HID = int(DIM * 4 * 2 / 3)
        B, N = (2, 1024)
        QK_SCALE = 8.0

        def shift_token(t):
            t1, t2 = jnp.split(t, 2, axis=-1)
            t2 = jnp.pad(t2, ((0, 0), (1, 0), (0, 0)))[:, :-1]
            return jnp.concatenate([t1, t2], axis=-1)

        def l2norm(t):
            return t / jnp.clip(jnp.linalg.norm(t, axis=-1, keepdims=True), 1e-12)

        def rotate_half(x):
            x1, x2 = jnp.split(x, 2, axis=-1)
            return jnp.concatenate([-x2, x1], axis=-1)

        def rotary_xpos(q, k):
            n = q.shape[-2]
            half_idx = jnp.arange(0, DIM_HEAD, 2, dtype=jnp.float32)
            inv_freq = 1.0 / 10000.0 ** (half_idx / DIM_HEAD)
            t = jnp.arange(n, dtype=jnp.float32)
            freqs = t[:, None] * inv_freq[None, :]
            freqs = jnp.concatenate([freqs, freqs], axis=-1)
            base = (half_idx + 0.4 * DIM_HEAD) / (1.4 * DIM_HEAD)
            power = (t - n // 2) / float(WINDOW // 2)
            scale = base[None, :] ** power[:, None]
            scale = jnp.concatenate([scale, scale], axis=-1)
            cos, sin = (jnp.cos(freqs), jnp.sin(freqs))
            q = q * cos * scale + rotate_half(q) * sin * scale
            k = k * cos / scale + rotate_half(k) * sin / scale
            return (q, k)

        def local_attention(q, k, v):
            b, h, n, d = q.shape
            w = n // WINDOW
            bq = q.reshape(b, h, w, WINDOW, d) * QK_SCALE
            bk = k.reshape(b, h, w, WINDOW, d)
            bv = v.reshape(b, h, w, WINDOW, d)

            def look_around(t):
                p = jnp.pad(t, ((0, 0), (0, 0), (1, 0), (0, 0), (0, 0)))
                return jnp.concatenate([p[:, :, :w], p[:, :, 1:]], axis=3)
            bk, bv = (look_around(bk), look_around(bv))
            bt = jnp.arange(n).reshape(w, WINDOW)
            btp = jnp.pad(bt, ((1, 0), (0, 0)), constant_values=-1)
            btk = jnp.concatenate([btp[:w], btp[1:]], axis=1)
            sim = jnp.einsum('bhwid,bhwjd->bhwij', bq, bk)
            i = bt[:, :, None]
            j = btk[:, None, :]
            mask = (i < j) | (i > j + WINDOW) | (j == -1)
            sim = jnp.where(mask, -jnp.finfo(sim.dtype).max, sim)
            attn = jax.nn.softmax(sim, axis=-1)
            out = jnp.einsum('bhwij,bhwjd->bhwid', attn, bv)
            return out.reshape(b, h, n, d)

        def _layer(x, wqkv, qs, ksc, wo, lg, lb, w1, b1, w2, b2):
            b, n, _ = x.shape
            h = shift_token(x)
            qkv = h @ wqkv
            q, k, v = jnp.split(qkv, 3, axis=-1)
            to_heads = lambda t: t.reshape(b, n, HEADS, DIM_HEAD).transpose(0, 2, 1, 3)
            q, k, v = (to_heads(q), to_heads(k), to_heads(v))
            q = l2norm(q) * qs
            k = l2norm(k) * ksc
            q, k = rotary_xpos(q, k)
            o = local_attention(q, k, v)
            o = o.transpose(0, 2, 1, 3).reshape(b, n, INNER)
            x = x + o @ wo
            h = shift_token(x)
            mu = h.mean(-1, keepdims=True)
            var = h.var(-1, keepdims=True)
            h = (h - mu) / jnp.sqrt(var + 1e-05) * lg + lb
            h = h @ w1 + b1
            a, g = jnp.split(h, 2, axis=-1)
            h = a * jax.nn.gelu(g, approximate=False)
            x = x + h @ w2 + b2
            return x
        key = jax.random.key(seed)
        ks = jax.random.split(key, 6)
        return {'x': jax.random.normal(ks[0], (B, N, DIM), jnp.float32), 'wqkv': jax.random.normal(ks[1], (DEPTH, DIM, 3 * INNER), jnp.float32) * 0.02, 'q_scale': jnp.ones((DEPTH, DIM_HEAD), jnp.float32), 'k_scale': jnp.ones((DEPTH, DIM_HEAD), jnp.float32), 'wo': jax.random.normal(ks[2], (DEPTH, INNER, DIM), jnp.float32) * 0.02, 'ln_g': jnp.ones((DEPTH, DIM), jnp.float32), 'ln_b': jnp.zeros((DEPTH, DIM), jnp.float32), 'w1': jax.random.normal(ks[3], (DEPTH, DIM, 2 * HID), jnp.float32) * 0.02, 'b1': jnp.zeros((DEPTH, 2 * HID), jnp.float32), 'w2': jax.random.normal(ks[4], (DEPTH, HID, DIM), jnp.float32) * 0.02, 'b2': jnp.zeros((DEPTH, DIM), jnp.float32)}
    _L1_ffn_in = _L1_ffn_setup()

    def _L2_attn_a_setup():
        import jax, jax.numpy as jnp
        from jax import lax
        import numpy as np
        B, L, D_MODEL = (2, 128, 128)
        ED, N, DT_RANK, D_CONV = (256, 16, 64, 4)
        key = jax.random.key(seed)
        ks = jax.random.split(key, 8)
        dt = jnp.exp(jax.random.uniform(ks[6], (ED,)) * (np.log(0.1) - np.log(0.001)) + np.log(0.001))
        dt = jnp.clip(dt, 0.0001, None)
        inv_dt = dt + jnp.log(-jnp.expm1(-dt))
        return {'x': jax.random.normal(ks[0], (B, L, D_MODEL), dtype=jnp.float32), 'in_proj_w': jax.random.normal(ks[1], (D_MODEL, 2 * ED), dtype=jnp.float32) * 0.02, 'conv_w': jax.random.normal(ks[2], (ED, 1, D_CONV), dtype=jnp.float32) * 0.3, 'conv_b': jax.random.normal(ks[3], (ED,), dtype=jnp.float32) * 0.05, 'x_proj_w': jax.random.normal(ks[4], (ED, DT_RANK + 2 * N), dtype=jnp.float32) * 0.02, 'dt_proj_w': jax.random.uniform(ks[5], (DT_RANK, ED), dtype=jnp.float32, minval=-DT_RANK ** (-0.5), maxval=DT_RANK ** (-0.5)), 'dt_proj_b': inv_dt, 'A_log': jnp.log(jnp.tile(jnp.arange(1.0, N + 1.0, dtype=jnp.float32)[None, :], (ED, 1))), 'D': jnp.ones((ED,), dtype=jnp.float32), 'out_proj_w': jax.random.normal(ks[7], (ED, D_MODEL), dtype=jnp.float32) * 0.02}
    _L2_attn_a_in = _L2_attn_a_setup()

    def _L2_attn_b_setup():
        import jax, jax.numpy as jnp
        import numpy as np
        NUM_HEADS = 16
        WINDOW = 32
        HIDDEN = 128
        HEAD_DIM = HIDDEN // NUM_HEADS
        key = jax.random.key(seed)
        ks = jax.random.split(key, 9)
        B, S, H = (2, 256, HIDDEN)
        s = 0.02
        return {'hidden_states': jax.random.normal(ks[0], (B, S, H), jnp.float32), 'Wq': jax.random.normal(ks[1], (H, H), jnp.float32) * s, 'bq': jnp.zeros((H,), jnp.float32), 'Wk': jax.random.normal(ks[2], (H, H), jnp.float32) * s, 'bk': jnp.zeros((H,), jnp.float32), 'Wv': jax.random.normal(ks[3], (H, H), jnp.float32) * s, 'bv': jnp.zeros((H,), jnp.float32), 'Wo': jax.random.normal(ks[4], (H, H), jnp.float32) * s, 'bo': jnp.zeros((H,), jnp.float32)}
    _L2_attn_b_in = _L2_attn_b_setup()

    def _L2_ffn_setup():
        import jax, jax.numpy as jnp
        import numpy as np
        TOP_K = 2

        def _route(x2d, gate_w, num_experts, top_k):
            scores = jax.nn.softmax((x2d @ gate_w.T).astype(jnp.float32), axis=1)
            top_scores, sel = jax.lax.top_k(scores, top_k)
            sel_flat = sel.reshape(-1)
            counts = jnp.bincount(sel_flat, length=num_experts)
            order = jnp.argsort(sel_flat, stable=True)
            top_scores_sorted = top_scores.reshape(-1)[order]
            token_idx = order // top_k
            return (top_scores_sorted, token_idx, counts)

        def _grouped_swiglu(xr, w1, w2, w3, eid):
            out = jnp.zeros((xr.shape[0], w2.shape[-1]), dtype=xr.dtype)
            for e in range(w1.shape[0]):
                xe = jnp.where((eid == e)[:, None], xr, 0.0)
                h = jax.nn.silu(xe @ w1[e]) * (xe @ w3[e])
                out = out + h @ w2[e]
            return out
        key = jax.random.key(seed)
        ks = jax.random.split(key, 5)
        bs, slen, dim, hidden, E = (2, 256, 128, 352, 8)
        x = jax.random.normal(ks[0], (bs, slen, dim), dtype=jnp.float32)
        gate_w = jax.random.normal(ks[1], (E, dim), dtype=jnp.float32) * 0.02
        w1 = jax.random.normal(ks[2], (E, dim, hidden), dtype=jnp.float32) * 0.02
        w2 = jax.random.normal(ks[3], (E, hidden, dim), dtype=jnp.float32) * 0.02
        w3 = jax.random.normal(ks[4], (E, dim, hidden), dtype=jnp.float32) * 0.02
        return {'x': x, 'gate_w': gate_w, 'w1': w1, 'w2': w2, 'w3': w3}
    _L2_ffn_in = _L2_ffn_setup()

    def _L3_attn_a_setup():
        import jax, jax.numpy as jnp
        import numpy as np
        DIM = 128
        NUM_HEADS = 16
        BLK = 128
        TOPK_FRAC = 0.5

        def _sparse_attn(q, k, v, scale):
            B, H, N, d = q.shape
            nB = N // BLK
            topk = max(1, int(TOPK_FRAC * nB))
            qm = q.reshape(B, H, nB, BLK, d).mean(axis=3)
            km = k.reshape(B, H, nB, BLK, d).mean(axis=3)
            sim = jnp.einsum('bhqd,bhkd->bhqk', qm, km)
            _, idx = jax.lax.top_k(sim, topk)
            blk_mask = jax.nn.one_hot(idx, nB, dtype=jnp.float32).sum(axis=-2) > 0
            full_mask = jnp.repeat(jnp.repeat(blk_mask, BLK, axis=-2), BLK, axis=-1)
            scores = jnp.einsum('bhqd,bhkd->bhqk', q, k) * scale
            neg = jnp.asarray(-1000000000.0, scores.dtype)
            scores = jnp.where(full_mask, scores, neg)
            attn = jax.nn.softmax(scores, axis=-1)
            return jnp.einsum('bhqk,bhkd->bhqd', attn, v)
        key = jax.random.key(seed)
        k_x, k_qkv, k_pw, k_pb = jax.random.split(key, 4)
        B, N, C = (1, 512, DIM)
        x = jax.random.normal(k_x, (B, N, C), dtype=jnp.float32)
        qkv_w = jax.random.normal(k_qkv, (3 * C, C), dtype=jnp.float32) * 0.02
        proj_w = jax.random.normal(k_pw, (C, C), dtype=jnp.float32) * 0.02
        proj_b = jax.random.normal(k_pb, (C,), dtype=jnp.float32) * 0.02
        return {'x': x, 'qkv_w': qkv_w, 'proj_w': proj_w, 'proj_b': proj_b}
    _L3_attn_a_in = _L3_attn_a_setup()

    def _L3_attn_b_setup():
        import jax, jax.numpy as jnp
        import numpy as np
        D = 128
        H = 16
        KVH = 4
        HD = D // H
        LAT = 32
        WIN = 32
        B, S = (1, 256)
        BASE_G, BASE_L = (1000000.0, 10000.0)
        EPS = 1e-06

        def rmsnorm(x, w):
            return x * jax.lax.rsqrt(jnp.mean(x * x, axis=-1, keepdims=True) + EPS) * w

        def qk_norm(x):
            return x * jax.lax.rsqrt(jnp.mean(x * x, axis=-1, keepdims=True) + EPS)

        def rope(x, base):
            s, hd = (x.shape[-2], x.shape[-1])
            inv_freq = 1.0 / base ** (jnp.arange(0, hd, 2, dtype=jnp.float32) / hd)
            freqs = jnp.arange(s, dtype=jnp.float32)[:, None] * inv_freq[None, :]
            cos, sin = (jnp.cos(freqs), jnp.sin(freqs))
            xe, xo = (x[..., ::2], x[..., 1::2])
            out = jnp.stack([xe * cos - xo * sin, xe * sin + xo * cos], axis=-1)
            return out.reshape(x.shape)

        def split_heads(x, n_heads):
            b, s, _ = x.shape
            return x.reshape(b, s, n_heads, HD).transpose(0, 2, 1, 3)

        def repeat_kv(x):
            return jnp.repeat(x, H // KVH, axis=1)

        def sdpa(q, k, v, mask):
            scores = jnp.einsum('bhqd,bhkd->bhqk', q, k) / np.sqrt(HD).astype(np.float32)
            scores = jnp.where(mask, scores, jnp.float32(-1e+30))
            probs = jax.nn.softmax(scores, axis=-1)
            return jnp.einsum('bhqk,bhkd->bhqd', probs, v)

        def merge_heads(x):
            b, h, s, hd = x.shape
            return x.transpose(0, 2, 1, 3).reshape(b, s, h * hd)

        def global_latent_attn(x, wq, w_kv_down, w_k_up, w_v_up, wo):
            q = split_heads(x @ wq, H)
            latent = x @ w_kv_down
            k = split_heads(latent @ w_k_up, KVH)
            v = split_heads(latent @ w_v_up, KVH)
            q, k = (rope(q, BASE_G), rope(k, BASE_G))
            q, k = (qk_norm(q), qk_norm(k))
            k, v = (repeat_kv(k), repeat_kv(v))
            i = jnp.arange(x.shape[1])
            causal = i[:, None] >= i[None, :]
            return merge_heads(sdpa(q, k, v, causal)) @ wo

        def local_gqa_attn(x, wq, wk, wv, wo):
            q = split_heads(x @ wq, H)
            k = split_heads(x @ wk, KVH)
            v = split_heads(x @ wv, KVH)
            q, k = (rope(q, BASE_L), rope(k, BASE_L))
            q, k = (qk_norm(q), qk_norm(k))
            k, v = (repeat_kv(k), repeat_kv(v))
            i = jnp.arange(x.shape[1])
            diff = i[:, None] - i[None, :]
            mask = (diff >= 0) & (diff < WIN)
            return merge_heads(sdpa(q, k, v, mask)) @ wo
        key = jax.random.key(seed)
        ks = jax.random.split(key, 12)
        std = 0.02
        return {'hidden': jax.random.normal(ks[0], (B, S, D), dtype=jnp.float32), 'norm1_w': jnp.ones((D,), jnp.float32), 'norm2_w': jnp.ones((D,), jnp.float32), 'g_wq': jax.random.normal(ks[1], (D, H * HD), jnp.float32) * std, 'g_kv_down': jax.random.normal(ks[2], (D, LAT), jnp.float32) * std, 'g_k_up': jax.random.normal(ks[3], (LAT, KVH * HD), jnp.float32) * std, 'g_v_up': jax.random.normal(ks[4], (LAT, KVH * HD), jnp.float32) * std, 'g_wo': jax.random.normal(ks[5], (D, D), jnp.float32) * std, 'l_wq': jax.random.normal(ks[6], (D, H * HD), jnp.float32) * std, 'l_wk': jax.random.normal(ks[7], (D, KVH * HD), jnp.float32) * std, 'l_wv': jax.random.normal(ks[8], (D, KVH * HD), jnp.float32) * std, 'l_wo': jax.random.normal(ks[9], (D, D), jnp.float32) * std}
    _L3_attn_b_in = _L3_attn_b_setup()

    def _L3_ffn_setup():
        import jax, jax.numpy as jnp
        import numpy as np
        B, T, D = (8, 512, 128)
        NUM_SLOTS = 64
        TOP_K = 8
        DQ = D // 4
        DH = D // 2

        def _forward(x, slot_init, w1, b1, w2, b2, tau, Wih, Whh, bih, bhh, wq, bq, wk, bk, wv, bv, ln_g, ln_b, wvp, bvp, wo, bo):
            Bx, Tx, Dx = x.shape
            S = jnp.broadcast_to(slot_init[None], (Bx, NUM_SLOTS, Dx)).astype(x.dtype)
            slot_mean = jnp.broadcast_to(S.mean(axis=1, keepdims=True), (Bx, Tx, Dx))
            ctx = jnp.concatenate([x, slot_mean], axis=-1)
            h = jax.nn.gelu(ctx @ w1 + b1, approximate=False)
            route_logits = (h @ w2 + b2) / (jnp.abs(tau) + 0.1)
            topk_vals, topk_idx = jax.lax.top_k(route_logits, TOP_K)
            topk_w = jax.nn.softmax(topk_vals, axis=-1)
            alpha = (jax.nn.one_hot(topk_idx, NUM_SLOTS, dtype=x.dtype) * topk_w[..., None]).sum(axis=-2)
            slot_input = jnp.einsum('bts,btd->bsd', alpha, x)
            denom = alpha.sum(axis=1) + 1e-08
            si = slot_input / denom[..., None]
            gi = si @ Wih.T + bih
            gh = S @ Whh.T + bhh
            i_r, i_z, i_n = jnp.split(gi, 3, axis=-1)
            h_r, h_z, h_n = jnp.split(gh, 3, axis=-1)
            r = jax.nn.sigmoid(i_r + h_r)
            z = jax.nn.sigmoid(i_z + h_z)
            n = jnp.tanh(i_n + r * h_n)
            S_new = (1.0 - z) * n + z * S
            q = S_new @ wq + bq
            k = S_new @ wk + bk
            v = S_new @ wv + bv
            scale = DQ ** (-0.5)
            attn = jax.nn.softmax(jnp.einsum('bsq,btq->bst', q, k) * scale, axis=-1)
            S_comm = jnp.einsum('bst,btd->bsd', attn, v)
            y = S_new + S_comm
            mu = y.mean(axis=-1, keepdims=True)
            var = y.var(axis=-1, keepdims=True)
            y = (y - mu) * jax.lax.rsqrt(var + 1e-05) * ln_g + ln_b
            slot_values = y @ wvp + bvp
            out = jnp.einsum('bts,bsd->btd', alpha, slot_values)
            return out @ wo + bo
        key = jax.random.key(seed)
        ks = jax.random.split(key, 24)
        n = lambda k, shp, s=0.02: jax.random.normal(k, shp, dtype=jnp.float32) * s
        return {'x': jax.random.normal(ks[0], (B, T, D), dtype=jnp.float32), 'slot_init': n(ks[1], (NUM_SLOTS, D)), 'w1': n(ks[2], (2 * D, DH)), 'b1': jnp.zeros((DH,)), 'w2': n(ks[3], (DH, NUM_SLOTS)), 'b2': jnp.zeros((NUM_SLOTS,)), 'tau': jnp.ones((1,)), 'Wih': n(ks[4], (3 * D, D)), 'Whh': n(ks[5], (3 * D, D)), 'bih': jnp.zeros((3 * D,)), 'bhh': jnp.zeros((3 * D,)), 'wq': n(ks[6], (D, DQ)), 'bq': jnp.zeros((DQ,)), 'wk': n(ks[7], (D, DQ)), 'bk': jnp.zeros((DQ,)), 'wv': n(ks[8], (D, D)), 'bv': jnp.zeros((D,)), 'ln_g': jnp.ones((D,)), 'ln_b': jnp.zeros((D,)), 'wvp': n(ks[9], (D, D)), 'bvp': jnp.zeros((D,)), 'wo': n(ks[10], (D, D)), 'bo': jnp.zeros((D,))}
    _L3_ffn_in = _L3_ffn_setup()
    _d = {'L0_attn_a_x': _L0_attn_a_in['x'], 'L0_attn_a_W_in': _L0_attn_a_in['W_in'], 'L0_attn_a_W_xproj': _L0_attn_a_in['W_xproj'], 'L0_attn_a_W_dt': _L0_attn_a_in['W_dt'], 'L0_attn_a_b_dt': _L0_attn_a_in['b_dt'], 'L0_attn_a_A_log': _L0_attn_a_in['A_log'], 'L0_attn_a_D': _L0_attn_a_in['D'], 'L0_attn_a_W_out': _L0_attn_a_in['W_out'], 'L0_attn_b_Wq': _L0_attn_b_in['Wq'], 'L0_attn_b_Wk': _L0_attn_b_in['Wk'], 'L0_attn_b_Wv': _L0_attn_b_in['Wv'], 'L0_attn_b_conv_q': _L0_attn_b_in['conv_q'], 'L0_attn_b_conv_k': _L0_attn_b_in['conv_k'], 'L0_attn_b_conv_v': _L0_attn_b_in['conv_v'], 'L0_attn_b_W_init': _L0_attn_b_in['W_init'], 'L0_attn_b_ln_gamma': _L0_attn_b_in['ln_gamma'], 'L0_attn_b_ln_beta': _L0_attn_b_in['ln_beta'], 'L0_attn_b_Wg': _L0_attn_b_in['Wg'], 'L0_attn_b_Wo': _L0_attn_b_in['Wo'], 'L0_ffn_router_w': _L0_ffn_in['router_w'], 'L0_ffn_router_b': _L0_ffn_in['router_b'], 'L0_ffn_lang_w': _L0_ffn_in['lang_w'], 'L0_ffn_lang_b': _L0_ffn_in['lang_b'], 'L0_ffn_w1': _L0_ffn_in['w1'], 'L0_ffn_b1': _L0_ffn_in['b1'], 'L0_ffn_w2': _L0_ffn_in['w2'], 'L0_ffn_b2': _L0_ffn_in['b2'], 'L1_attn_a_Wq': _L1_attn_a_in['Wq'], 'L1_attn_a_bq': _L1_attn_a_in['bq'], 'L1_attn_a_Wk': _L1_attn_a_in['Wk'], 'L1_attn_a_bk': _L1_attn_a_in['bk'], 'L1_attn_a_Wv': _L1_attn_a_in['Wv'], 'L1_attn_a_bv': _L1_attn_a_in['bv'], 'L1_attn_a_Wg': _L1_attn_a_in['Wg'], 'L1_attn_a_bg': _L1_attn_a_in['bg'], 'L1_attn_a_Wo': _L1_attn_a_in['Wo'], 'L1_attn_a_bo': _L1_attn_a_in['bo'], 'L1_attn_b_Wq': _L1_attn_b_in['Wq'], 'L1_attn_b_bq': _L1_attn_b_in['bq'], 'L1_attn_b_Wl': _L1_attn_b_in['Wl'], 'L1_attn_b_bl': _L1_attn_b_in['bl'], 'L1_attn_b_Wk': _L1_attn_b_in['Wk'], 'L1_attn_b_bk': _L1_attn_b_in['bk'], 'L1_attn_b_Wv': _L1_attn_b_in['Wv'], 'L1_attn_b_bv': _L1_attn_b_in['bv'], 'L1_attn_b_Wo': _L1_attn_b_in['Wo'], 'L1_attn_b_bo': _L1_attn_b_in['bo'], 'L1_ffn_wqkv': _L1_ffn_in['wqkv'], 'L1_ffn_q_scale': _L1_ffn_in['q_scale'], 'L1_ffn_k_scale': _L1_ffn_in['k_scale'], 'L1_ffn_wo': _L1_ffn_in['wo'], 'L1_ffn_ln_g': _L1_ffn_in['ln_g'], 'L1_ffn_ln_b': _L1_ffn_in['ln_b'], 'L1_ffn_w1': _L1_ffn_in['w1'], 'L1_ffn_b1': _L1_ffn_in['b1'], 'L1_ffn_w2': _L1_ffn_in['w2'], 'L1_ffn_b2': _L1_ffn_in['b2'], 'L2_attn_a_in_proj_w': _L2_attn_a_in['in_proj_w'], 'L2_attn_a_conv_w': _L2_attn_a_in['conv_w'], 'L2_attn_a_conv_b': _L2_attn_a_in['conv_b'], 'L2_attn_a_x_proj_w': _L2_attn_a_in['x_proj_w'], 'L2_attn_a_dt_proj_w': _L2_attn_a_in['dt_proj_w'], 'L2_attn_a_dt_proj_b': _L2_attn_a_in['dt_proj_b'], 'L2_attn_a_A_log': _L2_attn_a_in['A_log'], 'L2_attn_a_D': _L2_attn_a_in['D'], 'L2_attn_a_out_proj_w': _L2_attn_a_in['out_proj_w'], 'L2_attn_b_Wq': _L2_attn_b_in['Wq'], 'L2_attn_b_bq': _L2_attn_b_in['bq'], 'L2_attn_b_Wk': _L2_attn_b_in['Wk'], 'L2_attn_b_bk': _L2_attn_b_in['bk'], 'L2_attn_b_Wv': _L2_attn_b_in['Wv'], 'L2_attn_b_bv': _L2_attn_b_in['bv'], 'L2_attn_b_Wo': _L2_attn_b_in['Wo'], 'L2_attn_b_bo': _L2_attn_b_in['bo'], 'L2_ffn_gate_w': _L2_ffn_in['gate_w'], 'L2_ffn_w1': _L2_ffn_in['w1'], 'L2_ffn_w2': _L2_ffn_in['w2'], 'L2_ffn_w3': _L2_ffn_in['w3'], 'L3_attn_a_qkv_w': _L3_attn_a_in['qkv_w'], 'L3_attn_a_proj_w': _L3_attn_a_in['proj_w'], 'L3_attn_a_proj_b': _L3_attn_a_in['proj_b'], 'L3_attn_b_norm1_w': _L3_attn_b_in['norm1_w'], 'L3_attn_b_norm2_w': _L3_attn_b_in['norm2_w'], 'L3_attn_b_g_wq': _L3_attn_b_in['g_wq'], 'L3_attn_b_g_kv_down': _L3_attn_b_in['g_kv_down'], 'L3_attn_b_g_k_up': _L3_attn_b_in['g_k_up'], 'L3_attn_b_g_v_up': _L3_attn_b_in['g_v_up'], 'L3_attn_b_g_wo': _L3_attn_b_in['g_wo'], 'L3_attn_b_l_wq': _L3_attn_b_in['l_wq'], 'L3_attn_b_l_wk': _L3_attn_b_in['l_wk'], 'L3_attn_b_l_wv': _L3_attn_b_in['l_wv'], 'L3_attn_b_l_wo': _L3_attn_b_in['l_wo'], 'L3_ffn_slot_init': _L3_ffn_in['slot_init'], 'L3_ffn_w1': _L3_ffn_in['w1'], 'L3_ffn_b1': _L3_ffn_in['b1'], 'L3_ffn_w2': _L3_ffn_in['w2'], 'L3_ffn_b2': _L3_ffn_in['b2'], 'L3_ffn_tau': _L3_ffn_in['tau'], 'L3_ffn_Wih': _L3_ffn_in['Wih'], 'L3_ffn_Whh': _L3_ffn_in['Whh'], 'L3_ffn_bih': _L3_ffn_in['bih'], 'L3_ffn_bhh': _L3_ffn_in['bhh'], 'L3_ffn_wq': _L3_ffn_in['wq'], 'L3_ffn_bq': _L3_ffn_in['bq'], 'L3_ffn_wk': _L3_ffn_in['wk'], 'L3_ffn_bk': _L3_ffn_in['bk'], 'L3_ffn_wv': _L3_ffn_in['wv'], 'L3_ffn_bv': _L3_ffn_in['bv'], 'L3_ffn_ln_g': _L3_ffn_in['ln_g'], 'L3_ffn_ln_b': _L3_ffn_in['ln_b'], 'L3_ffn_wvp': _L3_ffn_in['wvp'], 'L3_ffn_bvp': _L3_ffn_in['bvp'], 'L3_ffn_wo': _L3_ffn_in['wo'], 'L3_ffn_bo': _L3_ffn_in['bo']}
    _x0 = _d['L0_attn_a_x']
    _d['L0_attn_a_x'] = jax.random.normal(jax.random.fold_in(jax.random.key(seed), 1), (8, 256, 128), dtype=_x0.dtype)
    del _x0
    return _d

def reference(L0_attn_a_x, L0_attn_a_W_in, L0_attn_a_W_xproj, L0_attn_a_W_dt, L0_attn_a_b_dt, L0_attn_a_A_log, L0_attn_a_D, L0_attn_a_W_out, L0_attn_b_Wq, L0_attn_b_Wk, L0_attn_b_Wv, L0_attn_b_conv_q, L0_attn_b_conv_k, L0_attn_b_conv_v, L0_attn_b_W_init, L0_attn_b_ln_gamma, L0_attn_b_ln_beta, L0_attn_b_Wg, L0_attn_b_Wo, L0_ffn_router_w, L0_ffn_router_b, L0_ffn_lang_w, L0_ffn_lang_b, L0_ffn_w1, L0_ffn_b1, L0_ffn_w2, L0_ffn_b2, L1_attn_a_Wq, L1_attn_a_bq, L1_attn_a_Wk, L1_attn_a_bk, L1_attn_a_Wv, L1_attn_a_bv, L1_attn_a_Wg, L1_attn_a_bg, L1_attn_a_Wo, L1_attn_a_bo, L1_attn_b_Wq, L1_attn_b_bq, L1_attn_b_Wl, L1_attn_b_bl, L1_attn_b_Wk, L1_attn_b_bk, L1_attn_b_Wv, L1_attn_b_bv, L1_attn_b_Wo, L1_attn_b_bo, L1_ffn_wqkv, L1_ffn_q_scale, L1_ffn_k_scale, L1_ffn_wo, L1_ffn_ln_g, L1_ffn_ln_b, L1_ffn_w1, L1_ffn_b1, L1_ffn_w2, L1_ffn_b2, L2_attn_a_in_proj_w, L2_attn_a_conv_w, L2_attn_a_conv_b, L2_attn_a_x_proj_w, L2_attn_a_dt_proj_w, L2_attn_a_dt_proj_b, L2_attn_a_A_log, L2_attn_a_D, L2_attn_a_out_proj_w, L2_attn_b_Wq, L2_attn_b_bq, L2_attn_b_Wk, L2_attn_b_bk, L2_attn_b_Wv, L2_attn_b_bv, L2_attn_b_Wo, L2_attn_b_bo, L2_ffn_gate_w, L2_ffn_w1, L2_ffn_w2, L2_ffn_w3, L3_attn_a_qkv_w, L3_attn_a_proj_w, L3_attn_a_proj_b, L3_attn_b_norm1_w, L3_attn_b_norm2_w, L3_attn_b_g_wq, L3_attn_b_g_kv_down, L3_attn_b_g_k_up, L3_attn_b_g_v_up, L3_attn_b_g_wo, L3_attn_b_l_wq, L3_attn_b_l_wk, L3_attn_b_l_wv, L3_attn_b_l_wo, L3_ffn_slot_init, L3_ffn_w1, L3_ffn_b1, L3_ffn_w2, L3_ffn_b2, L3_ffn_tau, L3_ffn_Wih, L3_ffn_Whh, L3_ffn_bih, L3_ffn_bhh, L3_ffn_wq, L3_ffn_bq, L3_ffn_wk, L3_ffn_bk, L3_ffn_wv, L3_ffn_bv, L3_ffn_ln_g, L3_ffn_ln_b, L3_ffn_wvp, L3_ffn_bvp, L3_ffn_wo, L3_ffn_bo):

    def _L0_attn_a_ref(x, W_in, W_xproj, W_dt, b_dt, A_log, D, W_out):
        import jax, jax.numpy as jnp
        import numpy as np
        DT_MIN, DT_MAX = (0.001, 0.1)
        DT_RANK, D_STATE = (64, 16)

        def _selective_scan(xp, delta, A, Bm, Cm):
            batch, L, d_inner = xp.shape
            d_state = A.shape[1]

            def step(h, inp):
                x_t, dt_t, B_t, C_t = inp
                A_bar = 1.0 + A[None] * dt_t[..., None]
                B_bar = B_t[:, None, :] * dt_t[..., None]
                h = A_bar * h + B_bar * x_t[..., None]
                y_t = jnp.sum(C_t[:, None, :] * h, axis=-1)
                return (h, y_t)
            h0 = jnp.zeros((batch, d_inner, d_state), xp.dtype)
            xs = (jnp.swapaxes(xp, 0, 1), jnp.swapaxes(delta, 0, 1), jnp.swapaxes(Bm, 0, 1), jnp.swapaxes(Cm, 0, 1))
            _, ys = jax.lax.scan(step, h0, xs)
            return jnp.swapaxes(ys, 0, 1)
        xz = x @ W_in
        xp, z = jnp.split(xz, 2, axis=-1)
        x_dbl = xp @ W_xproj
        dlt, Bm, Cm = jnp.split(x_dbl, [DT_RANK, DT_RANK + D_STATE], axis=-1)
        delta = jnp.clip(jax.nn.softplus(dlt @ W_dt + b_dt), DT_MIN, DT_MAX)
        A = -jnp.exp(A_log)
        y = _selective_scan(xp, delta, A, Bm, Cm)
        y = y + D[None, None, :] * xp
        y = y * jax.nn.silu(z)
        return y @ W_out

    def _L0_attn_b_ref(hidden_states, Wq, Wk, Wv, conv_q, conv_k, conv_v, W_init, ln_gamma, ln_beta, Wg, Wo):
        import jax, jax.numpy as jnp
        import numpy as np
        import math
        KSIZE = 4
        EPS_NORM = 1e-12
        EPS_LN = 1e-05

        def short_conv(x, w):
            b, l, c = x.shape
            K = w.shape[1]
            xp = jnp.pad(x, ((0, 0), (K - 1, 0), (0, 0)))
            y = x
            for j in range(K):
                y = y + xp[:, j:j + l, :] * w[:, j]
            return y

        def l2norm(x):
            return x * jax.lax.rsqrt(jnp.sum(x * x, axis=-1, keepdims=True) + EPS_NORM)

        def titans_forward(hidden_states, Wq, Wk, Wv, conv_q, conv_k, conv_v, W_init, ln_gamma, ln_beta, Wg, Wo, num_heads=16, chunk_size=16):
            b, l, dim = hidden_states.shape
            h = num_heads
            dk = dim // h
            cs = chunk_size
            nc = l // cs
            q = l2norm(jax.nn.silu(short_conv(hidden_states @ Wq.T, conv_q)).reshape(b, l, h, dk))
            k = l2norm(jax.nn.silu(short_conv(hidden_states @ Wk.T, conv_k)).reshape(b, l, h, dk))
            v = jax.nn.silu(short_conv(hidden_states @ Wv.T, conv_v)).reshape(b, l, h, dk)
            qc = q.reshape(b, nc, cs, h, dk).transpose(1, 0, 2, 3, 4)
            kc = k.reshape(b, nc, cs, h, dk).transpose(1, 0, 2, 3, 4)
            vc = v.reshape(b, nc, cs, h, dk).transpose(1, 0, 2, 3, 4)
            mask = jnp.tril(jnp.ones((cs, cs), q.dtype))
            W0 = jnp.broadcast_to(W_init, (b, h, dk, dk))

            def step(W, chunk):
                q_c, k_c, v_c = chunk
                inter = jnp.einsum('bqhk,bhkv->bqhv', q_c, W)
                qk = jnp.einsum('bqhd,bkhd->bhqk', q_c, k_c) * mask
                intra = jnp.einsum('bhqk,bkhv->bqhv', qk, v_c)
                W_new = W + jnp.einsum('bchk,bchv->bhkv', k_c, v_c)
                return (W_new, inter + intra)
            _, o = jax.lax.scan(step, W0, (qc, kc, vc))
            o = o.transpose(1, 0, 2, 3, 4).reshape(b, l, h, dk)
            mu = jnp.mean(o, axis=-1, keepdims=True)
            var = jnp.mean((o - mu) ** 2, axis=-1, keepdims=True)
            o = (o - mu) * jax.lax.rsqrt(var + EPS_LN) * ln_gamma + ln_beta
            o = o.reshape(b, l, dim)
            gate = hidden_states @ Wg.T
            return o * gate @ Wo.T
        return titans_forward(hidden_states, Wq, Wk, Wv, conv_q, conv_k, conv_v, W_init, ln_gamma, ln_beta, Wg, Wo)

    def _L0_ffn_ref(x, router_w, router_b, lang_w, lang_b, w1, b1, w2, b2):
        import jax, jax.numpy as jnp
        import numpy as np
        NUM_EXPERTS = 8
        NUM_LANGS = 4
        TOP_K = 2
        D_MODEL = 128
        EXPERT_SIZE = 512
        B, S = (2, 256)
        lang_logits = x @ lang_w.T + lang_b
        lang_probs = jax.nn.softmax(lang_logits, axis=-1)
        lp_pad = jnp.pad(lang_probs, ((0, 0), (0, 0), (0, 1)))
        idx = jnp.arange(NUM_EXPERTS) % NUM_LANGS
        expert_weights = lp_pad[..., idx] + lp_pad[..., idx + 1]
        router_logits = x @ router_w.T + router_b + 0.1 * expert_weights
        router_probs = jax.nn.softmax(router_logits, axis=-1)
        top_p, top_i = jax.lax.top_k(router_probs, TOP_K)
        top_p = top_p / top_p.sum(axis=-1, keepdims=True)
        h = jax.nn.gelu(jnp.einsum('bsd,edh->bseh', x, w1) + b1, approximate=False)
        expert_out = jnp.einsum('bseh,ehd->bsed', h, w2) + b2
        sel = jnp.take_along_axis(expert_out, top_i[..., None], axis=2)
        return (top_p[..., None] * sel).sum(axis=2)

    def _L1_attn_a_ref(hidden_state, Wq, bq, Wk, bk, Wv, bv, Wg, bg, Wo, bo):
        import jax, jax.numpy as jnp
        import numpy as np

        def _gla_forward(hidden_state, Wq, bq, Wk, bk, Wv, bv, Wg, bg, Wo, bo):
            q = hidden_state @ Wq + bq
            k = jax.nn.sigmoid(hidden_state @ Wk + bk)
            g = jax.nn.sigmoid(hidden_state @ Wg + bg)
            v = hidden_state @ Wv + bv
            B = hidden_state.shape[0]
            K = Wq.shape[1]
            V = Wv.shape[1]
            state0 = jnp.zeros((B, K, V), dtype=hidden_state.dtype)

            def step(state, inp):
                q_t, k_t, g_t, v_t = inp
                state = state * g_t[:, :, None] + k_t[:, :, None] * v_t[:, None, :]
                out_t = jnp.einsum('bkv,bk->bv', state, q_t)
                return (state, out_t)
            xs = (jnp.swapaxes(q, 0, 1), jnp.swapaxes(k, 0, 1), jnp.swapaxes(g, 0, 1), jnp.swapaxes(v, 0, 1))
            final_state, outs = jax.lax.scan(step, state0, xs)
            out = jnp.swapaxes(outs, 0, 1)
            out = out @ Wo + bo
            return (out, final_state)

        def _reference_tuple_inner(hidden_state, Wq, bq, Wk, bk, Wv, bv, Wg, bg, Wo, bo):
            return _gla_forward(hidden_state, Wq, bq, Wk, bk, Wv, bv, Wg, bg, Wo, bo)
        return _reference_tuple_inner(hidden_state, Wq, bq, Wk, bk, Wv, bv, Wg, bg, Wo, bo)[0]

    def _L1_attn_b_ref(x, Wq, bq, Wl, bl, Wk, bk, Wv, bv, Wo, bo):
        import jax, jax.numpy as jnp
        import numpy as np
        DIM = 128
        HEADS = 16
        DIM_HEAD = DIM // HEADS
        LATENT = DIM // 4
        SCALE = DIM_HEAD ** (-0.5)
        B, S, D = x.shape
        H, Dh = (HEADS, DIM_HEAD)
        q = (x @ Wq + bq).reshape(B, S, H, Dh)
        latent = x @ Wl + bl
        k = (latent @ Wk + bk).reshape(B, S, H, Dh)
        v = (latent @ Wv + bv).reshape(B, S, H, Dh)
        scores = jnp.einsum('bihd,bjhd->bhij', q, k) * SCALE
        attn = jax.nn.softmax(scores, axis=-1)
        out = jnp.einsum('bhij,bjhd->bihd', attn, v).reshape(B, S, D)
        out = out @ Wo + bo
        return out

    def _L1_ffn_ref(x, wqkv, q_scale, k_scale, wo, ln_g, ln_b, w1, b1, w2, b2):
        import jax, jax.numpy as jnp
        import numpy as np
        DIM = 128
        DEPTH = 2
        HEADS = 8
        DIM_HEAD = 64
        WINDOW = 64
        INNER = HEADS * DIM_HEAD
        HID = int(DIM * 4 * 2 / 3)
        B, N = (2, 1024)
        QK_SCALE = 8.0

        def shift_token(t):
            t1, t2 = jnp.split(t, 2, axis=-1)
            t2 = jnp.pad(t2, ((0, 0), (1, 0), (0, 0)))[:, :-1]
            return jnp.concatenate([t1, t2], axis=-1)

        def l2norm(t):
            return t / jnp.clip(jnp.linalg.norm(t, axis=-1, keepdims=True), 1e-12)

        def rotate_half(x):
            x1, x2 = jnp.split(x, 2, axis=-1)
            return jnp.concatenate([-x2, x1], axis=-1)

        def rotary_xpos(q, k):
            n = q.shape[-2]
            half_idx = jnp.arange(0, DIM_HEAD, 2, dtype=jnp.float32)
            inv_freq = 1.0 / 10000.0 ** (half_idx / DIM_HEAD)
            t = jnp.arange(n, dtype=jnp.float32)
            freqs = t[:, None] * inv_freq[None, :]
            freqs = jnp.concatenate([freqs, freqs], axis=-1)
            base = (half_idx + 0.4 * DIM_HEAD) / (1.4 * DIM_HEAD)
            power = (t - n // 2) / float(WINDOW // 2)
            scale = base[None, :] ** power[:, None]
            scale = jnp.concatenate([scale, scale], axis=-1)
            cos, sin = (jnp.cos(freqs), jnp.sin(freqs))
            q = q * cos * scale + rotate_half(q) * sin * scale
            k = k * cos / scale + rotate_half(k) * sin / scale
            return (q, k)

        def local_attention(q, k, v):
            b, h, n, d = q.shape
            w = n // WINDOW
            bq = q.reshape(b, h, w, WINDOW, d) * QK_SCALE
            bk = k.reshape(b, h, w, WINDOW, d)
            bv = v.reshape(b, h, w, WINDOW, d)

            def look_around(t):
                p = jnp.pad(t, ((0, 0), (0, 0), (1, 0), (0, 0), (0, 0)))
                return jnp.concatenate([p[:, :, :w], p[:, :, 1:]], axis=3)
            bk, bv = (look_around(bk), look_around(bv))
            bt = jnp.arange(n).reshape(w, WINDOW)
            btp = jnp.pad(bt, ((1, 0), (0, 0)), constant_values=-1)
            btk = jnp.concatenate([btp[:w], btp[1:]], axis=1)
            sim = jnp.einsum('bhwid,bhwjd->bhwij', bq, bk)
            i = bt[:, :, None]
            j = btk[:, None, :]
            mask = (i < j) | (i > j + WINDOW) | (j == -1)
            sim = jnp.where(mask, -jnp.finfo(sim.dtype).max, sim)
            attn = jax.nn.softmax(sim, axis=-1)
            out = jnp.einsum('bhwij,bhwjd->bhwid', attn, bv)
            return out.reshape(b, h, n, d)

        def _layer(x, wqkv, qs, ksc, wo, lg, lb, w1, b1, w2, b2):
            b, n, _ = x.shape
            h = shift_token(x)
            qkv = h @ wqkv
            q, k, v = jnp.split(qkv, 3, axis=-1)
            to_heads = lambda t: t.reshape(b, n, HEADS, DIM_HEAD).transpose(0, 2, 1, 3)
            q, k, v = (to_heads(q), to_heads(k), to_heads(v))
            q = l2norm(q) * qs
            k = l2norm(k) * ksc
            q, k = rotary_xpos(q, k)
            o = local_attention(q, k, v)
            o = o.transpose(0, 2, 1, 3).reshape(b, n, INNER)
            x = x + o @ wo
            h = shift_token(x)
            mu = h.mean(-1, keepdims=True)
            var = h.var(-1, keepdims=True)
            h = (h - mu) / jnp.sqrt(var + 1e-05) * lg + lb
            h = h @ w1 + b1
            a, g = jnp.split(h, 2, axis=-1)
            h = a * jax.nn.gelu(g, approximate=False)
            x = x + h @ w2 + b2
            return x
        for l in range(DEPTH):
            x = _layer(x, wqkv[l], q_scale[l], k_scale[l], wo[l], ln_g[l], ln_b[l], w1[l], b1[l], w2[l], b2[l])
        return x

    def _L2_attn_a_ref(x, in_proj_w, conv_w, conv_b, x_proj_w, dt_proj_w, dt_proj_b, A_log, D, out_proj_w):
        import jax, jax.numpy as jnp
        from jax import lax
        import numpy as np
        B, L, D_MODEL = (2, 128, 128)
        ED, N, DT_RANK, D_CONV = (256, 16, 64, 4)
        xz = x @ in_proj_w
        xc, z = jnp.split(xz, 2, axis=-1)
        xt = jnp.transpose(xc, (0, 2, 1))
        xt = lax.conv_general_dilated(xt, conv_w, (1,), [(D_CONV - 1, 0)], dimension_numbers=('NCH', 'OIH', 'NCH'), feature_group_count=ED)
        xt = xt + conv_b[None, :, None]
        xc = jax.nn.silu(jnp.transpose(xt, (0, 2, 1)))
        A = -jnp.exp(A_log)
        dbc = xc @ x_proj_w
        delta, Bm, Cm = jnp.split(dbc, [DT_RANK, DT_RANK + N], axis=-1)
        delta = jax.nn.softplus(delta @ dt_proj_w + dt_proj_b)
        deltaA = jnp.exp(delta[..., None] * A)
        BX = delta[..., None] * Bm[:, :, None, :] * xc[..., None]

        def combine(c1, c2):
            a1, x1 = c1
            a2, x2 = c2
            return (a1 * a2, a2 * x1 + x2)
        _, hs = lax.associative_scan(combine, (deltaA, BX), axis=1)
        y = jnp.einsum('blen,bln->ble', hs, Cm) + D * xc
        y = y * jax.nn.silu(z)
        return y @ out_proj_w

    def _L2_attn_b_ref(hidden_states, Wq, bq, Wk, bk, Wv, bv, Wo, bo):
        import jax, jax.numpy as jnp
        import numpy as np
        NUM_HEADS = 16
        WINDOW = 32
        HIDDEN = 128
        HEAD_DIM = HIDDEN // NUM_HEADS
        B, S, H = hidden_states.shape
        scale = jnp.sqrt(jnp.asarray(HEAD_DIM, hidden_states.dtype))
        q = (hidden_states @ Wq.T + bq).reshape(B, S, NUM_HEADS, HEAD_DIM)
        k = (hidden_states @ Wk.T + bk).reshape(B, S, NUM_HEADS, HEAD_DIM)
        v = (hidden_states @ Wv.T + bv).reshape(B, S, NUM_HEADS, HEAD_DIM)
        scores = jnp.einsum('bihd,bjhd->bhij', q, k) / scale
        blk = jnp.arange(S) // WINDOW
        allowed = blk[:, None] >= blk[None, :]
        scores = jnp.where(allowed, scores, jnp.zeros((), scores.dtype))
        probs = jax.nn.softmax(scores, axis=-1)
        ctx = jnp.einsum('bhij,bjhd->bihd', probs, v).reshape(B, S, H)
        return ctx @ Wo.T + bo

    def _L2_ffn_ref(x, gate_w, w1, w2, w3):
        import jax, jax.numpy as jnp
        import numpy as np
        TOP_K = 2

        def _route(x2d, gate_w, num_experts, top_k):
            scores = jax.nn.softmax((x2d @ gate_w.T).astype(jnp.float32), axis=1)
            top_scores, sel = jax.lax.top_k(scores, top_k)
            sel_flat = sel.reshape(-1)
            counts = jnp.bincount(sel_flat, length=num_experts)
            order = jnp.argsort(sel_flat, stable=True)
            top_scores_sorted = top_scores.reshape(-1)[order]
            token_idx = order // top_k
            return (top_scores_sorted, token_idx, counts)

        def _grouped_swiglu(xr, w1, w2, w3, eid):
            out = jnp.zeros((xr.shape[0], w2.shape[-1]), dtype=xr.dtype)
            for e in range(w1.shape[0]):
                xe = jnp.where((eid == e)[:, None], xr, 0.0)
                h = jax.nn.silu(xe @ w1[e]) * (xe @ w3[e])
                out = out + h @ w2[e]
            return out
        bs, slen, dim = x.shape
        E, top_k = (gate_w.shape[0], TOP_K)
        x2d = x.reshape(bs * slen, dim)
        top_scores, token_idx, counts = _route(x2d, gate_w, E, top_k)
        routed_in = (x2d[token_idx].astype(jnp.float32) * top_scores[:, None]).astype(x.dtype)
        Tr = bs * slen * top_k
        eid = jnp.repeat(jnp.arange(E), counts, total_repeat_length=Tr)
        routed_out = _grouped_swiglu(routed_in, w1, w2, w3, eid)
        out = jnp.zeros((bs * slen, dim), dtype=x.dtype).at[token_idx].add(routed_out)
        return out.reshape(bs, slen, dim)

    def _L3_attn_a_ref(x, qkv_w, proj_w, proj_b):
        import jax, jax.numpy as jnp
        import numpy as np
        DIM = 128
        NUM_HEADS = 16
        BLK = 128
        TOPK_FRAC = 0.5

        def _sparse_attn(q, k, v, scale):
            B, H, N, d = q.shape
            nB = N // BLK
            topk = max(1, int(TOPK_FRAC * nB))
            qm = q.reshape(B, H, nB, BLK, d).mean(axis=3)
            km = k.reshape(B, H, nB, BLK, d).mean(axis=3)
            sim = jnp.einsum('bhqd,bhkd->bhqk', qm, km)
            _, idx = jax.lax.top_k(sim, topk)
            blk_mask = jax.nn.one_hot(idx, nB, dtype=jnp.float32).sum(axis=-2) > 0
            full_mask = jnp.repeat(jnp.repeat(blk_mask, BLK, axis=-2), BLK, axis=-1)
            scores = jnp.einsum('bhqd,bhkd->bhqk', q, k) * scale
            neg = jnp.asarray(-1000000000.0, scores.dtype)
            scores = jnp.where(full_mask, scores, neg)
            attn = jax.nn.softmax(scores, axis=-1)
            return jnp.einsum('bhqk,bhkd->bhqd', attn, v)
        B, N, C = x.shape
        H = NUM_HEADS
        d = C // H
        scale = d ** (-0.5)
        qkv = x @ qkv_w.T
        qkv = qkv.reshape(B, N, 3, H, d).transpose(2, 0, 3, 1, 4)
        q, k, v = (qkv[0], qkv[1], qkv[2])
        o = _sparse_attn(q, k, v, scale)
        o = o.transpose(0, 2, 1, 3).reshape(B, N, C)
        return o @ proj_w.T + proj_b

    def _L3_attn_b_ref(hidden, norm1_w, norm2_w, g_wq, g_kv_down, g_k_up, g_v_up, g_wo, l_wq, l_wk, l_wv, l_wo):
        import jax, jax.numpy as jnp
        import numpy as np
        D = 128
        H = 16
        KVH = 4
        HD = D // H
        LAT = 32
        WIN = 32
        B, S = (1, 256)
        BASE_G, BASE_L = (1000000.0, 10000.0)
        EPS = 1e-06

        def rmsnorm(x, w):
            return x * jax.lax.rsqrt(jnp.mean(x * x, axis=-1, keepdims=True) + EPS) * w

        def qk_norm(x):
            return x * jax.lax.rsqrt(jnp.mean(x * x, axis=-1, keepdims=True) + EPS)

        def rope(x, base):
            s, hd = (x.shape[-2], x.shape[-1])
            inv_freq = 1.0 / base ** (jnp.arange(0, hd, 2, dtype=jnp.float32) / hd)
            freqs = jnp.arange(s, dtype=jnp.float32)[:, None] * inv_freq[None, :]
            cos, sin = (jnp.cos(freqs), jnp.sin(freqs))
            xe, xo = (x[..., ::2], x[..., 1::2])
            out = jnp.stack([xe * cos - xo * sin, xe * sin + xo * cos], axis=-1)
            return out.reshape(x.shape)

        def split_heads(x, n_heads):
            b, s, _ = x.shape
            return x.reshape(b, s, n_heads, HD).transpose(0, 2, 1, 3)

        def repeat_kv(x):
            return jnp.repeat(x, H // KVH, axis=1)

        def sdpa(q, k, v, mask):
            scores = jnp.einsum('bhqd,bhkd->bhqk', q, k) / np.sqrt(HD).astype(np.float32)
            scores = jnp.where(mask, scores, jnp.float32(-1e+30))
            probs = jax.nn.softmax(scores, axis=-1)
            return jnp.einsum('bhqk,bhkd->bhqd', probs, v)

        def merge_heads(x):
            b, h, s, hd = x.shape
            return x.transpose(0, 2, 1, 3).reshape(b, s, h * hd)

        def global_latent_attn(x, wq, w_kv_down, w_k_up, w_v_up, wo):
            q = split_heads(x @ wq, H)
            latent = x @ w_kv_down
            k = split_heads(latent @ w_k_up, KVH)
            v = split_heads(latent @ w_v_up, KVH)
            q, k = (rope(q, BASE_G), rope(k, BASE_G))
            q, k = (qk_norm(q), qk_norm(k))
            k, v = (repeat_kv(k), repeat_kv(v))
            i = jnp.arange(x.shape[1])
            causal = i[:, None] >= i[None, :]
            return merge_heads(sdpa(q, k, v, causal)) @ wo

        def local_gqa_attn(x, wq, wk, wv, wo):
            q = split_heads(x @ wq, H)
            k = split_heads(x @ wk, KVH)
            v = split_heads(x @ wv, KVH)
            q, k = (rope(q, BASE_L), rope(k, BASE_L))
            q, k = (qk_norm(q), qk_norm(k))
            k, v = (repeat_kv(k), repeat_kv(v))
            i = jnp.arange(x.shape[1])
            diff = i[:, None] - i[None, :]
            mask = (diff >= 0) & (diff < WIN)
            return merge_heads(sdpa(q, k, v, mask)) @ wo
        x = hidden
        x = x + global_latent_attn(rmsnorm(x, norm1_w), g_wq, g_kv_down, g_k_up, g_v_up, g_wo)
        x = x + local_gqa_attn(rmsnorm(x, norm2_w), l_wq, l_wk, l_wv, l_wo)
        return x

    def _L3_ffn_ref(x, slot_init, w1, b1, w2, b2, tau, Wih, Whh, bih, bhh, wq, bq, wk, bk, wv, bv, ln_g, ln_b, wvp, bvp, wo, bo):
        import jax, jax.numpy as jnp
        import numpy as np
        B, T, D = (8, 512, 128)
        NUM_SLOTS = 64
        TOP_K = 8
        DQ = D // 4
        DH = D // 2

        def _forward(x, slot_init, w1, b1, w2, b2, tau, Wih, Whh, bih, bhh, wq, bq, wk, bk, wv, bv, ln_g, ln_b, wvp, bvp, wo, bo):
            Bx, Tx, Dx = x.shape
            S = jnp.broadcast_to(slot_init[None], (Bx, NUM_SLOTS, Dx)).astype(x.dtype)
            slot_mean = jnp.broadcast_to(S.mean(axis=1, keepdims=True), (Bx, Tx, Dx))
            ctx = jnp.concatenate([x, slot_mean], axis=-1)
            h = jax.nn.gelu(ctx @ w1 + b1, approximate=False)
            route_logits = (h @ w2 + b2) / (jnp.abs(tau) + 0.1)
            topk_vals, topk_idx = jax.lax.top_k(route_logits, TOP_K)
            topk_w = jax.nn.softmax(topk_vals, axis=-1)
            alpha = (jax.nn.one_hot(topk_idx, NUM_SLOTS, dtype=x.dtype) * topk_w[..., None]).sum(axis=-2)
            slot_input = jnp.einsum('bts,btd->bsd', alpha, x)
            denom = alpha.sum(axis=1) + 1e-08
            si = slot_input / denom[..., None]
            gi = si @ Wih.T + bih
            gh = S @ Whh.T + bhh
            i_r, i_z, i_n = jnp.split(gi, 3, axis=-1)
            h_r, h_z, h_n = jnp.split(gh, 3, axis=-1)
            r = jax.nn.sigmoid(i_r + h_r)
            z = jax.nn.sigmoid(i_z + h_z)
            n = jnp.tanh(i_n + r * h_n)
            S_new = (1.0 - z) * n + z * S
            q = S_new @ wq + bq
            k = S_new @ wk + bk
            v = S_new @ wv + bv
            scale = DQ ** (-0.5)
            attn = jax.nn.softmax(jnp.einsum('bsq,btq->bst', q, k) * scale, axis=-1)
            S_comm = jnp.einsum('bst,btd->bsd', attn, v)
            y = S_new + S_comm
            mu = y.mean(axis=-1, keepdims=True)
            var = y.var(axis=-1, keepdims=True)
            y = (y - mu) * jax.lax.rsqrt(var + 1e-05) * ln_g + ln_b
            slot_values = y @ wvp + bvp
            out = jnp.einsum('bts,bsd->btd', alpha, slot_values)
            return out @ wo + bo
        return _forward(x, slot_init, w1, b1, w2, b2, tau, Wih, Whh, bih, bhh, wq, bq, wk, bk, wv, bv, ln_g, ln_b, wvp, bvp, wo, bo)
    x = L0_attn_a_x
    x = x + _L0_attn_a_ref(_layernorm(x, axis=-1), L0_attn_a_W_in, L0_attn_a_W_xproj, L0_attn_a_W_dt, L0_attn_a_b_dt, L0_attn_a_A_log, L0_attn_a_D, L0_attn_a_W_out)
    x = x + _L0_ffn_ref(_layernorm(x, axis=-1), L0_ffn_router_w, L0_ffn_router_b, L0_ffn_lang_w, L0_ffn_lang_b, L0_ffn_w1, L0_ffn_b1, L0_ffn_w2, L0_ffn_b2)
    x = x + _L0_attn_b_ref(_layernorm(x, axis=-1), L0_attn_b_Wq, L0_attn_b_Wk, L0_attn_b_Wv, L0_attn_b_conv_q, L0_attn_b_conv_k, L0_attn_b_conv_v, L0_attn_b_W_init, L0_attn_b_ln_gamma, L0_attn_b_ln_beta, L0_attn_b_Wg, L0_attn_b_Wo)
    x = x + _L0_ffn_ref(_layernorm(x, axis=-1), L0_ffn_router_w, L0_ffn_router_b, L0_ffn_lang_w, L0_ffn_lang_b, L0_ffn_w1, L0_ffn_b1, L0_ffn_w2, L0_ffn_b2)
    x = x + _L1_attn_a_ref(_layernorm(x, axis=-1), L1_attn_a_Wq, L1_attn_a_bq, L1_attn_a_Wk, L1_attn_a_bk, L1_attn_a_Wv, L1_attn_a_bv, L1_attn_a_Wg, L1_attn_a_bg, L1_attn_a_Wo, L1_attn_a_bo)
    x = x + _L1_ffn_ref(_layernorm(x, axis=-1), L1_ffn_wqkv, L1_ffn_q_scale, L1_ffn_k_scale, L1_ffn_wo, L1_ffn_ln_g, L1_ffn_ln_b, L1_ffn_w1, L1_ffn_b1, L1_ffn_w2, L1_ffn_b2)
    x = x + _L1_attn_b_ref(_layernorm(x, axis=-1), L1_attn_b_Wq, L1_attn_b_bq, L1_attn_b_Wl, L1_attn_b_bl, L1_attn_b_Wk, L1_attn_b_bk, L1_attn_b_Wv, L1_attn_b_bv, L1_attn_b_Wo, L1_attn_b_bo)
    x = x + _L1_ffn_ref(_layernorm(x, axis=-1), L1_ffn_wqkv, L1_ffn_q_scale, L1_ffn_k_scale, L1_ffn_wo, L1_ffn_ln_g, L1_ffn_ln_b, L1_ffn_w1, L1_ffn_b1, L1_ffn_w2, L1_ffn_b2)
    x = x + _L2_attn_a_ref(_layernorm(x, axis=-1), L2_attn_a_in_proj_w, L2_attn_a_conv_w, L2_attn_a_conv_b, L2_attn_a_x_proj_w, L2_attn_a_dt_proj_w, L2_attn_a_dt_proj_b, L2_attn_a_A_log, L2_attn_a_D, L2_attn_a_out_proj_w)
    x = x + _L2_ffn_ref(_layernorm(x, axis=-1), L2_ffn_gate_w, L2_ffn_w1, L2_ffn_w2, L2_ffn_w3)
    x = x + _L2_attn_b_ref(_layernorm(x, axis=-1), L2_attn_b_Wq, L2_attn_b_bq, L2_attn_b_Wk, L2_attn_b_bk, L2_attn_b_Wv, L2_attn_b_bv, L2_attn_b_Wo, L2_attn_b_bo)
    x = x + _L2_ffn_ref(_layernorm(x, axis=-1), L2_ffn_gate_w, L2_ffn_w1, L2_ffn_w2, L2_ffn_w3)
    x = x + _L3_attn_a_ref(_layernorm(x, axis=-1), L3_attn_a_qkv_w, L3_attn_a_proj_w, L3_attn_a_proj_b)
    x = x + _L3_ffn_ref(_layernorm(x, axis=-1), L3_ffn_slot_init, L3_ffn_w1, L3_ffn_b1, L3_ffn_w2, L3_ffn_b2, L3_ffn_tau, L3_ffn_Wih, L3_ffn_Whh, L3_ffn_bih, L3_ffn_bhh, L3_ffn_wq, L3_ffn_bq, L3_ffn_wk, L3_ffn_bk, L3_ffn_wv, L3_ffn_bv, L3_ffn_ln_g, L3_ffn_ln_b, L3_ffn_wvp, L3_ffn_bvp, L3_ffn_wo, L3_ffn_bo)
    x = x + _L3_attn_b_ref(_layernorm(x, axis=-1), L3_attn_b_norm1_w, L3_attn_b_norm2_w, L3_attn_b_g_wq, L3_attn_b_g_kv_down, L3_attn_b_g_k_up, L3_attn_b_g_v_up, L3_attn_b_g_wo, L3_attn_b_l_wq, L3_attn_b_l_wk, L3_attn_b_l_wv, L3_attn_b_l_wo)
    x = x + _L3_ffn_ref(_layernorm(x, axis=-1), L3_ffn_slot_init, L3_ffn_w1, L3_ffn_b1, L3_ffn_w2, L3_ffn_b2, L3_ffn_tau, L3_ffn_Wih, L3_ffn_Whh, L3_ffn_bih, L3_ffn_bhh, L3_ffn_wq, L3_ffn_bq, L3_ffn_wk, L3_ffn_bk, L3_ffn_wv, L3_ffn_bv, L3_ffn_ln_g, L3_ffn_ln_b, L3_ffn_wvp, L3_ffn_bvp, L3_ffn_wo, L3_ffn_bo)
    return x

_drawn_inputs = setup_inputs


def setup_inputs(seed=0):
    import zlib

    import numpy as np

    out = dict(_drawn_inputs(seed))
    spreads = {'L0_attn_a_D': (1.0, 0.2),
     'L0_attn_b_ln_gamma': (1.0, 0.2),
     'L0_attn_b_ln_beta': (0.0, 0.1),
     'L0_ffn_router_b': (0.0, 0.1),
     'L0_ffn_lang_b': (0.0, 0.1),
     'L0_ffn_b1': (0.0, 0.1),
     'L0_ffn_b2': (0.0, 0.1),
     'L1_attn_b_bq': (0.0, 0.1),
     'L1_attn_b_bl': (0.0, 0.1),
     'L1_attn_b_bk': (0.0, 0.1),
     'L1_attn_b_bv': (0.0, 0.1),
     'L1_attn_b_bo': (0.0, 0.1),
     'L1_ffn_q_scale': (1.0, 0.2),
     'L1_ffn_k_scale': (1.0, 0.2),
     'L1_ffn_ln_g': (1.0, 0.2),
     'L1_ffn_ln_b': (0.0, 0.1),
     'L1_ffn_b1': (0.0, 0.1),
     'L1_ffn_b2': (0.0, 0.1),
     'L2_attn_a_D': (1.0, 0.2),
     'L2_attn_b_bq': (0.0, 0.1),
     'L2_attn_b_bk': (0.0, 0.1),
     'L2_attn_b_bv': (0.0, 0.1),
     'L2_attn_b_bo': (0.0, 0.1),
     'L3_attn_b_norm1_w': (1.0, 0.2),
     'L3_attn_b_norm2_w': (1.0, 0.2),
     'L3_ffn_b1': (0.0, 0.1),
     'L3_ffn_b2': (0.0, 0.1),
     'L3_ffn_bih': (0.0, 0.1),
     'L3_ffn_bhh': (0.0, 0.1),
     'L3_ffn_bq': (0.0, 0.1),
     'L3_ffn_bk': (0.0, 0.1),
     'L3_ffn_bv': (0.0, 0.1),
     'L3_ffn_ln_g': (1.0, 0.2),
     'L3_ffn_ln_b': (0.0, 0.1),
     'L3_ffn_bvp': (0.0, 0.1),
     'L3_ffn_bo': (0.0, 0.1)}
    factors = {}
    for name, (base, spread) in spreads.items():
        noise = np.random.default_rng([zlib.crc32(name.encode()), seed]).standard_normal(out[name].shape)
        drawn = base * np.exp(spread * noise) if base else spread * noise
        out[name] = jnp.asarray(drawn.astype(out[name].dtype))
    for name, factor in factors.items():
        out[name] = (out[name] * factor).astype(out[name].dtype)
    return out
```

```python
from contextlib import ExitStack

import numpy as np

import concourse.bass as bass
from concourse import mybir

ALU = mybir.AluOpType
ACT = mybir.ActivationFunctionType
F32 = mybir.dt.float32
BF16 = mybir.dt.bfloat16
AX = mybir.AxisListType.X

P = 128
BATCHES, TOKENS = 8, 256
N_STREAMS = 4
PER_STREAM = BATCHES // N_STREAMS
COLS = PER_STREAM * TOKENS
TILES = COLS // P
BANK = 512
HEADS8, HD8 = 16, 8
NEG = -1.0e30


def k_tiles(w):
    k, n = w.shape
    nt = -(-k // P)
    out = np.zeros((nt * P, n), w.dtype)
    out[:k] = w
    return out.reshape(nt, P, n).transpose(1, 0, 2).reshape(P, nt * n)


def as_cols(v):
    return k_tiles(v.reshape(-1, 1))


def as_rows(v):
    return np.broadcast_to(v.reshape(1, -1), (P, v.size))


def pack(parts):
    where, at = {}, 0
    for name, a in parts.items():
        where[name] = (at, a.shape[0], a.shape[1])
        at += a.shape[1]
    out = np.zeros((P, at), np.float32)
    for name, a in parts.items():
        c, r, n = where[name]
        out[:r, c:c + n] = a
    return out, where


def constants():
    ch = np.arange(P)
    c = {"ident": np.eye(P), "mean": np.full((P, P), 1.0 / P), "center": np.eye(P) - 1.0 / P,
         "ones": np.ones((P, P))}
    g8 = (ch[:, None] // HD8 == ch[None] // HD8).astype(float)
    c["group8"] = g8
    c["mean8"] = g8 / HD8
    c["center8"] = np.eye(P) - g8 / HD8
    c["head_of_row_group"] = (ch[:, None] % 32 // HD8 == np.arange(4)[None]).astype(float)
    q, k = np.arange(P)[:, None], np.arange(P)[None]
    c["keys_up_to_query"] = (q <= k).astype(float)
    kk = np.arange(TOKENS)[None]
    for t in range(2):
        c[f"block32_{t}"] = ((q + t * P) // 32 >= kk // 32).astype(float)
    rot = np.zeros((P, P))
    for i in range(0, P, 2):
        rot[i + 1, i] = -1.0
        rot[i, i + 1] = 1.0
    c["pair_rotation"] = rot
    f = np.float32
    for name, base in (("global", 1000000.0), ("local", 10000.0)):
        inv = (f(1.0) / f(base) ** (np.arange(0, HD8, 2, dtype=f) / f(HD8))).astype(f)
        ang = (np.arange(TOKENS, dtype=f)[:, None] * inv[None]).astype(f)
        ang = ang[:, (ch % HD8) // 2].T
        c[f"cos_{name}"], c[f"sin_{name}"] = np.cos(ang), np.sin(ang)
    hd, window = 64, 64
    half = np.arange(0, hd, 2, dtype=f)
    inv = (f(1.0) / f(10000.0) ** (half / f(hd))).astype(f)
    t = np.arange(TOKENS, dtype=f)
    ang = (t[:, None] * inv[None]).astype(f)
    scale = ((half + f(0.4 * hd)) / f(1.4 * hd))[None] ** ((t - TOKENS // 2) / f(window // 2))[:, None]
    scale = scale.astype(f)
    for name, s in (("q", scale), ("k", (f(1.0) / scale).astype(f))):
        cs, sn = np.cos(ang) * s, np.sin(ang) * s
        c[f"xpos_cos_{name}"] = k_tiles(np.concatenate([cs, cs], 1))
        c[f"xpos_sin_{name}"] = k_tiles(np.concatenate([-sn, sn], 1))
    c["eps"] = np.tile(np.array([[1e-5, 1e-12, 1e-6]]), (P, 1))
    return {k: np.ascontiguousarray(v, np.float32) for k, v in c.items()}


def masks():
    out = {"ident": np.eye(P)}
    q, k = np.arange(P)[:, None], np.arange(TOKENS)[None]
    for name, band in (("causal", TOKENS), ("band32", 31), ("band64", 64)):
        for t in range(2):
            d = (q + t * P) - k[:, 0:(t + 1) * P]
            out[f"{name}_{t}"] = np.where((d >= 0) & (d <= band), 0.0, NEG)
    return {k: v.astype(np.float32) for k, v in out.items()}


def gla_spread(K=32):
    per = P // K
    row, p = np.arange(K)[:, None], np.arange(P)[None]
    tiles = [(row == per * i + p // K) for i in range(K // per)] + [row == p % K]
    return np.tile(np.concatenate(tiles, 1).astype(np.float32), (P // K, 1))


def scan_layout(p, w_in, w_xproj, w_dt, b_dt, a_log, d, w_out):
    return {"w_in": p[w_in], "w_xproj": k_tiles(p[w_xproj]), "w_dt": p[w_dt], "b_dt": as_cols(p[b_dt]),
            "a_log": k_tiles(p[a_log]), "d": as_cols(p[d]), "w_out": k_tiles(p[w_out])}


def layouts(p):
    g = {}
    g["L0_scan"] = scan_layout(p, *(f"L0_attn_a_{n}" for n in
                                    ("W_in", "W_xproj", "W_dt", "b_dt", "A_log", "D", "W_out")))
    n = "L0_attn_b_"
    w0 = np.zeros((P, P), np.float32)
    for h in range(HEADS8):
        w0[h * HD8:(h + 1) * HD8, h * HD8:(h + 1) * HD8] = p[n + "W_init"][0, h]
    g["L0_linear"] = {**{w: p[n + w].T for w in ("Wq", "Wk", "Wv", "Wg", "Wo")},
                      **{w: p[n + w] for w in ("conv_q", "conv_k", "conv_v")}, "state0": w0,
                      "ln_gamma": as_cols(np.tile(p[n + "ln_gamma"], HEADS8)),
                      "ln_beta": as_cols(np.tile(p[n + "ln_beta"], HEADS8))}
    n = "L0_ffn_"
    e = p[n + "w1"].shape[0]
    g["L0_experts"] = {"w_route": np.concatenate([p[n + "lang_w"], p[n + "router_w"]]).T,
                       "b_route": as_rows(np.concatenate([p[n + "lang_b"], p[n + "router_b"]])),
                       "b1": as_cols(p[n + "b1"].reshape(-1)), "b2": p[n + "b2"],
                       "w1": p[n + "w1"].transpose(1, 0, 2).reshape(P, -1),
                       "w2": k_tiles(p[n + "w2"].reshape(-1, P))}
    n = "L1_attn_a_"
    g["L1_gla"] = {"w_qkgv": np.concatenate([p[n + w] for w in ("Wq", "Wk", "Wg", "Wv")], 1),
                   "b_qkgv": as_cols(np.concatenate([p[n + w] for w in ("bq", "bk", "bg", "bv")])),
                   "Wo": np.tile(p[n + "Wo"], (4, 1)), "bo": as_cols(p[n + "bo"]), "spread": gla_spread()}
    n = "L1_attn_b_"
    g["L1_attn"] = {**{w: p[n + w] for w in ("Wq", "Wl", "Wk", "Wv", "Wo")},
                    **{w: as_cols(p[n + w]) for w in ("bq", "bk", "bo")},
                    "bl": p[n + "bl"].reshape(-1, 1), "bv": as_rows(p[n + "bv"])}
    n = "L1_ffn_"
    g["L1_local"] = {}
    for d in range(p[n + "wqkv"].shape[0]):
        g["L1_local"].update({
            f"wqkv{d}": p[n + "wqkv"][d], f"q_scale{d}": as_rows(p[n + "q_scale"][d]),
            f"k_scale{d}": as_rows(p[n + "k_scale"][d]), f"wo{d}": k_tiles(p[n + "wo"][d]),
            f"ln_g{d}": as_cols(p[n + "ln_g"][d]), f"ln_b{d}": as_cols(p[n + "ln_b"][d]),
            f"w1{d}": p[n + "w1"][d], f"w2{d}": k_tiles(p[n + "w2"][d]), f"b2{d}": as_cols(p[n + "b2"][d]),
            f"b1a{d}": as_cols(np.split(p[n + "b1"][d], 2)[0]),
            f"b1g{d}": as_cols(np.split(p[n + "b1"][d], 2)[1])})
    n = "L2_attn_a_"
    g["L2_scan"] = scan_layout(p, *(n + w for w in ("in_proj_w", "x_proj_w", "dt_proj_w", "dt_proj_b",
                                                    "A_log", "D", "out_proj_w")))
    g["L2_scan"]["conv_w"] = k_tiles(p[n + "conv_w"][:, 0])
    g["L2_scan"]["conv_b"] = as_cols(p[n + "conv_b"])
    n = "L2_attn_b_"
    g["L2_attn"] = {**{w: p[n + w].T for w in ("Wq", "Wk", "Wv", "Wo")},
                    **{w: as_cols(p[n + w]) for w in ("bq", "bk", "bo")}, "bv": as_rows(p[n + "bv"])}
    n = "L2_ffn_"
    g["L2_experts"] = {"w_route": p[n + "gate_w"].T,
                       "w1": p[n + "w1"].transpose(1, 0, 2).reshape(P, -1),
                       "w3": p[n + "w3"].transpose(1, 0, 2).reshape(P, -1),
                       "w2": np.concatenate([k_tiles(p[n + "w2"][i]) for i in range(e)], 1)}
    n = "L3_attn_a_"
    g["L3_blocks"] = {"w_qkv": p[n + "qkv_w"].T, "Wo": p[n + "proj_w"].T, "bo": as_cols(p[n + "proj_b"])}
    n = "L3_attn_b_"

    def over_heads(w):
        return np.repeat(w.reshape(w.shape[0], -1, HD8), HEADS8 * HD8 // w.shape[1], axis=1).reshape(w.shape[0], P)

    g["L3_gqa"] = {"norm1": as_cols(p[n + "norm1_w"]), "norm2": as_cols(p[n + "norm2_w"]),
                   "g_wq": p[n + "g_wq"], "g_down": p[n + "g_kv_down"], "g_wk": over_heads(p[n + "g_k_up"]),
                   "g_wv": over_heads(p[n + "g_v_up"]), "g_wo": p[n + "g_wo"], "l_wq": p[n + "l_wq"],
                   "l_wk": over_heads(p[n + "l_wk"]), "l_wv": over_heads(p[n + "l_wv"]), "l_wo": p[n + "l_wo"]}
    n = "L3_ffn_"
    g["L3_slots"] = {"slots": p[n + "slot_init"].T, "w1x": p[n + "w1"][:P], "w1s": p[n + "w1"][P:],
                     "b1": p[n + "b1"].reshape(-1, 1), "w2": p[n + "w2"], "b2": as_rows(p[n + "b2"]),
                     "tau": as_rows(p[n + "tau"]), "Wih": p[n + "Wih"].T, "Whh": p[n + "Whh"].T,
                     "bih": as_cols(p[n + "bih"]), "bhh": as_cols(p[n + "bhh"]),
                     "wq": p[n + "wq"], "bq": p[n + "bq"].reshape(-1, 1), "wk": p[n + "wk"],
                     "bk": p[n + "bk"].reshape(-1, 1), "wv": p[n + "wv"], "bv": as_rows(p[n + "bv"]),
                     "ln_g": as_cols(p[n + "ln_g"]), "ln_b": as_cols(p[n + "ln_b"]), "wvp": p[n + "wvp"],
                     "bvp": as_rows(p[n + "bvp"]), "wo": p[n + "wo"], "bo": as_cols(p[n + "bo"])}
    return g


class Core:

    def __init__(self, nc, ctx):
        self.nc = nc
        self.engines = {"pe": nc.tensor, "act": nc.scalar, "dve": nc.vector, "pool": nc.gpsimd, "sp": nc.sync}
        self.sems = {e: ctx.enter_context(nc.semaphore(f"steps_{e}")) for e in ("pe", "act", "dve", "pool")}
        self.count = dict.fromkeys(self.sems, 0)
        self.waited = {}

    def wait(self, engine, sem_name, value):
        if self.waited.get((engine, sem_name), 0) < value:
            self.waited[engine, sem_name] = value
            self.engines[engine].wait_ge(self.sems[sem_name], value)

    def count_up(self, engine, instruction):
        self.count[engine] += 1
        instruction.then_inc(self.sems[engine], 1)
        return engine, self.count[engine]


class Weights:

    def __init__(self, buf, where):
        self.buf, self.where, self.extra = buf, where, None

    def __getitem__(self, name):
        c, r, n = self.where[name]
        return self.buf[0:r, c:c + n]


class Stream:

    def __init__(self, core, index, x, scratch, psum, const, masks):
        self.core, self.index, self.x, self.scratch, self.psum = core, index, x, scratch, psum
        self.c, self.m = const, masks
        self.a, self.b = psum[:, 0:BANK], psum[:, BANK:2 * BANK]
        self.last, self.engine, self.used = None, None, 0
        self.past_first_experts = None

    def _on(self, engine):
        if self.last is not None:
            self.core.wait(engine, *self.last)
        self.engine = engine
        return self.core.engines[engine]

    def pe(self):
        return self._on("pe")

    def act(self):
        return self._on("act")

    def dve(self):
        return self._on("dve")

    def pool(self):
        return self._on("pool")

    def end(self, instruction):
        self.last = self.core.count_up(self.engine, instruction)

    def needs(self, group):
        for e in ("pe", "act", "dve", "pool"):
            self.core.wait(e, f"load_{group}", 16)

    def wait_all(self, engine, value):
        for e in ("dve", "pool"):
            self.core.wait(e, engine, value)

    def fresh(self):
        self.used = 0

    def take(self, *shape, parts=P):
        n = int(np.prod(shape))
        ap = self.scratch[0:parts, self.used:self.used + n]
        self.used += n
        assert self.used <= SCRATCH, (self.used, shape)
        if len(shape) == 2:
            ap = ap.rearrange("p (a b) -> p a b", b=shape[1])
        if len(shape) == 3:
            ap = ap.rearrange("p (a b c) -> p a b c", b=shape[1], c=shape[2])
        return ap


SCRATCH = 5152


def v2(ap, n):
    return ap.rearrange("p (a b) -> p a b", b=n)


def over(ap, shape):
    return ap.broadcast_to(shape)


def normalise(s, src, out, center, mean, eps, gain=None, shift=None):
    n = src.shape[-1]
    mark = s.used
    sq = s.take(n)
    a, b = s.a[:, 0:n], s.b[:, 0:n]
    centred = src
    if center is not None:
        s.end(s.pe().matmul(a, center, src, start=True, stop=True)); yield
        centred = a
    s.end(s.act().activation(sq, centred, ACT.Square)); yield
    s.end(s.pe().matmul(b, mean, sq, start=True, stop=True)); yield
    s.end(s.act().activation(sq, b, ACT.Ln, bias=eps)); yield
    s.end(s.act().activation(sq, sq, ACT.Exp, scale=-0.5)); yield
    s.end(s.dve().tensor_tensor(out, centred, sq, ALU.mult)); yield
    if gain is not None:
        if shift is not None:
            s.end(s.dve().tensor_scalar(out, out, gain, shift, ALU.mult, ALU.add)); yield
        else:
            s.end(s.dve().tensor_scalar(out, out, gain, None, ALU.mult)); yield
    s.used = mark


def layer_norm(s, src, out, gain=None, shift=None):
    yield from normalise(s, src, out, s.c["center"], s.c["mean"], s.c["eps"][:, 0:1], gain, shift)


def to_channels(s, src, dst, bank):
    t = dst.shape[1]
    e = s.pe()
    for i in range(t):
        last = e.transpose(bank[:, i * P:(i + 1) * P], src[:, i * P:(i + 1) * P], s.c["ident"])
    s.end(last); yield
    s.end(s.act().activation(dst, v2(bank[:, 0:t * P], P), ACT.Copy)); yield


def scan_block(s, w, conv, a_is_exp, clip):
    D, N = 2, 16
    rank = w["w_dt"].shape[0]
    T = TOKENS
    s.fresh()
    xn = s.take(COLS)
    yield from layer_norm(s, s.x, xn)
    xc, z, delta, dx, a, b, h = (s.take(D, T) for _ in range(7))
    dbc = s.take(T, parts=rank + 2 * N)
    A = s.take(D, N)
    if conv:
        padded = s.take(D, T + 3)
        s.end(s.dve().memset(padded[:, :, 0:3], 0.0)); yield
    s.end(s.act().activation(A, v2(w["a_log"], N), ACT.Exp)); yield
    s.end(s.dve().tensor_scalar(A, A, -1.0, None, ALU.mult)); yield
    s.end(s.dve().memset(a, 0.0)); yield
    A2, B2 = v2(s.a, T), v2(s.b, T)
    for bt in range(PER_STREAM):
        xb = xn[:, bt * T:(bt + 1) * T]
        e = s.pe()
        for d in range(D):
            last = e.matmul(A2[:, d, :], w["w_in"][:, d * P:(d + 1) * P], xb, start=True, stop=True)
        for d in range(D):
            last = e.matmul(B2[:, d, :], w["w_in"][:, (D + d) * P:(D + d + 1) * P], xb, start=True, stop=True)
        s.end(last); yield
        if conv:
            s.end(s.dve().tensor_copy(padded[:, :, 3:3 + T], A2)); yield
            taps = v2(w["conv_w"], 4)
            for k in range(4):
                e = s.dve()
                for d in range(D):
                    tap = taps[:, d, k:k + 1]
                    if k == 0:
                        last = e.tensor_scalar(b[:, d, :], padded[:, d, 0:T], tap, w["conv_b"][:, d:d + 1],
                                               ALU.mult, ALU.add)
                    else:
                        last = e.scalar_tensor_tensor(b[:, d, :], padded[:, d, k:k + T], tap, b[:, d, :],
                                                      ALU.mult, ALU.add)
                s.end(last); yield
            s.end(s.act().activation(xc, b, ACT.Silu)); yield
        else:
            s.end(s.dve().tensor_copy(xc, A2)); yield
        s.end(s.act().activation(z, B2, ACT.Silu)); yield
        e = s.pe()
        nd = rank + 2 * N
        for d in range(D):
            last = e.matmul(s.a[0:nd, 0:T], w["w_xproj"][:, d * nd:(d + 1) * nd], xc[:, d, :],
                            start=(d == 0), stop=(d == D - 1))
        s.end(last); yield
        s.end(s.dve().tensor_copy(dbc, s.a[0:nd, 0:T])); yield
        e = s.pe()
        for d in range(D):
            last = e.matmul(B2[:, d, :], w["w_dt"][:, d * P:(d + 1) * P], dbc[0:rank, :], start=True, stop=True)
        s.end(last); yield
        e = s.act()
        for d in range(D):
            last = e.activation(delta[:, d, :], B2[:, d, :], ACT.Identity, bias=w["b_dt"][:, d:d + 1])
        s.end(last); yield
        s.end(s.dve().scalar_tensor_tensor(dx, delta, -1.0, delta, ALU.mult, ALU.max)); yield
        s.end(s.act().activation(dx, dx, ACT.Exp, scale=-1.0)); yield
        s.end(s.act().activation(dx, dx, ACT.Ln, bias=1.0)); yield
        s.end(s.dve().scalar_tensor_tensor(delta, delta, 0.0, dx, ALU.max, ALU.add)); yield
        if clip:
            s.end(s.dve().tensor_scalar(delta, delta, clip[0], clip[1], ALU.max, ALU.min)); yield
        s.end(s.dve().tensor_tensor(dx, delta, xc, ALU.mult)); yield
        for n in range(N):
            e = s.pe()
            for i in range(2):
                row = rank + i * N + n
                last = e.matmul(B2[:, i, :], over(s.c["ident"][0:nd, row:row + 1], [nd, P]), dbc, start=True, stop=True)
            before = s.last
            s.end(last)
            bc_done = s.last
            s.last = before
            e = s.act()
            for d in range(D):
                last = e.activation(a[:, d, 1:T], delta[:, d, 1:T], ACT.Exp if a_is_exp else ACT.Identity,
                                    scale=A[:, d, n:n + 1], bias=0.0 if a_is_exp else 1.0)
            s.end(last)
            a_done = s.last
            s.last = bc_done
            yield
            bn, cn = (over(B2[:, i:i + 1, :], [P, D, T]) for i in range(2))
            s.end(s.dve().tensor_tensor(b, dx, bn, ALU.mult)); yield
            s.core.wait("dve", *a_done)
            s.end(s.dve().tensor_tensor_scan(h.rearrange("p a b -> p (a b)"), a.rearrange("p a b -> p (a b)"),
                                             b.rearrange("p a b -> p (a b)"), 0.0, ALU.mult, ALU.add)); yield
            s.end(s.dve().tensor_tensor(h, h, cn, ALU.mult)); yield
            s.end(s.pe().matmul(s.a, s.c["ident"], h.rearrange("p a b -> p (a b)"), start=(n == 0), stop=(n == N - 1))); yield
        e = s.dve()
        for d in range(D):
            last = e.scalar_tensor_tensor(b[:, d, :], xc[:, d, :], w["d"][:, d:d + 1], A2[:, d, :], ALU.mult, ALU.add)
        s.end(last); yield
        s.end(s.dve().tensor_tensor(b, b, z, ALU.mult)); yield
        e = s.pe()
        for d in range(D):
            last = e.matmul(s.b[:, 0:T], w["w_out"][:, d * P:(d + 1) * P], b[:, d, :], start=(d == 0), stop=(d == D - 1))
        s.end(last); yield
        xs = s.x[:, bt * T:(bt + 1) * T]
        s.end(s.dve().tensor_tensor(xs, xs, s.b[:, 0:T], ALU.add)); yield


def linear_attention(s, w):
    s.fresh()
    T = TOKENS
    xn = s.take(COLS)
    yield from layer_norm(s, s.x, xn)
    padded = s.take(PER_STREAM, T + 3)
    s.end(s.dve().memset(padded[:, :, 0:3], 0.0)); yield
    q, k, v = (s.take(COLS) for _ in range(3))
    for name, dst in (("q", q), ("k", k), ("v", v)):
        s.end(s.pe().matmul(s.a, w[f"W{name}"], xn, start=True, stop=True)); yield
        s.end(s.act().activation(padded[:, :, 3:], v2(s.a, T), ACT.Copy)); yield
        taps, y = w[f"conv_{name}"], v2(dst, T)
        for j in range(4):
            s.end(s.dve().scalar_tensor_tensor(y, padded[:, :, j:j + T], taps[:, j:j + 1],
                                               padded[:, :, 3:] if j == 0 else y, ALU.mult, ALU.add)); yield
        s.end(s.act().activation(dst, dst, ACT.Silu)); yield
        if name != "v":
            yield from normalise(s, dst, dst, None, s.c["group8"], s.c["eps"][:, 1:2])
    v_tok, k_tok = s.take(TILES, P), s.take(PER_STREAM, P)
    e = s.pe()
    for t in range(TILES):
        last = e.transpose(s.a[:, t * P:(t + 1) * P], v[:, t * P:(t + 1) * P], s.c["ident"])
    for bt in range(PER_STREAM):
        last = e.transpose(s.b[:, bt * P:(bt + 1) * P], k[:, bt * T:bt * T + P], s.c["ident"])
    s.end(last); yield
    s.end(s.act().activation(v_tok, v2(s.a, P), ACT.Copy)); yield
    s.end(s.act().activation(k_tok, v2(s.b[:, 0:PER_STREAM * P], P), ACT.Copy)); yield
    state = s.take(P)
    o = v
    qm, st, o_tok = s.take(4, P), s.take(4, P), s.take(P)
    for t in range(TILES):
        bt, chunk = divmod(t, T // P)
        cols = slice(t * P, (t + 1) * P)
        if chunk == 0:
            carried = w["state0"]
        else:
            s.end(s.pe().matmul(s.a[:, 0:P], k_tok[:, bt, :], v_tok[:, t - 1, :], start=True, stop=True)); yield
            s.end(s.dve().tensor_tensor(state, s.c["group8"], s.a[:, 0:P], ALU.mult)); yield
            s.end(s.dve().tensor_tensor(state, state, w["state0"], ALU.add)); yield
            carried = state
        e = s.dve()
        for j in range(4):
            last = e.tensor_scalar(qm[:, j, :], q[:, cols], s.c["head_of_row_group"][:, j:j + 1], None, ALU.mult)
        s.end(last); yield
        s.end(s.pe().matmul(s.b[:, 0:P], q[:, cols], carried, start=True, stop=False, skip_group_check=True)); yield
        for g in range(4):
            rows = slice(32 * g, 32 * g + 32)
            e = s.pe()
            for j in range(4):
                last = e.matmul(s.a[:, j * P:(j + 1) * P], k[rows, cols], qm[rows, j, :], start=True, stop=True)
            s.end(last); yield
            s.end(s.dve().tensor_tensor(st, v2(s.a, P), over(s.c["keys_up_to_query"].unsqueeze(1), [P, 4, P]), ALU.mult)); yield
            e = s.pe()
            for j in range(4):
                hc = slice((4 * g + j) * HD8, (4 * g + j + 1) * HD8)
                last = e.matmul(s.b[:, hc], st[:, j, :], v_tok[:, t, hc], start=False, stop=(g == 3 and j == 3), skip_group_check=True)
            s.end(last); yield
        s.end(s.act().activation(o_tok, s.b[:, 0:P], ACT.Copy)); yield
        s.end(s.pe().transpose(s.a[:, 0:P], o_tok, s.c["ident"])); yield
        s.end(s.act().activation(o[:, cols], s.a[:, 0:P], ACT.Copy)); yield
    yield from normalise(s, o, o, s.c["center8"], s.c["mean8"], s.c["eps"][:, 0:1], w["ln_gamma"], w["ln_beta"])
    s.end(s.pe().matmul(s.a, w["Wg"], xn, start=True, stop=True)); yield
    s.end(s.dve().tensor_tensor(o, o, s.a, ALU.mult)); yield
    s.end(s.pe().matmul(s.b, w["Wo"], o, start=True, stop=True)); yield
    s.end(s.dve().tensor_tensor(s.x, s.x, s.b, ALU.add)); yield


def keep_top(s, values, kept, n_top, fill):
    rows, n = values.shape[1], values.shape[2]
    top = s.take(rows, 8)
    e = s.dve()
    for r in range(rows):
        last = e.max(top[:, r, :], values[:, r, :])
    s.end(last); yield
    if n_top < 8:
        s.end(s.dve().memset(top[:, :, n_top:8], fill)); yield
    for r in range(rows):
        s.end(s.dve().match_replace(kept[:, r, :], top[:, r, :], values[:, r, :], 2 * fill)); yield
    s.end(s.dve().tensor_tensor(kept, kept, values, ALU.not_equal)); yield
    return top


def row_exp(s, logits, out, rows, n):
    m = s.take(rows)
    s.end(s.dve().tensor_reduce(m, logits, AX, ALU.max)); yield
    s.end(s.dve().tensor_tensor(out, logits, over(m.unsqueeze(2), [P, rows, n]), ALU.subtract)); yield
    s.end(s.act().activation(out, out, ACT.Exp)); yield


def row_scale(s, values, rows, n):
    m = s.take(rows)
    s.end(s.dve().tensor_reduce(m, values, AX, ALU.add)); yield
    s.end(s.dve().reciprocal(m, m)); yield
    s.end(s.dve().tensor_tensor(values, values, over(m.unsqueeze(2), [P, rows, n]), ALU.mult)); yield


def gates_to_rows(s, gates, gates_t, n):
    e = s.pe()
    for t in range(TILES):
        last = e.transpose(s.a[0:n, t * P:(t + 1) * P], gates[:, t, :], s.c["ident"])
    s.end(last); yield
    s.end(s.act().activation(gates_t, s.a[0:n, :], ACT.Copy)); yield


def expert_mix(s, w):
    E, L = 8, 4
    s.fresh()
    xn = s.take(COLS)
    yield from layer_norm(s, s.x, xn)
    mark = s.used
    e = s.pe()
    for t in range(TILES):
        last = e.matmul(s.a[:, t * 16:t * 16 + L + E], xn[:, t * P:(t + 1) * P], w["w_route"], start=True, stop=True)
    s.end(last); yield
    logits = s.take(TILES, L + E)
    s.end(s.dve().tensor_tensor(logits, over(w["b_route"].unsqueeze(1), [P, TILES, L + E]),
                                v2(s.a[:, 0:16 * TILES], 16)[:, :, 0:L + E], ALU.add)); yield
    lang = s.take(TILES, L + 1)
    s.end(s.dve().memset(lang, 0.0)); yield
    yield from row_exp(s, logits[:, :, 0:L], lang[:, :, 0:L], TILES, L)
    yield from row_scale(s, lang[:, :, 0:L], TILES, L)
    pair = s.take(TILES, L)
    s.end(s.dve().tensor_tensor(pair, lang[:, :, 0:L], lang[:, :, 1:L + 1], ALU.add)); yield
    route, gates = s.take(TILES, E), s.take(TILES, E)
    e = s.dve()
    for i in range(E // L):
        last = e.scalar_tensor_tensor(route[:, :, i * L:(i + 1) * L], pair, 0.1,
                                      logits[:, :, L + i * L:L + (i + 1) * L], ALU.mult, ALU.add)
    s.end(last); yield
    yield from row_exp(s, route, route, TILES, E)
    yield from row_scale(s, route, TILES, E)
    yield from keep_top(s, route, gates, 2, -1.0)
    s.end(s.dve().tensor_tensor(gates, gates, route, ALU.mult)); yield
    yield from row_scale(s, gates, TILES, E)
    gates_t = s.take(COLS, parts=E)
    yield from gates_to_rows(s, gates, gates_t, E)
    s.end(s.pe().matmul(s.b, w["b2"], gates_t, start=True, stop=True)); yield
    s.end(s.dve().tensor_tensor(s.x, s.x, s.b, ALU.add)); yield
    h, gate = s.take(COLS), s.take(COLS)
    H = w["w1"].shape[-1] // E // P
    for x in range(E):
        s.end(s.pe().matmul(s.a, over(s.c["ident"][0:E, x:x + 1], [E, P]), gates_t, start=True, stop=True)); yield
        s.end(s.dve().tensor_copy(gate, s.a)); yield
        for t in range(H):
            i = x * H + t
            s.end(s.pe().matmul(s.a, w["w1"][:, i * P:(i + 1) * P], xn, start=True, stop=True)); yield
            s.end(s.act().activation(h, s.a, ACT.Gelu, bias=w["b1"][:, i:i + 1])); yield
            s.end(s.pe().matmul(s.b, w["w2"][:, i * P:(i + 1) * P], h, start=(t == 0), stop=(t == H - 1))); yield
        s.end(s.dve().tensor_tensor(gate, gate, s.b, ALU.mult)); yield
        s.end(s.pool().tensor_tensor(s.x, s.x, gate, ALU.add)); yield


def expert_swiglu(s, w):
    E = 8
    s.fresh()
    xn = s.take(COLS)
    yield from layer_norm(s, s.x, xn)
    e = s.pe()
    for t in range(TILES):
        last = e.matmul(s.a[:, t * E:(t + 1) * E], xn[:, t * P:(t + 1) * P], w["w_route"], start=True, stop=True)
    s.end(last); yield
    scores, gates = s.take(TILES, E), s.take(TILES, E)
    s.end(s.dve().tensor_copy(scores, v2(s.a[:, 0:TILES * E], E))); yield
    yield from row_exp(s, scores, scores, TILES, E)
    yield from row_scale(s, scores, TILES, E)
    yield from keep_top(s, scores, gates, 2, -1.0)
    s.end(s.dve().tensor_tensor(gates, gates, scores, ALU.mult)); yield
    gates_t = s.take(COLS, parts=E)
    yield from gates_to_rows(s, gates, gates_t, E)
    hidden = w["w1"].shape[-1] // E
    sizes = [min(P, hidden - i) for i in range(0, hidden, P)]
    xe, h = s.take(COLS), s.take(COLS)
    for x in range(E):
        s.end(s.pe().matmul(s.a, over(s.c["ident"][0:E, x:x + 1], [E, P]), gates_t, start=True, stop=True)); yield
        s.end(s.dve().tensor_tensor(xe, xn, s.a, ALU.mult)); yield
        for t, m in enumerate(sizes):
            c = x * hidden + t * P
            s.end(s.pe().matmul(s.a[0:m, :], w["w1"][:, c:c + m], xe, start=True, stop=True)); yield
            s.end(s.act().activation(h[0:m, :], s.a[0:m, :], ACT.Silu)); yield
            s.end(s.pe().matmul(s.a[0:m, :], w["w3"][:, c:c + m], xe, start=True, stop=True)); yield
            s.end(s.dve().tensor_tensor(h[0:m, :], h[0:m, :], s.a[0:m, :], ALU.mult)); yield
            i = (x * len(sizes) + t) * P
            s.end(s.pe().matmul(s.b, w["w2"][0:m, i:i + P], h[0:m, :], start=(x == 0 and t == 0),
                                stop=(x == E - 1 and t == len(sizes) - 1))); yield
    s.end(s.dve().tensor_tensor(s.x, s.x, s.b, ALU.add)); yield


def gated_linear_attention(s, w):
    K = 32
    per = P // K
    s.fresh()
    xn = s.take(COLS)
    yield from layer_norm(s, s.x, xn)
    qkgv = s.take(COLS)
    s.end(s.pe().matmul(s.a, w["w_qkgv"], xn, start=True, stop=True)); yield
    e = s.act()
    for i, f in enumerate((ACT.Identity, ACT.Sigmoid, ACT.Sigmoid, ACT.Identity)):
        rows = slice(K * i, K * i + K)
        last = e.activation(qkgv[rows, :], s.a[rows, :], f, bias=w["b_qkgv"][rows, :])
    s.end(last); yield
    v_all, b, h = s.take(COLS), s.take(COLS), s.take(COLS)

    def spread(which, i):
        rows = slice(K * which, K * which + K)
        return s.pe().matmul(s.a, w["spread"][rows, i * P:(i + 1) * P], qkgv[rows, :], start=True, stop=True)

    s.end(spread(3, K // per)); yield
    s.end(s.act().activation(v_all, s.a, ACT.Copy)); yield
    for i in range(K // per):
        s.end(spread(1, i)); yield
        s.end(s.dve().tensor_tensor(b, v_all, s.a, ALU.mult)); yield
        s.end(spread(2, i)); yield
        e = s.dve()
        for bt in range(PER_STREAM):
            c = slice(bt * TOKENS, (bt + 1) * TOKENS)
            last = e.tensor_tensor_scan(h[:, c], s.a[:, c], b[:, c], 0.0, ALU.mult, ALU.add)
        s.end(last); yield
        s.end(spread(0, i)); yield
        s.end(s.dve().tensor_tensor(h, h, s.a, ALU.mult)); yield
        s.end(s.pe().matmul(s.b, w["Wo"], h, start=(i == 0), stop=(i == K // per - 1))); yield
    s.end(s.dve().scalar_tensor_tensor(s.x, s.b, w["bo"], s.x, ALU.add, ALU.add)); yield


def attend8(s, q, keys, v_tok, n_tiles, o, scale, add_mask=None, zero_mask=None):
    nk = n_tiles * P
    mark = s.used
    qm, p = s.take(4, P), s.take(4, 2 * P)
    pt = p
    o_raw, sums, m = s.take(P), s.take(HEADS8), s.take(4)
    S = v2(s.psum, 2 * P)[:, :, 0:nk]
    e = s.dve()
    for j in range(4):
        last = e.tensor_scalar(qm[:, j, :], q, s.c["head_of_row_group"][:, j:j + 1], None, ALU.mult)
    s.end(last); yield
    for gp in range(2):
        for jp in range(2):
            heads = [(2 * gp + i // 2, 2 * jp + i % 2) for i in range(4)]
            if add_mask is not None:
                e = s.pe()
                for i in (0, 2):
                    last = e.matmul(S[:, i:i + 2, :], s.m["ident"], over(add_mask.unsqueeze(1), [P, 2, nk]),
                                    start=True, stop=True)
                s.end(last); yield
            e = s.pe()
            for i, (g, j) in enumerate(heads):
                rows = slice(32 * g, 32 * g + 32)
                last = e.matmul(S[:, i, :], qm[rows, j, :], keys[rows, 0:nk], start=(add_mask is None),
                                stop=True, skip_group_check=True)
            s.end(last); yield
            scores = S
            if zero_mask is not None:
                scores = p[:, :, 0:nk]
                s.end(s.dve().tensor_tensor(scores, S, over(zero_mask[:, 0:nk].unsqueeze(1), [P, 4, nk]), ALU.mult)); yield
            s.end(s.dve().tensor_reduce(m, scores, AX, ALU.max)); yield
            s.end(s.dve().tensor_scalar(m, m, -scale, None, ALU.mult)); yield
            e = s.act()
            for i, (g, j) in enumerate(heads):
                hh = 4 * g + j
                last = e.activation(p[:, i, 0:nk], scores[:, i, :], ACT.Exp, bias=m[:, i:i + 1], scale=scale,
                                    accum_out=sums[:, hh:hh + 1])
            s.end(last); yield
            e = s.pe()
            for i in range(4):
                for c in range(n_tiles):
                    last = e.transpose(S[:, i, c * P:(c + 1) * P], p[:, i, c * P:(c + 1) * P], s.c["ident"])
            s.end(last); yield
            if gp == jp:
                s.end(s.dve().tensor_copy(pt[:, :, 0:nk], S)); yield
            else:
                s.end(s.act().activation(pt[:, :, 0:nk], S, ACT.Copy)); yield
            e = s.pe()
            for i, (g, j) in enumerate(heads):
                hc = slice((4 * g + j) * HD8, (4 * g + j + 1) * HD8)
                for c in range(n_tiles):
                    last = e.matmul(s.a[:, hc], pt[:, i, c * P:(c + 1) * P], v_tok[:, c, hc],
                                    start=(c == 0), stop=(c == n_tiles - 1), skip_group_check=True)
            s.end(last); yield
            pick = lambda ap: ap[:, 0:P].rearrange("p (g j d) -> p g (j d)", g=4, j=4)[:, 2 * gp:2 * gp + 2, 2 * jp * HD8:(2 * jp + 2) * HD8]
            s.end(s.dve().tensor_copy(pick(o_raw), pick(s.a))); yield
    s.end(s.dve().reciprocal(sums, sums)); yield
    s.end(s.dve().tensor_tensor(v2(o_raw, HD8), v2(o_raw, HD8), over(sums.unsqueeze(2), [P, HEADS8, HD8]), ALU.mult)); yield
    s.end(s.pe().transpose(s.a[:, 0:P], o_raw, s.c["ident"])); yield
    s.end(s.act().activation(o, s.a[:, 0:P], ACT.Copy)); yield
    s.used = mark


def values_by_token(s, src, wv, v_tok, bias=None):
    e = s.pe()
    for t in range(TILES):
        last = e.matmul(s.a[:, t * P:(t + 1) * P], src[:, t * P:(t + 1) * P], wv, start=True, stop=True)
    s.end(last); yield
    if bias is None:
        s.end(s.act().activation(v_tok, v2(s.a, P), ACT.Copy)); yield
    else:
        s.end(s.dve().tensor_tensor(v_tok, over(bias.unsqueeze(1), [P, TILES, P]), v2(s.a, P), ALU.add)); yield


def project(s, w, src, dst, bias=None):
    m = w.shape[-1]
    s.end(s.pe().matmul(s.a[0:m, :], w, src, start=True, stop=True)); yield
    if bias is None:
        s.end(s.act().activation(dst, s.a[0:m, :], ACT.Copy)); yield
    else:
        s.end(s.act().activation(dst, s.a[0:m, :], ACT.Identity, bias=bias)); yield


def attention(s, w, latent, masked):
    s.fresh()
    xn = s.take(COLS)
    yield from layer_norm(s, s.x, xn)
    q, k, v_tok = s.take(COLS), s.take(COLS), s.take(TILES, P)
    yield from project(s, w["Wq"], xn, q, w["bq"])
    src = xn
    if latent:
        m = w["Wl"].shape[-1]
        src = s.take(COLS, parts=m)
        yield from project(s, w["Wl"], xn, src, w["bl"])
    yield from project(s, w["Wk"], src, k, w["bk"])
    yield from values_by_token(s, src, w["Wv"], v_tok, w["bv"])
    o = xn
    for t in range(TILES):
        bt, qt = divmod(t, 2)
        cols = slice(t * P, (t + 1) * P)
        yield from attend8(s, q[:, cols], k[:, bt * TOKENS:(bt + 1) * TOKENS], v_tok[:, 2 * bt:2 * bt + 2, :], 2,
                           o[:, cols], HD8 ** -0.5, zero_mask=s.c[f"block32_{qt}"] if masked else None)
    s.end(s.pe().matmul(s.a, w["Wo"], o, start=True, stop=True)); yield
    s.end(s.dve().scalar_tensor_tensor(s.x, s.a, w["bo"], s.x, ALU.add, ALU.add)); yield


def block_attention(s, w):
    s.fresh()
    xn = s.take(COLS)
    yield from layer_norm(s, s.x, xn)
    q, k, v = (s.take(COLS) for _ in range(3))
    for i, dst in enumerate((q, k, v)):
        yield from project(s, w["w_qkv"][:, i * P:(i + 1) * P], xn, dst)
    qs, ks, prod = s.take(TILES), s.take(TILES), s.take(TILES, 2)
    s.end(s.dve().tensor_reduce(qs, v2(q, P), AX, ALU.add)); yield
    s.end(s.dve().tensor_reduce(ks, v2(k, P), AX, ALU.add)); yield
    s.end(s.dve().tensor_scalar(qs, qs, 1.0 / P, None, ALU.mult)); yield
    s.end(s.dve().tensor_scalar(ks, ks, 1.0 / P, None, ALU.mult)); yield
    e = s.dve()
    for bt in range(PER_STREAM):
        two = slice(2 * bt, 2 * bt + 2)
        last = e.tensor_tensor(prod[:, two, :], over(qs[:, two].unsqueeze(2), [P, 2, 2]),
                               over(ks[:, two].unsqueeze(1), [P, 2, 2]), ALU.mult)
    s.end(last); yield
    n = TILES * 2
    s.end(s.pe().matmul(s.a[:, 0:n], s.c["group8"], prod.rearrange("p a b -> p (a b)"), start=True, stop=True)); yield
    s.end(s.dve().tensor_copy(prod, v2(s.a[:, 0:n], 2))); yield
    second, first = s.take(TILES), s.take(TILES)
    s.end(s.dve().tensor_tensor(second, prod[:, :, 1], prod[:, :, 0], ALU.is_gt)); yield
    s.end(s.dve().tensor_scalar(first, second, -1.0, 1.0, ALU.mult, ALU.add)); yield
    kc, vc, v_tok = s.take(P), s.take(P), s.take(1, P)
    o = xn
    for t in range(TILES):
        lo = t // 2 * TOKENS
        for src, dst in ((k, kc), (v, vc)):
            s.end(s.dve().tensor_scalar(dst, src[:, lo:lo + P], first[:, t:t + 1], None, ALU.mult)); yield
            s.end(s.dve().scalar_tensor_tensor(dst, src[:, lo + P:lo + 2 * P], second[:, t:t + 1], dst, ALU.mult, ALU.add)); yield
        yield from to_channels(s, vc, v_tok, s.a)
        cols = slice(t * P, (t + 1) * P)
        yield from attend8(s, q[:, cols], kc, v_tok, 1, o[:, cols], HD8 ** -0.5)
    s.end(s.pe().matmul(s.a, w["Wo"], o, start=True, stop=True)); yield
    s.end(s.dve().scalar_tensor_tensor(s.x, s.a, w["bo"], s.x, ALU.add, ALU.add)); yield


def grouped_query_attention(s, w):
    s.fresh()
    y, xn, q, k = (s.take(COLS) for _ in range(4))
    v_tok = s.take(TILES, P)
    yield from layer_norm(s, s.x, y)

    def rotate_and_norm(dst, kind):
        tmp = s.take(COLS)
        s.end(s.pe().matmul(s.a, s.c["pair_rotation"], dst, start=True, stop=True)); yield
        sin = over(s.c[f"sin_{kind}"].unsqueeze(1), [P, PER_STREAM, TOKENS])
        cos = over(s.c[f"cos_{kind}"].unsqueeze(1), [P, PER_STREAM, TOKENS])
        s.end(s.dve().tensor_tensor(v2(tmp, TOKENS), sin, v2(s.a, TOKENS), ALU.mult)); yield
        s.end(s.dve().tensor_tensor(v2(dst, TOKENS), v2(dst, TOKENS), cos, ALU.mult)); yield
        s.end(s.dve().tensor_tensor(dst, dst, tmp, ALU.add)); yield
        s.used -= COLS
        yield from normalise(s, dst, dst, None, s.c["mean8"], s.c["eps"][:, 2:3])

    for kind, gain in (("global", "norm1"), ("local", "norm2")):
        yield from normalise(s, y, xn, None, s.c["mean"], s.c["eps"][:, 2:3], w[gain])
        p = kind[0] + "_"
        yield from project(s, w[p + "wq"], xn, q)
        src = xn
        mark = s.used
        if kind == "global":
            src = s.take(COLS, parts=w["g_down"].shape[-1])
            yield from project(s, w["g_down"], xn, src)
        yield from project(s, w[p + "wk"], src, k)
        yield from values_by_token(s, src, w[p + "wv"], v_tok)
        s.used = mark
        for dst in (q, k):
            yield from rotate_and_norm(dst, kind)
        for t in range(TILES):
            bt, qt = divmod(t, 2)
            cols = slice(t * P, (t + 1) * P)
            yield from attend8(s, q[:, cols], k[:, bt * TOKENS:(bt + 1) * TOKENS], v_tok[:, 2 * bt:2 * bt + 2, :],
                               qt + 1, xn[:, cols], HD8 ** -0.5,
                               add_mask=s.m[f"{'causal' if kind == 'global' else 'band32'}_{qt}"])
        s.end(s.pe().matmul(s.a, w[p + "wo"], xn, start=True, stop=True)); yield
        s.end(s.dve().tensor_tensor(y, y, s.a, ALU.add)); yield
    s.end(s.dve().tensor_tensor(s.x, s.x, y, ALU.add)); yield


def shift_tokens(s, src, out):
    src, out = v2(src, TOKENS), v2(out, TOKENS)
    half = P // 2
    e = s.dve()
    e.tensor_copy(out[0:half], src[0:half])
    e.memset(out[half:P, :, 0:1], 0.0)
    s.end(e.tensor_copy(out[half:P, :, 1:TOKENS], src[half:P, :, 0:TOKENS - 1])); yield


def xpos_tables(w, d):
    T2, HD = TOKENS // P, 64
    n = T2 * HD
    at = [v2(w.extra[:, (4 * d + i) * n:(4 * d + i + 1) * n], HD) for i in range(4)]
    return {"q": at[0], "k": at[1]}, {"q": at[2], "k": at[3]}


def prepare_xpos(s, w):
    T2, HD = TOKENS // P, 64
    half = HD // 2
    e = s.dve()
    for d in range(2):
        cos_t, sin_t = xpos_tables(w, d)
        for n in "qk":
            g = w[f"{n}_scale{d}"]
            e.tensor_tensor(cos_t[n], v2(s.c[f"xpos_cos_{n}"], HD), over(g.unsqueeze(1), [P, T2, HD]), ALU.mult)
            for i in range(2):
                o, p = slice(half * i, half * i + half), slice(half - half * i, 2 * half - half * i)
                last = e.tensor_tensor(sin_t[n][:, :, o], v2(s.c[f"xpos_sin_{n}"], HD)[:, :, o],
                                       over(g[:, p].unsqueeze(1), [P, T2, half]), ALU.mult)
    s.end(last)


def local_layer(s, w, d, x):
    H, HD = 8, 64
    T2 = TOKENS // P
    inner = H * HD
    s.used = COLS
    h = s.take(COLS)
    yield from shift_tokens(s, x, h)
    mark = s.used
    half = HD // 2
    cos_t, sin_t = xpos_tables(w, d)
    q, k, v = s.take(inner // P, P), s.take(inner // P, TOKENS), s.take(T2, inner)
    tmp, tok, ss = s.take(inner), s.take(inner), s.take(H)
    p, sums, m = s.take(2, 2 * P), s.take(H), s.take(2)
    pt = p
    heads = lambda ap: v2(ap, HD)
    for bt in range(PER_STREAM):
        hb = h[:, bt * TOKENS:(bt + 1) * TOKENS]

        def rotated(n, t, dst):
            col = 0 if n == "q" else inner
            s.end(s.pe().matmul(s.a, hb[:, t * P:(t + 1) * P], w[f"wqkv{d}"][:, col:col + inner], start=True, stop=True)); yield
            s.end(s.act().activation(tmp, s.a, ACT.Square)); yield
            s.end(s.dve().tensor_reduce(ss, heads(tmp), AX, ALU.add)); yield
            s.end(s.act().activation(ss, ss, ACT.Sqrt)); yield
            s.end(s.dve().tensor_scalar(ss, ss, 1e-12, None, ALU.max)); yield
            s.end(s.dve().reciprocal(ss, ss)); yield
            s.end(s.dve().tensor_tensor(heads(tmp), heads(s.a), over(ss.unsqueeze(2), [P, H, HD]), ALU.mult)); yield
            e = s.dve()
            for i in range(2):
                o, pa = slice(half * i, half * i + half), slice(half - half * i, 2 * half - half * i)
                last = e.tensor_tensor(heads(tok)[:, :, o], heads(tmp)[:, :, pa],
                                       over(sin_t[n][:, t:t + 1, o], [P, H, half]), ALU.mult)
            s.end(last); yield
            s.end(s.pool().tensor_tensor(heads(tmp), heads(tmp), over(cos_t[n][:, t:t + 1, :], [P, H, HD]), ALU.mult)); yield
            s.end(s.pool().tensor_tensor(tok, tok, tmp, ALU.add)); yield
            yield from to_channels(s, tok, dst, s.a)

        for t in range(T2):
            yield from rotated("k", t, k[:, :, t * P:(t + 1) * P])
            s.end(s.pe().matmul(s.b, hb[:, t * P:(t + 1) * P], w[f"wqkv{d}"][:, 2 * inner:3 * inner], start=True, stop=True)); yield
            s.end(s.act().activation(v[:, t, :], s.b, ACT.Copy)); yield
        for t in range(T2):
            yield from rotated("q", t, q)
            nk = (t + 1) * P
            mask = s.m[f"band64_{t}"]
            for pair in range(H // 2):
                S = v2(s.psum, BANK)[:, :, 0:nk]
                e = s.pe()
                for i in range(2):
                    last = e.matmul(S[:, i, :], s.m["ident"], mask, start=True, stop=False)
                s.end(last); yield
                e = s.pe()
                for i in range(2):
                    rows = slice(64 * i, 64 * i + 64)
                    last = e.matmul(S[:, i, :], q[rows, pair, :], k[rows, pair, 0:nk], start=False, stop=True)
                s.end(last); yield
                s.end(s.dve().tensor_reduce(m, S, AX, ALU.max)); yield
                s.end(s.dve().tensor_scalar(m, m, -8.0, None, ALU.mult)); yield
                e = s.act()
                for i in range(2):
                    hh = 2 * pair + i
                    last = e.activation(p[:, i, 0:nk], S[:, i, :], ACT.Exp, bias=m[:, i:i + 1], scale=8.0,
                                        accum_out=sums[:, hh:hh + 1])
                s.end(last); yield
                e = s.pe()
                for i in range(2):
                    for c in range(t + 1):
                        last = e.transpose(S[:, i, c * P:(c + 1) * P], p[:, i, c * P:(c + 1) * P], s.c["ident"])
                s.end(last); yield
                s.end(s.dve().tensor_copy(pt[:, :, 0:nk], S)); yield
                e = s.pe()
                for i in range(2):
                    hc = slice((2 * pair + i) * HD, (2 * pair + i + 1) * HD)
                    for c in range(t + 1):
                        last = e.matmul(s.a[:, i * HD:(i + 1) * HD], pt[:, i, c * P:(c + 1) * P], v[:, c, hc],
                                        start=(c == 0), stop=(c == t))
                s.end(last); yield
                s.end(s.act().activation(tok[:, pair * P:(pair + 1) * P], s.a[:, 0:P], ACT.Copy)); yield
            s.end(s.dve().reciprocal(sums, sums)); yield
            s.end(s.dve().tensor_tensor(heads(tok), heads(tok), over(sums.unsqueeze(2), [P, H, HD]), ALU.mult)); yield
            yield from to_channels(s, tok, v2(tmp, P), s.a)
            e = s.pe()
            for i in range(inner // P):
                last = e.matmul(s.b[:, 0:P], w[f"wo{d}"][:, i * P:(i + 1) * P], tmp[:, i * P:(i + 1) * P],
                                start=(i == 0), stop=(i == inner // P - 1))
            s.end(last); yield
            xs = x[:, bt * TOKENS + t * P:bt * TOKENS + (t + 1) * P]
            s.end(s.dve().tensor_tensor(xs, xs, s.b[:, 0:P], ALU.add)); yield
    s.used = mark
    yield from shift_tokens(s, x, h)
    yield from layer_norm(s, h, h, w[f"ln_g{d}"], w[f"ln_b{d}"])
    hid = w[f"w1{d}"].shape[-1] // 2
    sizes = [min(P, hid - i) for i in range(0, hid, P)]
    gate = s.take(COLS)
    for i, n in enumerate(sizes):
        ca, cg = i * P, hid + i * P
        s.end(s.pe().matmul(s.a[0:n, :], w[f"w1{d}"][:, cg:cg + n], h, start=True, stop=True)); yield
        s.end(s.act().activation(gate[0:n, :], s.a[0:n, :], ACT.Gelu, bias=w[f"b1g{d}"][0:n, i:i + 1])); yield
        s.end(s.pe().matmul(s.a[0:n, :], w[f"w1{d}"][:, ca:ca + n], h, start=True, stop=True)); yield
        s.end(s.dve().scalar_tensor_tensor(gate[0:n, :], s.a[0:n, :], w[f"b1a{d}"][0:n, i:i + 1], gate[0:n, :],
                                           ALU.add, ALU.mult)); yield
        s.end(s.pe().matmul(s.b, w[f"w2{d}"][0:n, i * P:(i + 1) * P], gate[0:n, :], start=(i == 0),
                            stop=(i == len(sizes) - 1))); yield
    s.end(s.dve().scalar_tensor_tensor(x, s.b, w[f"b2{d}"], x, ALU.add, ALU.add)); yield


def local_transformer(s, w):
    s.fresh()
    y = s.take(COLS)
    yield from layer_norm(s, s.x, y)
    for d in range(2):
        yield from local_layer(s, w, d, y)
    s.end(s.dve().tensor_tensor(s.x, s.x, y, ALU.add)); yield


def slot_memory(s, w):
    N, TOP = 64, 8
    B = PER_STREAM
    s.fresh()
    xn, alpha, x_tok, hT = s.take(COLS), s.take(TILES, N), s.take(TILES, P), s.take(COLS, parts=N)
    yield from layer_norm(s, s.x, xn)
    col = s.take(4)
    s.end(s.dve().tensor_reduce(col[:, 0:1], w["slots"], AX, ALU.add)); yield
    s.end(s.dve().tensor_scalar(col[:, 0:1], col[:, 0:1], 1.0 / N, None, ALU.mult)); yield
    s.end(s.pe().matmul(s.a[0:N, 0:1], w["w1s"], col[:, 0:1], start=True, stop=True)); yield
    s.end(s.dve().tensor_tensor(col[0:N, 1:2], w["b1"], s.a[0:N, 0:1], ALU.add)); yield
    s.end(s.dve().scalar_tensor_tensor(col[:, 2:3], w["tau"], -1.0, w["tau"], ALU.mult, ALU.max)); yield
    s.end(s.dve().tensor_scalar(col[:, 2:3], col[:, 2:3], 0.1, None, ALU.add)); yield
    s.end(s.dve().reciprocal(col[:, 2:3], col[:, 2:3])); yield
    s.end(s.pe().matmul(s.a[0:N, :], w["w1x"], xn, start=True, stop=True)); yield
    s.end(s.act().activation(hT, s.a[0:N, :], ACT.Gelu, bias=col[0:N, 1:2])); yield
    e = s.pe()
    for t in range(TILES):
        last = e.matmul(s.b[:, t * N:(t + 1) * N], hT[:, t * P:(t + 1) * P], w["w2"], start=True, stop=True)
    s.end(last); yield
    logits = s.take(TILES, N)
    s.end(s.dve().tensor_tensor(logits, over(w["b2"].unsqueeze(1), [P, TILES, N]), v2(s.b[:, 0:TILES * N], N), ALU.add)); yield
    s.end(s.dve().tensor_scalar(logits, logits, col[:, 2:3], None, ALU.mult)); yield
    top = yield from keep_top(s, logits, alpha, TOP, -1.5e38)
    s.end(s.dve().tensor_tensor(logits, logits, over(top[:, :, 0:1], [P, TILES, N]), ALU.subtract)); yield
    s.end(s.act().activation(logits, logits, ACT.Exp)); yield
    s.end(s.dve().tensor_tensor(alpha, alpha, logits, ALU.mult)); yield
    yield from row_scale(s, alpha, TILES, N)
    e = s.pe()
    for t in range(TILES):
        last = e.transpose(s.a[:, t * P:(t + 1) * P], xn[:, t * P:(t + 1) * P], s.c["ident"])
    s.end(last); yield
    s.end(s.act().activation(x_tok, v2(s.a, P), ACT.Copy)); yield
    e = s.pe()
    for bt in range(B):
        for i in range(2):
            last = e.matmul(s.a[:, bt * N:(bt + 1) * N], x_tok[:, 2 * bt + i, :], alpha[:, 2 * bt + i, :], start=(i == 0), stop=(i == 1))
    for bt in range(B):
        for i in range(2):
            last = e.matmul(s.b[:, bt * N:(bt + 1) * N], s.c["ones"], alpha[:, 2 * bt + i, :], start=(i == 0), stop=(i == 1))
    s.end(last); yield
    M = B * N
    si, gh, gi, new, tmp = s.take(M), s.take(3, N), s.take(3, M), s.take(M), s.take(M)
    s.end(s.dve().tensor_scalar(si, s.b[:, 0:M], 1e-8, None, ALU.add)); yield
    s.end(s.dve().reciprocal(si, si)); yield
    s.end(s.dve().tensor_tensor(si, si, s.a[:, 0:M], ALU.mult)); yield
    e = s.pe()
    for i in range(3):
        last = e.matmul(s.a[:, i * M:(i + 1) * M], w["Wih"][:, i * P:(i + 1) * P], si, start=True, stop=True)
    for i in range(3):
        last = e.matmul(s.b[:, i * N:(i + 1) * N], w["Whh"][:, i * P:(i + 1) * P], w["slots"], start=True, stop=True)
    s.end(last); yield
    e = s.dve()
    for i in range(3):
        e.tensor_scalar(gi[:, i, :], s.a[:, i * M:(i + 1) * M], w["bih"][:, i:i + 1], None, ALU.add)
        last = e.tensor_scalar(gh[:, i, :], s.b[:, i * N:(i + 1) * N], w["bhh"][:, i:i + 1], None, ALU.add)
    s.end(last); yield
    e = s.dve()
    for i in range(2):
        last = e.tensor_tensor(v2(gi[:, i, :], N), v2(gi[:, i, :], N), over(gh[:, i:i + 1, :], [P, B, N]), ALU.add)
    s.end(last); yield
    s.end(s.act().activation(gi[:, 0:2, :], gi[:, 0:2, :], ACT.Sigmoid)); yield
    s.end(s.dve().tensor_tensor(v2(tmp, N), v2(gi[:, 0, :], N), over(gh[:, 2:3, :], [P, B, N]), ALU.mult)); yield
    s.end(s.dve().tensor_tensor(tmp, tmp, gi[:, 2, :], ALU.add)); yield
    s.end(s.act().activation(new, tmp, ACT.Tanh)); yield
    s.end(s.dve().tensor_tensor(v2(tmp, N), over(w["slots"].unsqueeze(1), [P, B, N]), v2(new, N), ALU.subtract)); yield
    s.end(s.dve().tensor_tensor(tmp, tmp, gi[:, 1, :], ALU.mult)); yield
    s.end(s.dve().tensor_tensor(new, new, tmp, ALU.add)); yield
    DQ = w["wq"].shape[-1]
    qk, vt, pr, prT = s.take(2, M, parts=DQ), s.take(B, P, parts=N), s.take(B, N, parts=N), s.take(B, N, parts=N)
    m = s.take(B, parts=N)
    e = s.pe()
    e.matmul(s.a[0:DQ, 0:M], w["wq"], new, start=True, stop=True)
    e.matmul(s.a[0:DQ, M:2 * M], w["wk"], new, start=True, stop=True)
    for bt in range(B):
        last = e.matmul(s.b[0:N, bt * P:(bt + 1) * P], new[:, bt * N:(bt + 1) * N], w["wv"], start=True, stop=True)
    s.end(last); yield
    e = s.act()
    e.activation(qk[:, 0, :], s.a[0:DQ, 0:M], ACT.Identity, bias=w["bq"])
    s.end(e.activation(qk[:, 1, :], s.a[0:DQ, M:2 * M], ACT.Identity, bias=w["bk"])); yield
    s.end(s.dve().tensor_tensor(vt, over(w["bv"][0:N].unsqueeze(1), [N, B, P]), v2(s.b[0:N, 0:B * P], P), ALU.add)); yield
    e = s.pe()
    for bt in range(B):
        last = e.matmul(s.a[0:N, bt * N:(bt + 1) * N], qk[:, 0, bt * N:(bt + 1) * N], qk[:, 1, bt * N:(bt + 1) * N], start=True, stop=True)
    s.end(last); yield
    S = v2(s.a[0:N, 0:M], N)
    s.end(s.dve().tensor_reduce(m, S, AX, ALU.max)); yield
    s.end(s.dve().tensor_scalar(m, m, -DQ ** -0.5, None, ALU.mult)); yield
    e = s.act()
    for bt in range(B):
        last = e.activation(pr[:, bt, :], S[:, bt, :], ACT.Exp, bias=m[:, bt:bt + 1], scale=DQ ** -0.5)
    s.end(last); yield
    s.end(s.dve().tensor_reduce(m, pr, AX, ALU.add)); yield
    s.end(s.dve().reciprocal(m, m)); yield
    s.end(s.dve().tensor_tensor(pr, pr, over(m.unsqueeze(2), [N, B, N]), ALU.mult)); yield
    e = s.pe()
    for bt in range(B):
        last = e.transpose(s.b[0:N, bt * N:(bt + 1) * N], pr[:, bt, :], s.c["ident"][0:N, 0:N])
    s.end(last); yield
    s.end(s.act().activation(prT, v2(s.b[0:N, 0:M], N), ACT.Copy)); yield
    e = s.pe()
    for bt in range(B):
        last = e.matmul(s.a[:, bt * N:(bt + 1) * N], vt[:, bt, :], prT[:, bt, :], start=True, stop=True)
    s.end(last); yield
    s.end(s.dve().tensor_tensor(new, new, s.a[:, 0:M], ALU.add)); yield
    yield from layer_norm(s, new, new, w["ln_g"], w["ln_b"])
    e = s.pe()
    for bt in range(B):
        last = e.matmul(s.a[0:N, bt * P:(bt + 1) * P], new[:, bt * N:(bt + 1) * N], w["wvp"], start=True, stop=True)
    for t in range(TILES):
        last = e.transpose(s.b[0:N, t * P:(t + 1) * P], alpha[:, t, :], s.c["ident"])
    s.end(last); yield
    s.end(s.dve().tensor_tensor(vt, over(w["bvp"][0:N].unsqueeze(1), [N, B, P]), v2(s.a[0:N, 0:B * P], P), ALU.add)); yield
    s.end(s.act().activation(hT, s.b[0:N, :], ACT.Copy)); yield
    e = s.pe()
    for bt in range(B):
        c = slice(bt * TOKENS, (bt + 1) * TOKENS)
        last = e.matmul(s.a[:, c], vt[:, bt, :], hT[:, c], start=True, stop=True)
    s.end(last); yield
    s.end(s.act().activation(xn, s.a, ACT.Copy)); yield
    s.end(s.pe().matmul(s.b, w["wo"], xn, start=True, stop=True)); yield
    s.end(s.dve().scalar_tensor_tensor(s.x, s.b, w["bo"], s.x, ALU.add, ALU.add)); yield


NETWORK = [
    ("L0_scan", lambda s, w: scan_block(s, w, conv=False, a_is_exp=False, clip=(0.001, 0.1))),
    ("L0_experts", expert_mix),
    ("L0_linear", linear_attention),
    ("L0_experts", expert_mix),
    ("L1_gla", gated_linear_attention),
    ("L1_local", local_transformer),
    ("L1_attn", lambda s, w: attention(s, w, latent=True, masked=False)),
    ("L1_local", local_transformer),
    ("L2_scan", lambda s, w: scan_block(s, w, conv=True, a_is_exp=True, clip=None)),
    ("L2_experts", expert_swiglu),
    ("L2_attn", lambda s, w: attention(s, w, latent=False, masked=True)),
    ("L2_experts", expert_swiglu),
    ("L3_blocks", block_attention),
    ("L3_slots", slot_memory),
    ("L3_gqa", grouped_query_attention),
    ("L3_slots", slot_memory),
]
SHARED = ("L0_experts", "L2_experts")


def build(nc, x_dram, out_dram, packed_dram, where, network):
    with ExitStack() as ctx:
        core = Core(nc, ctx)
        engines = core.engines
        groups = ["constants"] + [g for i, (g, _) in enumerate(network) if g not in [n for n, _ in network[:i]]]
        for g in groups + ["x"]:
            core.sems[f"load_{g}"] = ctx.enter_context(nc.semaphore(f"load_{g}"))
        stored = ctx.enter_context(nc.semaphore("stored"))
        width = {g: packed_dram[g].shape[1] for g in groups}
        shared = ctx.enter_context(nc.sbuf_tensor("experts", [P, max(packed_dram[g].shape[1] for g in SHARED)], F32))
        weights = {}
        for g in groups:
            buf = shared if g in SHARED else ctx.enter_context(nc.sbuf_tensor(f"w_{g}", [P, width[g]], F32))
            weights[g] = Weights(buf, where[g])
        x = ctx.enter_context(nc.sbuf_tensor("x", [P, BATCHES * TOKENS], F32))
        scratch = ctx.enter_context(nc.sbuf_tensor("scratch", [P, N_STREAMS * SCRATCH], F32))
        psum = ctx.enter_context(nc.psum_tensor("psum", [P, N_STREAMS * 2 * BANK], F32))

        def load(g):
            nc.sync.dma_start(weights[g].buf[:, 0:width[g]], packed_dram[g]).then_inc(core.sems[f"load_{g}"], 16)

        n = packed_dram["masks"].shape[1]
        core.sems["load_masks"] = ctx.enter_context(nc.semaphore("load_masks"))
        bf16_masks = Weights(ctx.enter_context(nc.sbuf_tensor("bf16_masks", [P, n], BF16)), where["masks"])
        load("constants")
        nc.sync.dma_start(x[:, :], x_dram).then_inc(core.sems["load_x"], 16)
        staged = scratch[:, (N_STREAMS - 1) * SCRATCH:][:, 0:n]
        nc.sync.dma_start(staged, packed_dram["masks"]).then_inc(core.sems["load_masks"], 16)
        for g in groups[1:]:
            if g != SHARED[1]:
                load(g)

        streams = [Stream(core, i, x[:, i * COLS:(i + 1) * COLS], scratch[:, i * SCRATCH:(i + 1) * SCRATCH],
                          psum[:, i * 2 * BANK:(i + 1) * 2 * BANK], weights["constants"], bf16_masks) for i in range(N_STREAMS)]
        streams[0].needs("constants")
        streams[0].needs("x")
        streams[0].needs("masks")
        streams[-1].end(streams[-1].act().activation(bf16_masks.buf[:, :], staged, ACT.Copy))
        core.wait("pe", *streams[-1].last)
        for i, (g, block) in enumerate(network):
            if g == SHARED[1] and g not in [n for n, _ in network[:i]]:
                for s in streams:
                    if s.past_first_experts:
                        core.wait("sp", *s.past_first_experts)
                load(g)
            streams[0].needs(g)
            if g == "L1_local" and weights[g].extra is None:
                weights[g].extra = ctx.enter_context(nc.sbuf_tensor("xpos", [P, 8 * TOKENS // P * 64], F32))
                prepare_xpos(streams[0], weights[g])
                for s in streams[1:]:
                    s.wait_all(*streams[0].last)
            running = [block(s, weights[g]) for s in streams]
            while running:
                for r in list(running):
                    try:
                        next(r)
                    except StopIteration:
                        running.remove(r)
            if g == SHARED[0]:
                for s in streams:
                    s.past_first_experts = s.last
        for i, s in enumerate(streams):
            core.wait("sp", *s.last)
            nc.sync.dma_start(out_dram[:, i * COLS:(i + 1) * COLS], s.x).then_inc(stored, 16)
        nc.sync.wait_ge(stored, 16 * N_STREAMS)


def kernel(**inputs):
    import concourse.bacc as bacc
    from concourse.bass_utils import run_bass_kernel_spmd

    p = {k: np.asarray(v) for k, v in inputs.items()}
    packs = {"constants": pack(constants()), "masks": pack(masks()), **{g: pack(parts) for g, parts in layouts(p).items()}}
    x = np.ascontiguousarray(p["L0_attn_a_x"].reshape(BATCHES * TOKENS, P).T)
    nc = bacc.Bacc("TRN2", target_bir_lowering=False, num_devices=1)
    arrays = {"x_dram": x, **{f"{g}_dram": a for g, (a, _) in packs.items()}}
    aps = {n: nc.dram_tensor(n, a.shape, F32, kind="ExternalInput").ap() for n, a in arrays.items()}
    out = nc.dram_tensor("out_dram", x.shape, F32, kind="ExternalOutput").ap()
    build(nc, aps["x_dram"], out, {g: aps[f"{g}_dram"] for g in packs}, {g: w for g, (_, w) in packs.items()}, NETWORK)
    r = run_bass_kernel_spmd(nc, [arrays], core_ids=[0])
    y = r.results[0]["out_dram"]
    return np.ascontiguousarray(y.T).reshape(BATCHES, TOKENS, P)
```

```python
from contextlib import ExitStack

import numpy as np

import concourse.bass as bass
from concourse import mybir

ALU = mybir.AluOpType
ACT = mybir.ActivationFunctionType
F32 = mybir.dt.float32
BF16 = mybir.dt.bfloat16
AX = mybir.AxisListType.X

P = 128
BATCHES, TOKENS = 8, 256
N_STREAMS = 4
PER_STREAM = BATCHES // N_STREAMS
COLS = PER_STREAM * TOKENS
TILES = COLS // P
BANK = 512
HEADS8, HD8 = 16, 8
NEG = -1.0e30


def k_tiles(w):
    k, n = w.shape
    nt = -(-k // P)
    out = np.zeros((nt * P, n), w.dtype)
    out[:k] = w
    return out.reshape(nt, P, n).transpose(1, 0, 2).reshape(P, nt * n)


def as_cols(v):
    return k_tiles(v.reshape(-1, 1))


def as_rows(v):
    return np.broadcast_to(v.reshape(1, -1), (P, v.size))


def pack(parts):
    where, at = {}, 0
    for name, a in parts.items():
        where[name] = (at, a.shape[0], a.shape[1])
        at += a.shape[1]
    out = np.zeros((P, at), np.float32)
    for name, a in parts.items():
        c, r, n = where[name]
        out[:r, c:c + n] = a
    return out, where


def constants():
    ch = np.arange(P)
    c = {"ident": np.eye(P), "mean": np.full((P, P), 1.0 / P), "center": np.eye(P) - 1.0 / P,
         "ones": np.ones((P, P))}
    g8 = (ch[:, None] // HD8 == ch[None] // HD8).astype(float)
    c["group8"] = g8
    c["mean8"] = g8 / HD8
    c["center8"] = np.eye(P) - g8 / HD8
    c["head_of_row_group"] = (ch[:, None] % 32 // HD8 == np.arange(4)[None]).astype(float)
    c["head_of_col_group"] = np.tile(c["head_of_row_group"].T.reshape(1, -1), (P, 1))
    c["expand16"] = (np.arange(HEADS8)[:, None] == ch[None] // HD8).astype(float)
    c["expand8"] = (np.arange(8)[:, None] == np.arange(4 * P)[None] // 64).astype(float)
    q, k = np.arange(P)[:, None], np.arange(P)[None]
    c["keys_up_to_query"] = (q <= k).astype(float)
    kk = np.arange(TOKENS)[None]
    for t in range(2):
        c[f"block32_{t}"] = ((q + t * P) // 32 >= kk // 32).astype(float)
    rot = np.zeros((P, P))
    for i in range(0, P, 2):
        rot[i + 1, i] = -1.0
        rot[i, i + 1] = 1.0
    c["pair_rotation"] = rot
    f = np.float32
    for name, base in (("global", 1000000.0), ("local", 10000.0)):
        inv = (f(1.0) / f(base) ** (np.arange(0, HD8, 2, dtype=f) / f(HD8))).astype(f)
        ang = (np.arange(TOKENS, dtype=f)[:, None] * inv[None]).astype(f)
        ang = ang[:, (ch % HD8) // 2].T
        c[f"cos_{name}"], c[f"sin_{name}"] = np.cos(ang), np.sin(ang)
    hd, window = 64, 64
    half = np.arange(0, hd, 2, dtype=f)
    inv = (f(1.0) / f(10000.0) ** (half / f(hd))).astype(f)
    t = np.arange(TOKENS, dtype=f)
    ang = (t[:, None] * inv[None]).astype(f)
    scale = ((half + f(0.4 * hd)) / f(1.4 * hd))[None] ** ((t - TOKENS // 2) / f(window // 2))[:, None]
    scale = scale.astype(f)
    for name, s in (("q", scale), ("k", (f(1.0) / scale).astype(f))):
        cs, sn = np.cos(ang) * s, np.sin(ang) * s
        c[f"xpos_cos_{name}"] = k_tiles(np.concatenate([cs, cs], 1))
        c[f"xpos_sin_{name}"] = k_tiles(np.concatenate([-sn, sn], 1))
    c["eps"] = np.tile(np.array([[1e-5, 1e-12, 1e-6]]), (P, 1))
    return {k: np.ascontiguousarray(v, np.float32) for k, v in c.items()}


def masks():
    out = {"ident": np.eye(P)}
    q, k = np.arange(P)[:, None], np.arange(TOKENS)[None]
    for name, band in (("causal", TOKENS), ("band32", 31), ("band64", 64)):
        for t in range(2):
            first = 64 if (name, t) == ("band64", 1) else 0
            d = (q + t * P) - k[:, first:(t + 1) * P]
            out[f"{name}_{t}"] = np.where((d >= 0) & (d <= band), 0.0, NEG)
    out["row_of_32"] = np.tile(np.eye(32), (3, 1))
    out["row_of_8"] = np.tile(np.eye(8), (3, 1))
    out["spread"] = gla_spread()
    return {k: v.astype(np.float32) for k, v in out.items()}


def gla_spread(K=32):
    per = P // K
    row, p = np.arange(K)[:, None], np.arange(P)[None]
    tiles = [(row == per * i + p // K) for i in range(K // per)]
    return np.tile(np.concatenate(tiles, 1).astype(np.float32), (3, 1))


def scan_layout(p, w_in, w_xproj, w_dt, b_dt, a_log, d, w_out):
    return {"w_in": p[w_in], "w_rank": k_tiles(p[w_xproj][:, :p[w_dt].shape[0]]),
            "w_bc": k_tiles(np.tile(p[w_xproj][:, p[w_dt].shape[0]:], (1, 3))), "w_dt": p[w_dt], "b_dt": as_cols(p[b_dt]),
            "a_log": k_tiles(p[a_log]), "d": as_cols(p[d]), "w_out": k_tiles(p[w_out])}


def layouts(p):
    g = {}
    g["L0_scan"] = scan_layout(p, *(f"L0_attn_a_{n}" for n in
                                    ("W_in", "W_xproj", "W_dt", "b_dt", "A_log", "D", "W_out")))
    n = "L0_attn_b_"
    w0 = np.zeros((P, P), np.float32)
    for h in range(HEADS8):
        w0[h * HD8:(h + 1) * HD8, h * HD8:(h + 1) * HD8] = p[n + "W_init"][0, h]
    g["L0_linear"] = {**{w: p[n + w].T for w in ("Wq", "Wk", "Wv", "Wg", "Wo")},
                      **{w: p[n + w] for w in ("conv_q", "conv_k", "conv_v")}, "state0": w0,
                      "ln_gamma": as_cols(np.tile(p[n + "ln_gamma"], HEADS8)),
                      "ln_beta": as_cols(np.tile(p[n + "ln_beta"], HEADS8))}
    n = "L0_ffn_"
    e = p[n + "w1"].shape[0]
    g["L0_experts"] = {"w_route": np.concatenate([p[n + "lang_w"], p[n + "router_w"]]).T,
                       "b_route": as_rows(np.concatenate([p[n + "lang_b"], p[n + "router_b"]])),
                       "b1": as_cols(p[n + "b1"].reshape(-1)), "b2": np.tile(p[n + "b2"], (3, 1)),
                       "w1": p[n + "w1"].transpose(1, 0, 2).reshape(P, -1),
                       "w2": k_tiles(p[n + "w2"].reshape(-1, P))}
    n = "L1_attn_a_"
    g["L1_gla"] = {**{f"w{c}": np.tile(p[n + "W" + c], (1, 3)) for c in "qkg"},
                   **{f"b{c}": np.tile(p[n + "b" + c], 3).reshape(-1, 1) for c in "qkg"},
                   "wv": np.tile(p[n + "Wv"], (1, 4)), "bv": as_cols(np.tile(p[n + "bv"], 4)),
                   "Wo": np.tile(p[n + "Wo"], (4, 1)), "bo": as_cols(p[n + "bo"])}
    n = "L1_attn_b_"
    g["L1_attn"] = {**{w: p[n + w] for w in ("Wq", "Wl", "Wk", "Wv", "Wo")},
                    **{w: as_cols(p[n + w]) for w in ("bq", "bk", "bo")},
                    "bl": p[n + "bl"].reshape(-1, 1), "bv": as_rows(p[n + "bv"])}
    n = "L1_ffn_"
    g["L1_local"] = {}
    for d in range(p[n + "wqkv"].shape[0]):
        g["L1_local"].update({
            f"wqkv{d}": p[n + "wqkv"][d], f"q_scale{d}": as_rows(p[n + "q_scale"][d]),
            f"k_scale{d}": as_rows(p[n + "k_scale"][d]), f"wo{d}": k_tiles(p[n + "wo"][d]),
            f"ln_g{d}": as_cols(p[n + "ln_g"][d]), f"ln_b{d}": as_cols(p[n + "ln_b"][d]),
            f"w1{d}": p[n + "w1"][d], f"w2{d}": k_tiles(p[n + "w2"][d]), f"b2{d}": as_cols(p[n + "b2"][d]),
            f"b1a{d}": as_cols(np.split(p[n + "b1"][d], 2)[0]),
            f"b1g{d}": as_cols(np.split(p[n + "b1"][d], 2)[1])})
    n = "L2_attn_a_"
    g["L2_scan"] = scan_layout(p, *(n + w for w in ("in_proj_w", "x_proj_w", "dt_proj_w", "dt_proj_b",
                                                    "A_log", "D", "out_proj_w")))
    g["L2_scan"]["conv_w"] = k_tiles(p[n + "conv_w"][:, 0])
    g["L2_scan"]["conv_b"] = as_cols(p[n + "conv_b"])
    n = "L2_attn_b_"
    g["L2_attn"] = {**{w: p[n + w].T for w in ("Wq", "Wk", "Wv", "Wo")},
                    **{w: as_cols(p[n + w]) for w in ("bq", "bk", "bo")}, "bv": as_rows(p[n + "bv"])}
    n = "L2_ffn_"
    g["L2_experts"] = {"w_route": p[n + "gate_w"].T,
                       "w1": p[n + "w1"].transpose(1, 0, 2).reshape(P, -1),
                       "w3": p[n + "w3"].transpose(1, 0, 2).reshape(P, -1),
                       "w2": np.concatenate([k_tiles(p[n + "w2"][i]) for i in range(e)], 1)}
    n = "L3_attn_a_"
    g["L3_blocks"] = {"w_qkv": p[n + "qkv_w"].T, "Wo": p[n + "proj_w"].T, "bo": as_cols(p[n + "proj_b"])}
    n = "L3_attn_b_"

    def over_heads(w):
        return np.repeat(w.reshape(w.shape[0], -1, HD8), HEADS8 * HD8 // w.shape[1], axis=1).reshape(w.shape[0], P)

    g["L3_gqa"] = {"norm1": as_cols(p[n + "norm1_w"]), "norm2": as_cols(p[n + "norm2_w"]),
                   "g_wq": p[n + "g_wq"], "g_down": p[n + "g_kv_down"], "g_wk": over_heads(p[n + "g_k_up"]),
                   "g_wv": over_heads(p[n + "g_v_up"]), "g_wo": p[n + "g_wo"], "l_wq": p[n + "l_wq"],
                   "l_wk": over_heads(p[n + "l_wk"]), "l_wv": over_heads(p[n + "l_wv"]), "l_wo": p[n + "l_wo"]}
    n = "L3_ffn_"
    g["L3_slots"] = {"slots": p[n + "slot_init"].T, "w1x": p[n + "w1"][:P], "w1s": p[n + "w1"][P:],
                     "b1": p[n + "b1"].reshape(-1, 1), "w2": p[n + "w2"], "b2": as_rows(p[n + "b2"]),
                     "tau": as_rows(p[n + "tau"]), "Wih": p[n + "Wih"].T, "Whh": p[n + "Whh"].T,
                     "bih": as_cols(p[n + "bih"]), "bhh": as_cols(p[n + "bhh"]),
                     "wq": p[n + "wq"], "bq": p[n + "bq"].reshape(-1, 1), "wk": p[n + "wk"],
                     "bk": p[n + "bk"].reshape(-1, 1), "wv": p[n + "wv"], "bv": as_rows(p[n + "bv"]),
                     "ln_g": as_cols(p[n + "ln_g"]), "ln_b": as_cols(p[n + "ln_b"]), "wvp": p[n + "wvp"],
                     "bvp": as_rows(p[n + "bvp"]), "wo": p[n + "wo"], "bo": as_cols(p[n + "bo"])}
    return g


class Core:

    def __init__(self, nc, ctx):
        self.nc = nc
        self.engines = {"pe": nc.tensor, "act": nc.scalar, "dve": nc.vector, "pool": nc.gpsimd, "sp": nc.sync}
        self.sems = {e: ctx.enter_context(nc.semaphore(f"steps_{e}")) for e in ("pe", "act", "dve", "pool")}
        self.count = dict.fromkeys(self.sems, 0)
        self.waited = {}

    def wait(self, engine, sem_name, value):
        if self.waited.get((engine, sem_name), 0) < value:
            self.waited[engine, sem_name] = value
            self.engines[engine].wait_ge(self.sems[sem_name], value)

    def count_up(self, engine, instruction):
        self.count[engine] += 1
        instruction.then_inc(self.sems[engine], 1)
        return engine, self.count[engine]


class Weights:

    def __init__(self, buf, where):
        self.buf, self.where, self.extra = buf, where, None
        self.prepared = None

    def __getitem__(self, name):
        c, r, n = self.where[name]
        return self.buf[0:r, c:c + n]


class Stream:

    def __init__(self, core, index, x, scratch, psum, const, masks):
        self.core, self.index, self.x, self.scratch, self.psum = core, index, x, scratch, psum
        self.c, self.m = const, masks
        if psum is not None:
            self.a, self.b = psum[:, 0:BANK], psum[:, BANK:2 * BANK]
        self.last, self.engine, self.used = (), None, 0


    def _on(self, engine):
        for step in self.last:
            self.core.wait(engine, *step)
        self.engine = engine
        return self.core.engines[engine]

    def pe(self):
        return self._on("pe")

    def act(self):
        return self._on("act")

    def dve(self):
        return self._on("dve")

    def pool(self):
        return self._on("pool")

    def end(self, instruction):
        self.last = (self.core.count_up(self.engine, instruction),)

    def needs(self, group):
        for e in ("pe", "act", "dve", "pool"):
            self.core.wait(e, f"load_{group}", 16)

    def wait_all(self, engine, value):
        for e in ("dve", "pool"):
            self.core.wait(e, engine, value)

    def branch(self, i, scratch):
        base = self.used
        self.take(scratch)
        b = Stream(self.core, self.index, self.x, self.scratch[:, base:base + scratch], None, self.c, self.m)
        b.a, b.last = (self.a, self.b)[i], self.last
        return b

    def twin(self):
        t = Stream(self.core, self.index, self.x, self.scratch, self.psum, self.c, self.m)
        t.last, t.used = self.last, self.used
        return t

    def join(self, branches, chains, skew):
        behind = [i * skew for i in range(len(chains))]
        going = list(range(len(chains)))
        while going:
            for i in list(going):
                if behind[i]:
                    behind[i] -= 1
                    continue
                try:
                    next(chains[i])
                except StopIteration:
                    going.remove(i)
            yield
        self.last = tuple(step for b in branches for step in b.last)

    def take_bf16(self, n, parts=P):
        return self.take(n // 2, parts=parts).bitcast(BF16)

    def fresh(self):
        self.used = 0

    def take(self, *shape, parts=P):
        n = int(np.prod(shape))
        ap = self.scratch[0:parts, self.used:self.used + n]
        self.used += n
        assert self.used <= self.scratch.shape[1], (self.used, shape)
        if len(shape) == 2:
            ap = ap.rearrange("p (a b) -> p a b", b=shape[1])
        if len(shape) == 3:
            ap = ap.rearrange("p (a b c) -> p a b c", b=shape[1], c=shape[2])
        return ap


SCRATCH = 6144

SKEW = 3
BRANCH_SKEW = 3


def in_turns(chains):
    while chains:
        for c in list(chains):
            try:
                next(c)
            except StopIteration:
                chains.remove(c)
                continue
            yield


def v2(ap, n):
    return ap.rearrange("p (a b) -> p a b", b=n)


def over(ap, shape):
    return ap.broadcast_to(shape)


def normalise(s, src, out, center, mean, eps, gain=None, shift=None):
    n = src.shape[-1]
    mark = s.used
    sq = s.take(n)
    a, b = s.a[:, 0:n], s.b[:, 0:n]
    centred = src
    if center is not None:
        s.end(s.pe().matmul(a, center, src, start=True, stop=True)); yield
        centred = a
    s.end(s.act().activation(sq, centred, ACT.Square)); yield
    s.end(s.pe().matmul(b, mean, sq, start=True, stop=True)); yield
    s.end(s.act().activation(sq, b, ACT.Ln, bias=eps)); yield
    s.end(s.act().activation(sq, sq, ACT.Exp, scale=-0.5)); yield
    s.end(s.dve().tensor_tensor(out, centred, sq, ALU.mult)); yield
    if gain is not None:
        if shift is not None:
            s.end(s.dve().tensor_scalar(out, out, gain, shift, ALU.mult, ALU.add)); yield
        else:
            s.end(s.dve().tensor_scalar(out, out, gain, None, ALU.mult)); yield
    s.used = mark


def layer_norm(s, src, out, gain=None, shift=None):
    yield from normalise(s, src, out, s.c["center"], s.c["mean"], s.c["eps"][:, 0:1], gain, shift)


def to_channels(s, src, dst, bank):
    t = dst.shape[1]
    e = s.pe()
    for i in range(t):
        last = e.transpose(bank[:, i * P:(i + 1) * P], src[:, i * P:(i + 1) * P], s.c["ident"])
    s.end(last); yield
    s.end(s.act().activation(dst, v2(bank[:, 0:t * P], P), ACT.Copy)); yield


def split_rows(s, src, parts):
    mark = s.used
    n = src.shape[-1]
    rest = s.take(n)
    s.end(s.act().activation(parts, src, ACT.Copy)); yield
    s.end(s.dve().tensor_tensor(rest[0:64], src[0:64], parts[0:64], ALU.subtract)); yield
    s.end(s.dve().tensor_copy(parts[0:64], rest[0:64])); yield
    s.end(s.dve().tensor_tensor(rest[0:32], rest[0:32], parts[0:32], ALU.subtract)); yield
    s.end(s.dve().tensor_copy(parts[0:32], rest[0:32])); yield
    s.used = mark


def scan_block(s, w, conv, a_is_exp, clip):
    D, N = 2, 16
    rank = w["w_dt"].shape[0]
    T = TOKENS
    s.fresh()
    xn = s.take(COLS)
    yield from layer_norm(s, s.x, xn)
    xc, delta, dx = (s.take(D, T) for _ in range(3))
    mark = s.used
    padded = s.take(D, T + 3)
    s.used = mark
    bcn2, a2, b2 = ([s.take(D, T), s.take(D, T)] for _ in range(3))
    b = b2[0]
    low = s.take(T, parts=rank)
    bc = s.take_bf16(T, parts=3 * 2 * N)
    A = s.take(D, N)
    s.end(s.act().activation(A, v2(w["a_log"], N), ACT.Exp)); yield
    s.end(s.dve().tensor_scalar(A, A, -1.0, None, ALU.mult)); yield
    for a in a2:
        s.end(s.dve().memset(a, 0.0)); yield
    A2, B2 = v2(s.a, T), v2(s.b, T)
    for bt in range(PER_STREAM):
        xb = xn[:, bt * T:(bt + 1) * T]
        e = s.pe()
        for d in range(D):
            last = e.matmul(A2[:, d, :], w["w_in"][:, d * P:(d + 1) * P], xb, start=True, stop=True)
        s.end(last); yield
        if conv:
            s.end(s.dve().memset(padded[:, :, 0:3], 0.0)); yield
            s.end(s.dve().tensor_copy(padded[:, :, 3:3 + T], A2)); yield
            taps = v2(w["conv_w"], 4)
            for k in range(4):
                e = s.dve()
                for d in range(D):
                    tap = taps[:, d, k:k + 1]
                    if k == 0:
                        last = e.tensor_scalar(b[:, d, :], padded[:, d, 0:T], tap, w["conv_b"][:, d:d + 1],
                                               ALU.mult, ALU.add)
                    else:
                        last = e.scalar_tensor_tensor(b[:, d, :], padded[:, d, k:k + T], tap, b[:, d, :],
                                                      ALU.mult, ALU.add)
                s.end(last); yield
            s.end(s.act().activation(xc, b, ACT.Silu)); yield
        else:
            s.end(s.dve().tensor_copy(xc, A2)); yield
        e = s.pe()
        for d in range(D):
            last = e.matmul(s.a[0:rank, 0:T], w["w_rank"][:, d * rank:(d + 1) * rank], xc[:, d, :],
                            start=(d == 0), stop=(d == D - 1))
        for d in range(D):
            last = e.matmul(s.b[0:6 * N, 0:T], w["w_bc"][:, d * 6 * N:(d + 1) * 6 * N], xc[:, d, :],
                            start=(d == 0), stop=(d == D - 1))
        s.end(last); yield
        s.end(s.dve().tensor_copy(low, s.a[0:rank, 0:T])); yield
        yield from split_rows(s, s.b[0:6 * N, 0:T], bc)
        e = s.pe()
        for d in range(D):
            last = e.matmul(B2[:, d, :], w["w_dt"][:, d * P:(d + 1) * P], low, start=True, stop=True)
        s.end(last); yield
        e = s.act()
        for d in range(D):
            last = e.activation(delta[:, d, :], B2[:, d, :], ACT.Identity, bias=w["b_dt"][:, d:d + 1])
        s.end(last); yield
        s.end(s.dve().scalar_tensor_tensor(dx, delta, -1.0, delta, ALU.mult, ALU.max)); yield
        s.end(s.act().activation(dx, dx, ACT.Exp, scale=-1.0)); yield
        s.end(s.act().activation(dx, dx, ACT.Ln, bias=1.0)); yield
        s.end(s.dve().scalar_tensor_tensor(delta, delta, 0.0, dx, ALU.max, ALU.add)); yield
        if clip:
            s.end(s.dve().tensor_scalar(delta, delta, clip[0], clip[1], ALU.max, ALU.min)); yield
        s.end(s.dve().tensor_tensor(dx, delta, xc, ALU.mult)); yield

        make, use = s.twin(), s.twin()
        made, used = {}, {-2: s.last, -1: s.last}

        def make_state(n):
            a, b, bcn = a2[n % 2], b2[n % 2], bcn2[n % 2]
            make.last += used[n - 2]
            e = make.pe()
            for i in range(2):
                row = i * N + n
                last = e.matmul(B2[:, i, :], over(s.m["row_of_32"][:, row:row + 1], [6 * N, P]), bc, start=True, stop=True)
            make.end(last); yield
            make.end(make.act().activation(bcn, B2, ACT.Copy)); yield
            make.end(make.pool().tensor_tensor(b, dx, over(bcn[:, 0:1, :], [P, D, T]), ALU.mult))
            b_done = make.last
            e = core_act
            for d in range(D):
                last = e.activation(a[:, d, 1:T], delta[:, d, 1:T], ACT.Exp if a_is_exp else ACT.Identity,
                                    scale=A[:, d, n:n + 1], bias=0.0 if a_is_exp else 1.0)
            make.last = (s.core.count_up("act", last),)
            made[n] = make.last + b_done; yield

        def use_state(n):
            a, b, bcn = (x.rearrange("p a b -> p (a b)") for x in (a2[n % 2], b2[n % 2], bcn2[n % 2]))
            use.last += made[n]
            use.end(use.dve().tensor_tensor_scan(b, a, b, 0.0, ALU.mult, ALU.add)); yield
            use.end(use.dve().tensor_tensor(b2[n % 2], b2[n % 2], over(bcn2[n % 2][:, 1:2, :], [P, D, T]), ALU.mult)); yield
            use.end(use.pe().matmul(s.a, s.c["ident"], b, start=(n == 0), stop=(n == N - 1)))
            used[n] = use.last; yield

        core_act = s.core.engines["act"]
        for n in range(N + 1):
            yield from in_turns([use_state(n - 1)] * (n > 0) + [make_state(n)] * (n < N))
        s.last = use.last
        a, b = a2[0], b2[0]
        z = b2[1]
        e = s.pe()
        for d in range(D):
            last = e.matmul(B2[:, d, :], w["w_in"][:, (D + d) * P:(D + d + 1) * P], xb, start=True, stop=True)
        s.end(last); yield
        s.end(s.act().activation(z, B2, ACT.Silu)); yield
        e = s.dve()
        for d in range(D):
            last = e.scalar_tensor_tensor(b[:, d, :], xc[:, d, :], w["d"][:, d:d + 1], A2[:, d, :], ALU.mult, ALU.add)
        s.end(last); yield
        s.end(s.dve().tensor_tensor(b, b, z, ALU.mult)); yield
        e = s.pe()
        for d in range(D):
            last = e.matmul(s.b[:, 0:T], w["w_out"][:, d * P:(d + 1) * P], b[:, d, :], start=(d == 0), stop=(d == D - 1))
        s.end(last); yield
        xs = s.x[:, bt * T:(bt + 1) * T]
        s.end(s.dve().tensor_tensor(xs, xs, s.b[:, 0:T], ALU.add)); yield


def linear_attention(s, w):
    s.fresh()
    T = TOKENS
    xn = s.take(COLS)
    yield from layer_norm(s, s.x, xn)
    padded = s.take(PER_STREAM, T + 3)
    s.end(s.dve().memset(padded[:, :, 0:3], 0.0)); yield
    q, k, v = (s.take(COLS) for _ in range(3))
    for name, dst in (("q", q), ("k", k), ("v", v)):
        s.end(s.pe().matmul(s.a, w[f"W{name}"], xn, start=True, stop=True)); yield
        s.end(s.act().activation(padded[:, :, 3:], v2(s.a, T), ACT.Copy)); yield
        taps, y = w[f"conv_{name}"], v2(dst, T)
        for j in range(4):
            s.end(s.dve().scalar_tensor_tensor(y, padded[:, :, j:j + T], taps[:, j:j + 1],
                                               padded[:, :, 3:] if j == 0 else y, ALU.mult, ALU.add)); yield
        s.end(s.act().activation(dst, dst, ACT.Silu)); yield
        if name != "v":
            yield from normalise(s, dst, dst, None, s.c["group8"], s.c["eps"][:, 1:2])
    v_tok, k_tok = s.take(TILES, P), s.take(PER_STREAM, P)
    e = s.pe()
    for t in range(TILES):
        last = e.transpose(s.a[:, t * P:(t + 1) * P], v[:, t * P:(t + 1) * P], s.c["ident"])
    for bt in range(PER_STREAM):
        last = e.transpose(s.b[:, bt * P:(bt + 1) * P], k[:, bt * T:bt * T + P], s.c["ident"])
    s.end(last); yield
    s.end(s.act().activation(v_tok, v2(s.a, P), ACT.Copy)); yield
    s.end(s.act().activation(k_tok, v2(s.b[:, 0:PER_STREAM * P], P), ACT.Copy)); yield
    state = s.take(P)
    o = v
    qm, st, vm = s.take(4, P), s.take(4, P), s.take(4, P)
    for t in range(TILES):
        bt, chunk = divmod(t, T // P)
        cols = slice(t * P, (t + 1) * P)
        if chunk == 0:
            carried = w["state0"]
        else:
            s.end(s.pe().matmul(s.a[:, 0:P], k_tok[:, bt, :], v_tok[:, t - 1, :], start=True, stop=True)); yield
            s.end(s.dve().tensor_tensor(state, s.c["group8"], s.a[:, 0:P], ALU.mult)); yield
            s.end(s.dve().tensor_tensor(state, state, w["state0"], ALU.add)); yield
            carried = state
        e = s.dve()
        for j in range(4):
            last = e.tensor_scalar(qm[:, j, :], q[:, cols], s.c["head_of_row_group"][:, j:j + 1], None, ALU.mult)
        s.end(last); yield
        s.end(s.pool().tensor_tensor(vm, over(v_tok[:, t:t + 1, :], [P, 4, P]), v2(s.c["head_of_col_group"], P), ALU.mult)); yield
        s.end(s.pe().matmul(s.b[:, 0:P], carried, q[:, cols], start=True, stop=True, skip_group_check=True)); yield
        for g in range(4):
            rows = slice(32 * g, 32 * g + 32)
            e = s.pe()
            for j in range(4):
                last = e.matmul(s.a[:, j * P:(j + 1) * P], k[rows, cols], qm[rows, j, :], start=True, stop=True)
            s.end(last); yield
            s.end(s.dve().tensor_tensor(st, v2(s.a, P), over(s.c["keys_up_to_query"].unsqueeze(1), [P, 4, P]), ALU.mult)); yield
            e = s.pe()
            for j in range(4):
                last = e.matmul(s.b[rows, 0:P], vm[:, j, rows], st[:, j, :], start=False, stop=True, skip_group_check=True)
            s.end(last); yield
        s.end(s.act().activation(o[:, cols], s.b[:, 0:P], ACT.Copy)); yield
    yield from normalise(s, o, o, s.c["center8"], s.c["mean8"], s.c["eps"][:, 0:1], w["ln_gamma"], w["ln_beta"])
    s.end(s.pe().matmul(s.a, w["Wg"], xn, start=True, stop=True)); yield
    s.end(s.dve().tensor_tensor(o, o, s.a, ALU.mult)); yield
    s.end(s.pe().matmul(s.b, w["Wo"], o, start=True, stop=True)); yield
    s.end(s.dve().tensor_tensor(s.x, s.x, s.b, ALU.add)); yield


def keep_top(s, values, kept, n_top, fill):
    rows, n = values.shape[1], values.shape[2]
    top = s.take(rows, 8)
    e = s.dve()
    for r in range(rows):
        last = e.max(top[:, r, :], values[:, r, :])
    s.end(last); yield
    if n_top < 8:
        s.end(s.dve().memset(top[:, :, n_top:8], fill)); yield
    for r in range(rows):
        s.end(s.dve().match_replace(kept[:, r, :], top[:, r, :], values[:, r, :], 2 * fill)); yield
    s.end(s.dve().tensor_tensor(kept, kept, values, ALU.not_equal)); yield
    return top


def row_exp(s, logits, out, rows, n):
    m = s.take(rows)
    s.end(s.dve().tensor_reduce(m, logits, AX, ALU.max)); yield
    s.end(s.dve().tensor_tensor(out, logits, over(m.unsqueeze(2), [P, rows, n]), ALU.subtract)); yield
    s.end(s.act().activation(out, out, ACT.Exp)); yield


def row_scale(s, values, rows, n):
    m = s.take(rows)
    s.end(s.dve().tensor_reduce(m, values, AX, ALU.add)); yield
    s.end(s.dve().reciprocal(m, m)); yield
    s.end(s.dve().tensor_tensor(values, values, over(m.unsqueeze(2), [P, rows, n]), ALU.mult)); yield


def gates_to_rows(s, gates, rows_bf16, rows):
    n = gates.shape[2]
    mark = s.used
    part, rest = s.take_bf16(TILES * n).rearrange("p (t n) -> p t n", n=n), s.take(TILES, n)
    by_token = s.take(TILES, 3, n)
    s.end(s.dve().tensor_copy(part, gates)); yield
    s.end(s.dve().tensor_copy(by_token[:, :, 0, :], part)); yield
    s.end(s.dve().tensor_tensor(rest, gates, part, ALU.subtract)); yield
    s.end(s.dve().tensor_copy(part, rest)); yield
    s.end(s.dve().tensor_copy(by_token[:, :, 1, :], part)); yield
    s.end(s.dve().tensor_tensor(by_token[:, :, 2, :], rest, part, ALU.subtract)); yield
    e = s.pe()
    for t in range(TILES):
        last = e.transpose(s.a[0:3 * n, t * P:(t + 1) * P], by_token[:, t].rearrange("p a n -> p (a n)"), s.c["ident"])
    s.end(last); yield
    s.end(s.act().activation(rows_bf16, s.a[0:3 * n, :], ACT.Copy)); yield
    if rows is not None:
        s.end(s.act().activation(rows, s.a[0:3 * n, :], ACT.Copy)); yield
    s.used = mark


def expert_mix(s, w):
    E, L = 8, 4
    s.fresh()
    xn = s.take(COLS)
    yield from layer_norm(s, s.x, xn)
    mark = s.used
    e = s.pe()
    for t in range(TILES):
        last = e.matmul(s.a[:, t * 16:t * 16 + L + E], xn[:, t * P:(t + 1) * P], w["w_route"], start=True, stop=True)
    s.end(last); yield
    logits = s.take(TILES, L + E)
    s.end(s.dve().tensor_tensor(logits, over(w["b_route"].unsqueeze(1), [P, TILES, L + E]),
                                v2(s.a[:, 0:16 * TILES], 16)[:, :, 0:L + E], ALU.add)); yield
    lang = s.take(TILES, L + 1)
    s.end(s.dve().memset(lang, 0.0)); yield
    yield from row_exp(s, logits[:, :, 0:L], lang[:, :, 0:L], TILES, L)
    yield from row_scale(s, lang[:, :, 0:L], TILES, L)
    pair = s.take(TILES, L)
    s.end(s.dve().tensor_tensor(pair, lang[:, :, 0:L], lang[:, :, 1:L + 1], ALU.add)); yield
    route, gates = s.take(TILES, E), s.take(TILES, E)
    e = s.dve()
    for i in range(E // L):
        last = e.scalar_tensor_tensor(route[:, :, i * L:(i + 1) * L], pair, 0.1,
                                      logits[:, :, L + i * L:L + (i + 1) * L], ALU.mult, ALU.add)
    s.end(last); yield
    yield from row_exp(s, route, route, TILES, E)
    yield from row_scale(s, route, TILES, E)
    yield from keep_top(s, route, gates, 2, -1.0)
    s.end(s.dve().tensor_tensor(gates, gates, route, ALU.mult)); yield
    yield from row_scale(s, gates, TILES, E)
    gates_t, gates_16 = s.take(COLS, parts=3 * E), s.take_bf16(COLS, parts=3 * E)
    yield from gates_to_rows(s, gates, gates_16, gates_t)
    s.end(s.pe().matmul(s.b, w["b2"], gates_t, start=True, stop=True)); yield
    s.end(s.dve().tensor_tensor(s.x, s.x, s.b, ALU.add)); yield
    h, gate = s.take(COLS), s.take(COLS)
    H = w["w1"].shape[-1] // E // P
    for x in range(E):
        s.end(s.pe().matmul(s.a, over(s.m["row_of_8"][:, x:x + 1], [3 * E, P]), gates_16, start=True, stop=True)); yield
        s.end(s.dve().tensor_copy(gate, s.a)); yield
        for t in range(H):
            i = x * H + t
            s.end(s.pe().matmul(s.a, w["w1"][:, i * P:(i + 1) * P], xn, start=True, stop=True)); yield
            s.end(s.act().activation(h, s.a, ACT.Gelu, bias=w["b1"][:, i:i + 1])); yield
            s.end(s.pe().matmul(s.b, w["w2"][:, i * P:(i + 1) * P], h, start=(t == 0), stop=(t == H - 1))); yield
        s.end(s.dve().tensor_tensor(gate, gate, s.b, ALU.mult)); yield
        s.end(s.pool().tensor_tensor(s.x, s.x, gate, ALU.add)); yield


def expert_swiglu(s, w):
    E = 8
    s.fresh()
    xn = s.take(COLS)
    yield from layer_norm(s, s.x, xn)
    e = s.pe()
    for t in range(TILES):
        last = e.matmul(s.a[:, t * E:(t + 1) * E], xn[:, t * P:(t + 1) * P], w["w_route"], start=True, stop=True)
    s.end(last); yield
    scores, gates = s.take(TILES, E), s.take(TILES, E)
    s.end(s.dve().tensor_copy(scores, v2(s.a[:, 0:TILES * E], E))); yield
    yield from row_exp(s, scores, scores, TILES, E)
    yield from row_scale(s, scores, TILES, E)
    yield from keep_top(s, scores, gates, 2, -1.0)
    s.end(s.dve().tensor_tensor(gates, gates, scores, ALU.mult)); yield
    gates_16 = s.take_bf16(COLS, parts=3 * E)
    yield from gates_to_rows(s, gates, gates_16, None)
    hidden = w["w1"].shape[-1] // E
    sizes = [min(P, hidden - i) for i in range(0, hidden, P)]
    xe, h = s.take(COLS), s.take(COLS)
    for x in range(E):
        s.end(s.pe().matmul(s.a, over(s.m["row_of_8"][:, x:x + 1], [3 * E, P]), gates_16, start=True, stop=True)); yield
        s.end(s.dve().tensor_tensor(xe, xn, s.a, ALU.mult)); yield
        for t, m in enumerate(sizes):
            c = x * hidden + t * P
            s.end(s.pe().matmul(s.a[0:m, :], w["w1"][:, c:c + m], xe, start=True, stop=True)); yield
            s.end(s.act().activation(h[0:m, :], s.a[0:m, :], ACT.Silu)); yield
            s.end(s.pe().matmul(s.a[0:m, :], w["w3"][:, c:c + m], xe, start=True, stop=True)); yield
            s.end(s.dve().tensor_tensor(h[0:m, :], h[0:m, :], s.a[0:m, :], ALU.mult)); yield
            i = (x * len(sizes) + t) * P
            s.end(s.pe().matmul(s.b, w["w2"][0:m, i:i + P], h[0:m, :], start=(x == 0 and t == 0),
                                stop=(x == E - 1 and t == len(sizes) - 1))); yield
    s.end(s.dve().tensor_tensor(s.x, s.x, s.b, ALU.add)); yield


def gated_linear_attention(s, w):
    K = 32
    per = P // K
    s.fresh()
    xn = s.take(COLS)
    yield from layer_norm(s, s.x, xn)
    rows = {}
    for c, f in (("q", ACT.Identity), ("k", ACT.Sigmoid), ("g", ACT.Sigmoid)):
        mark = s.used
        rows[c] = s.take_bf16(COLS, parts=3 * K)
        full = s.take(COLS, parts=3 * K)
        s.end(s.pe().matmul(s.a[0:3 * K, :], w[f"w{c}"], xn, start=True, stop=True)); yield
        s.end(s.act().activation(full, s.a[0:3 * K, :], f, bias=w[f"b{c}"])); yield
        yield from split_rows(s, full, rows[c])
        s.used = mark + COLS // 2
    v_all, b, h = s.take(COLS), s.take(COLS), s.take(COLS)

    def spread(c, i):
        return s.pe().matmul(s.a, s.m["spread"][:, i * P:(i + 1) * P], rows[c], start=True, stop=True)

    s.end(s.pe().matmul(s.a, w["wv"], xn, start=True, stop=True)); yield
    s.end(s.act().activation(v_all, s.a, ACT.Identity, bias=w["bv"])); yield
    for i in range(K // per):
        s.end(spread("k", i)); yield
        s.end(s.dve().tensor_tensor(b, v_all, s.a, ALU.mult)); yield
        s.end(spread("g", i)); yield
        e = s.dve()
        for bt in range(PER_STREAM):
            c = slice(bt * TOKENS, (bt + 1) * TOKENS)
            last = e.tensor_tensor_scan(h[:, c], s.a[:, c], b[:, c], 0.0, ALU.mult, ALU.add)
        s.end(last); yield
        s.end(spread("q", i)); yield
        s.end(s.dve().tensor_tensor(h, h, s.a, ALU.mult)); yield
        s.end(s.pe().matmul(s.b, w["Wo"], h, start=(i == 0), stop=(i == K // per - 1))); yield
    s.end(s.dve().scalar_tensor_tensor(s.x, s.b, w["bo"], s.x, ALU.add, ALU.add)); yield


def attend8(s, q, keys, vm, n_tiles, o, sums, scale, add_mask=None, zero_mask=None):
    nk = n_tiles * P
    mark = s.used
    qm, p, m = s.take(2, P), s.take(2, nk), s.take(2)
    pt = p
    S = s.a[:, 0:2 * nk].rearrange("p (i k) -> p i k", k=nk)
    for half in range(2):
        js = (2 * half, 2 * half + 1)
        e = s.dve()
        for i, j in enumerate(js):
            last = e.tensor_scalar(qm[:, i, :], q, s.c["head_of_row_group"][:, j:j + 1], None, ALU.mult)
        s.end(last); yield
        for g in range(4):
            rows = slice(32 * g, 32 * g + 32)
            if add_mask is not None:
                s.end(s.pe().matmul(S, s.m["ident"], over(add_mask.unsqueeze(1), [P, 2, nk]), start=True, stop=True)); yield
            e = s.pe()
            for i in range(2):
                last = e.matmul(S[:, i, :], qm[rows, i, :], keys[rows, 0:nk], start=(add_mask is None),
                                stop=True, skip_group_check=True)
            s.end(last); yield
            scores = S
            if zero_mask is not None:
                scores = p
                s.end(s.dve().tensor_tensor(scores, S, over(zero_mask[:, 0:nk].unsqueeze(1), [P, 2, nk]), ALU.mult)); yield
            s.end(s.dve().tensor_reduce(m, scores, AX, ALU.max)); yield
            s.end(s.dve().tensor_scalar(m, m, -scale, None, ALU.mult)); yield
            e = s.act()
            for i, j in enumerate(js):
                last = e.activation(p[:, i, :], scores[:, i, :], ACT.Exp, bias=m[:, i:i + 1], scale=scale,
                                    accum_out=sums[:, 4 * g + j:4 * g + j + 1])
            s.end(last); yield
            e = s.pe()
            for i in range(2):
                for c in range(n_tiles):
                    last = e.transpose(S[:, i, c * P:(c + 1) * P], p[:, i, c * P:(c + 1) * P], s.c["ident"])
            s.end(last); yield
            if g % 2:
                s.end(s.dve().tensor_copy(pt, S)); yield
            else:
                s.end(s.act().activation(pt, S, ACT.Copy)); yield
            e = s.pe()
            for i, j in enumerate(js):
                for c in range(n_tiles):
                    last = e.matmul(s.a[rows, 0:P], vm[:, c, j, rows], pt[:, i, c * P:(c + 1) * P],
                                    start=(i + c == 0), stop=(i + c == n_tiles))
            s.end(last); yield
            if half == 0:
                s.end(s.act().activation(o[rows, :], s.a[rows, 0:P], ACT.Copy)); yield
            else:
                s.end(s.dve().tensor_tensor(o[rows, :], o[rows, :], s.a[rows, 0:P], ALU.add)); yield
    s.used = mark


def divide_by_sums(s, o, sums):
    mark = s.used
    n = sums.shape[1]
    by_head = s.take(n * P, parts=HEADS8)
    s.end(s.dve().reciprocal(sums, sums)); yield
    e = s.pe()
    for t in range(n):
        last = e.transpose(s.a[0:HEADS8, t * P:(t + 1) * P], sums[:, t, :], s.c["ident"])
    s.end(last); yield
    s.end(s.act().activation(by_head, s.a[0:HEADS8, 0:n * P], ACT.Copy)); yield
    s.end(s.pe().matmul(s.a[:, 0:n * P], s.c["expand16"], by_head, start=True, stop=True)); yield
    s.end(s.dve().tensor_tensor(o, o, s.a[:, 0:n * P], ALU.mult)); yield
    s.used = mark


BRANCH8 = 2 * P + 2 * 2 * P + 2 + 2 * HEADS8


def attend_batches(s, q, k, vm, o, n_tiles, **masks):
    mark = s.used
    branches = [s.branch(i, BRANCH8) for i in range(PER_STREAM)]

    def chain(b, bt):
        sums = b.take(2, HEADS8)
        for qt in range(2):
            cols = slice((2 * bt + qt) * P, (2 * bt + qt + 1) * P)
            yield from attend8(b, q[:, cols], k[:, bt * TOKENS:(bt + 1) * TOKENS], vm[:, 2 * bt:2 * bt + 2],
                               n_tiles[qt], o[:, cols], sums[:, qt, :], HD8 ** -0.5,
                               **{n: m[qt] for n, m in masks.items()})
        yield from divide_by_sums(b, o[:, bt * TOKENS:(bt + 1) * TOKENS], sums)

    yield from s.join(branches, [chain(b, i) for i, b in enumerate(branches)], BRANCH_SKEW)
    s.used = mark


def spread_values(s, v_tok, vm):
    n = v_tok.shape[1]
    mask = v2(s.c["head_of_col_group"], P)
    e = s.dve()
    for j in range(4):
        last = e.tensor_tensor(vm[:, :, j, :], v_tok, over(mask[:, j:j + 1, :], [P, n, P]), ALU.mult)
    s.end(last); yield


def values_by_token(s, src, wv, vm, bias=None):
    mark = s.used
    v_tok = s.take(TILES, P)
    e = s.pe()
    for t in range(TILES):
        last = e.matmul(s.a[:, t * P:(t + 1) * P], src[:, t * P:(t + 1) * P], wv, start=True, stop=True)
    s.end(last); yield
    if bias is None:
        s.end(s.act().activation(v_tok, v2(s.a, P), ACT.Copy)); yield
    else:
        s.end(s.dve().tensor_tensor(v_tok, over(bias.unsqueeze(1), [P, TILES, P]), v2(s.a, P), ALU.add)); yield
    yield from spread_values(s, v_tok, vm)
    s.used = mark


def project(s, w, src, dst, bias=None):
    m = w.shape[-1]
    s.end(s.pe().matmul(s.a[0:m, :], w, src, start=True, stop=True)); yield
    if bias is None:
        s.end(s.act().activation(dst, s.a[0:m, :], ACT.Copy)); yield
    else:
        s.end(s.act().activation(dst, s.a[0:m, :], ACT.Identity, bias=bias)); yield


def attention(s, w, latent, masked):
    s.fresh()
    xn = s.take(COLS)
    yield from layer_norm(s, s.x, xn)
    q, k, vm = s.take(COLS), s.take(COLS), s.take(TILES, 4, P)
    mark = s.used
    yield from project(s, w["Wq"], xn, q, w["bq"])
    src = xn
    if latent:
        m = w["Wl"].shape[-1]
        src = s.take(COLS, parts=m)
        yield from project(s, w["Wl"], xn, src, w["bl"])
    yield from project(s, w["Wk"], src, k, w["bk"])
    yield from values_by_token(s, src, w["Wv"], vm, w["bv"])
    s.used = mark
    o = xn
    zero = {"zero_mask": [s.c["block32_0"], s.c["block32_1"]]} if masked else {}
    yield from attend_batches(s, q, k, vm, o, (2, 2), **zero)
    s.end(s.pe().matmul(s.a, w["Wo"], o, start=True, stop=True)); yield
    s.end(s.dve().scalar_tensor_tensor(s.x, s.a, w["bo"], s.x, ALU.add, ALU.add)); yield


def block_attention(s, w):
    s.fresh()
    xn = s.take(COLS)
    yield from layer_norm(s, s.x, xn)
    q, k, v = (s.take(COLS) for _ in range(3))
    for i, dst in enumerate((q, k, v)):
        yield from project(s, w["w_qkv"][:, i * P:(i + 1) * P], xn, dst)
    qs, ks, prod = s.take(TILES), s.take(TILES), s.take(TILES, 2)
    s.end(s.dve().tensor_reduce(qs, v2(q, P), AX, ALU.add)); yield
    s.end(s.dve().tensor_reduce(ks, v2(k, P), AX, ALU.add)); yield
    s.end(s.dve().tensor_scalar(qs, qs, 1.0 / P, None, ALU.mult)); yield
    s.end(s.dve().tensor_scalar(ks, ks, 1.0 / P, None, ALU.mult)); yield
    e = s.dve()
    for bt in range(PER_STREAM):
        two = slice(2 * bt, 2 * bt + 2)
        last = e.tensor_tensor(prod[:, two, :], over(qs[:, two].unsqueeze(2), [P, 2, 2]),
                               over(ks[:, two].unsqueeze(1), [P, 2, 2]), ALU.mult)
    s.end(last); yield
    n = TILES * 2
    s.end(s.pe().matmul(s.a[:, 0:n], s.c["group8"], prod.rearrange("p a b -> p (a b)"), start=True, stop=True)); yield
    s.end(s.dve().tensor_copy(prod, v2(s.a[:, 0:n], 2))); yield
    second, first = s.take(TILES), s.take(TILES)
    s.end(s.dve().tensor_tensor(second, prod[:, :, 1], prod[:, :, 0], ALU.is_gt)); yield
    s.end(s.dve().tensor_scalar(first, second, -1.0, 1.0, ALU.mult, ALU.add)); yield
    o = xn
    branches = [s.branch(i, BRANCH8 - 2 * P + 7 * P) for i in range(PER_STREAM)]

    def chain(b, bt):
        kc, vc, v_tok, vm = b.take(P), b.take(P), b.take(1, P), b.take(1, 4, P)
        sums = b.take(2, HEADS8)
        lo = bt * TOKENS
        for t in (2 * bt, 2 * bt + 1):
            for src, dst in ((k, kc), (v, vc)):
                b.end(b.dve().tensor_scalar(dst, src[:, lo:lo + P], first[:, t:t + 1], None, ALU.mult)); yield
                b.end(b.dve().scalar_tensor_tensor(dst, src[:, lo + P:lo + 2 * P], second[:, t:t + 1], dst, ALU.mult, ALU.add)); yield
            yield from to_channels(b, vc, v_tok, b.a)
            yield from spread_values(b, v_tok, vm)
            cols = slice(t * P, (t + 1) * P)
            yield from attend8(b, q[:, cols], kc, vm, 1, o[:, cols], sums[:, t - 2 * bt, :], HD8 ** -0.5)
        yield from divide_by_sums(b, o[:, lo:lo + TOKENS], sums)

    yield from s.join(branches, [chain(b, i) for i, b in enumerate(branches)], BRANCH_SKEW)
    s.end(s.pe().matmul(s.a, w["Wo"], o, start=True, stop=True)); yield
    s.end(s.dve().scalar_tensor_tensor(s.x, s.a, w["bo"], s.x, ALU.add, ALU.add)); yield


def grouped_query_attention(s, w):
    s.fresh()
    y, xn, q, k = (s.take(COLS) for _ in range(4))
    vm = s.take(TILES, 4, P)
    yield from layer_norm(s, s.x, y)

    def rotate_and_norm(dst, kind):
        tmp = s.take(COLS)
        s.end(s.pe().matmul(s.a, s.c["pair_rotation"], dst, start=True, stop=True)); yield
        sin = over(s.c[f"sin_{kind}"].unsqueeze(1), [P, PER_STREAM, TOKENS])
        cos = over(s.c[f"cos_{kind}"].unsqueeze(1), [P, PER_STREAM, TOKENS])
        s.end(s.dve().tensor_tensor(v2(tmp, TOKENS), sin, v2(s.a, TOKENS), ALU.mult)); yield
        s.end(s.dve().tensor_tensor(v2(dst, TOKENS), v2(dst, TOKENS), cos, ALU.mult)); yield
        s.end(s.dve().tensor_tensor(dst, dst, tmp, ALU.add)); yield
        s.used -= COLS
        yield from normalise(s, dst, dst, None, s.c["mean8"], s.c["eps"][:, 2:3])

    for kind, gain in (("global", "norm1"), ("local", "norm2")):
        yield from normalise(s, y, xn, None, s.c["mean"], s.c["eps"][:, 2:3], w[gain])
        p = kind[0] + "_"
        yield from project(s, w[p + "wq"], xn, q)
        src = xn
        mark = s.used
        if kind == "global":
            src = s.take(COLS, parts=w["g_down"].shape[-1])
            yield from project(s, w["g_down"], xn, src)
        yield from project(s, w[p + "wk"], src, k)
        yield from values_by_token(s, src, w[p + "wv"], vm)
        s.used = mark
        for dst in (q, k):
            yield from rotate_and_norm(dst, kind)
        mask = "causal" if kind == "global" else "band32"
        yield from attend_batches(s, q, k, vm, xn, (1, 2), add_mask=[s.m[f"{mask}_0"], s.m[f"{mask}_1"]])
        s.end(s.pe().matmul(s.a, w[p + "wo"], xn, start=True, stop=True)); yield
        s.end(s.dve().tensor_tensor(y, y, s.a, ALU.add)); yield
    s.end(s.dve().tensor_tensor(s.x, s.x, y, ALU.add)); yield


def shift_tokens(s, src, out):
    src, out = v2(src, TOKENS), v2(out, TOKENS)
    half = P // 2
    e = s.dve()
    e.tensor_copy(out[0:half], src[0:half])
    e.memset(out[half:P, :, 0:1], 0.0)
    s.end(e.tensor_copy(out[half:P, :, 1:TOKENS], src[half:P, :, 0:TOKENS - 1])); yield


def xpos_tables(w, d):
    T2, HD = TOKENS // P, 64
    n = T2 * HD
    at = [v2(w.extra[:, (4 * d + i) * n:(4 * d + i + 1) * n], HD) for i in range(4)]
    return {"q": at[0], "k": at[1]}, {"q": at[2], "k": at[3]}


def prepare_xpos(s, w):
    T2, HD = TOKENS // P, 64
    half = HD // 2
    e = s.dve()
    for d in range(2):
        cos_t, sin_t = xpos_tables(w, d)
        for n in "qk":
            g = w[f"{n}_scale{d}"]
            e.tensor_tensor(cos_t[n], v2(s.c[f"xpos_cos_{n}"], HD), over(g.unsqueeze(1), [P, T2, HD]), ALU.mult)
            for i in range(2):
                o, p = slice(half * i, half * i + half), slice(half - half * i, 2 * half - half * i)
                last = e.tensor_tensor(sin_t[n][:, :, o], v2(s.c[f"xpos_sin_{n}"], HD)[:, :, o],
                                       over(g[:, p].unsqueeze(1), [P, T2, half]), ALU.mult)
    s.end(last)


def local_layer(s, w, d, x):
    H, HD = 8, 64
    T2 = TOKENS // P
    inner = H * HD
    s.used = COLS
    h = s.take(COLS)
    yield from shift_tokens(s, x, h)
    mark = s.used
    half = HD // 2
    cos_t, sin_t = xpos_tables(w, d)
    chunks = {0: [(0, P)], 1: [(1, P), (2, 64)]}
    first_token = (0, 64, 192)
    q, k, v = s.take(inner // P, P), s.take(inner // P, TOKENS), s.take(len(first_token), inner)
    tmp, tok, ss = s.take(inner), s.take(inner), s.take(H)
    p, sums, m = s.take(2, 2 * P), s.take(H), s.take(2)
    pt = p
    heads = lambda ap: v2(ap, HD)
    for bt in range(PER_STREAM):
        hb = h[:, bt * TOKENS:(bt + 1) * TOKENS]

        def rotated(n, t, dst):
            col = 0 if n == "q" else inner
            s.end(s.pe().matmul(s.a, hb[:, t * P:(t + 1) * P], w[f"wqkv{d}"][:, col:col + inner], start=True, stop=True)); yield
            s.end(s.act().activation(tmp, s.a, ACT.Square)); yield
            s.end(s.dve().tensor_reduce(ss, heads(tmp), AX, ALU.add)); yield
            s.end(s.act().activation(ss, ss, ACT.Sqrt)); yield
            s.end(s.dve().tensor_scalar(ss, ss, 1e-12, None, ALU.max)); yield
            s.end(s.dve().reciprocal(ss, ss)); yield
            s.end(s.dve().tensor_tensor(heads(tmp), heads(s.a), over(ss.unsqueeze(2), [P, H, HD]), ALU.mult)); yield
            e = s.dve()
            for i in range(2):
                o, pa = slice(half * i, half * i + half), slice(half - half * i, 2 * half - half * i)
                last = e.tensor_tensor(heads(tok)[:, :, o], heads(tmp)[:, :, pa],
                                       over(sin_t[n][:, t:t + 1, o], [P, H, half]), ALU.mult)
            s.end(last); yield
            s.end(s.pool().tensor_tensor(heads(tmp), heads(tmp), over(cos_t[n][:, t:t + 1, :], [P, H, HD]), ALU.mult)); yield
            s.end(s.pool().tensor_tensor(tok, tok, tmp, ALU.add)); yield
            yield from to_channels(s, tok, dst, s.a)

        for t in range(T2):
            yield from rotated("k", t, k[:, :, t * P:(t + 1) * P])
        for i, first in enumerate(first_token):
            n = min(P, TOKENS - first)
            s.end(s.pe().matmul(s.b[0:n, :], hb[:, first:first + n], w[f"wqkv{d}"][:, 2 * inner:3 * inner], start=True, stop=True)); yield
            s.end(s.act().activation(v[0:n, i, :], s.b[0:n, :], ACT.Copy)); yield
        for t in range(T2):
            yield from rotated("q", t, q)
            lo = 64 * t
            nk = P + 64 * t
            mask = s.m[f"band64_{t}"]
            o = v2(tok, P)
            for pair in range(H // 2):
                both = v2(s.psum, BANK)
                S = both[:, :, 0:nk]
                e = s.pe()
                for i in range(2):
                    last = e.matmul(S[:, i, :], s.m["ident"], mask, start=True, stop=False)
                s.end(last); yield
                e = s.pe()
                for i in range(2):
                    rows = slice(64 * i, 64 * i + 64)
                    last = e.matmul(S[:, i, :], q[rows, pair, :], k[rows, pair, lo:lo + nk], start=False, stop=True)
                s.end(last); yield
                s.end(s.dve().tensor_reduce(m, S, AX, ALU.max)); yield
                s.end(s.dve().tensor_scalar(m, m, -8.0, None, ALU.mult)); yield
                e = s.act()
                for i in range(2):
                    hh = 2 * pair + i
                    last = e.activation(p[:, i, 0:nk], S[:, i, :], ACT.Exp, bias=m[:, i:i + 1], scale=8.0,
                                        accum_out=sums[:, hh:hh + 1])
                s.end(last); yield
                e = s.pe()
                at = list(reversed(range(len(chunks[t]))))
                for i in range(2):
                    for c, (_, n) in enumerate(chunks[t]):
                        last = e.transpose(both[0:n, i, at[c] * P:(at[c] + 1) * P], p[:, i, c * P:c * P + n], s.c["ident"])
                s.end(last); yield
                width = len(chunks[t]) * P
                s.end(s.dve().tensor_copy(pt[:, :, 0:width], both[:, :, 0:width])); yield
                e = s.pe()
                for i in range(2):
                    hc = slice((2 * pair + i) * HD, (2 * pair + i + 1) * HD)
                    for c, (vc, n) in enumerate(chunks[t]):
                        last = e.matmul(both[i * HD:(i + 1) * HD, i, 0:P], v[0:n, vc, hc], pt[0:n, i, at[c] * P:(at[c] + 1) * P],
                                        start=(c == 0), stop=(c == len(chunks[t]) - 1))
                s.end(last); yield
                e = s.act()
                for i in range(2):
                    rows = slice(64 * i, 64 * i + 64)
                    last = e.activation(o[rows, pair, :], both[rows, i, 0:P], ACT.Copy)
                s.end(last); yield
            s.end(s.dve().reciprocal(sums, sums)); yield
            s.end(s.pe().transpose(s.a[0:H, 0:P], sums, s.c["ident"])); yield
            s.end(s.act().activation(tmp[0:H, 0:P], s.a[0:H, 0:P], ACT.Copy)); yield
            e = s.pe()
            for i in range(inner // P):
                last = e.matmul(s.a[:, i * P:(i + 1) * P], s.c["expand8"][:, i * P:(i + 1) * P], tmp[0:H, 0:P], start=True, stop=True)
            s.end(last); yield
            s.end(s.dve().tensor_tensor(tok, tok, s.a, ALU.mult)); yield
            e = s.pe()
            for i in range(inner // P):
                last = e.matmul(s.b[:, 0:P], w[f"wo{d}"][:, i * P:(i + 1) * P], o[:, i, :],
                                start=(i == 0), stop=(i == inner // P - 1))
            s.end(last); yield
            xs = x[:, bt * TOKENS + t * P:bt * TOKENS + (t + 1) * P]
            s.end(s.dve().tensor_tensor(xs, xs, s.b[:, 0:P], ALU.add)); yield
    s.used = mark
    yield from shift_tokens(s, x, h)
    yield from layer_norm(s, h, h, w[f"ln_g{d}"], w[f"ln_b{d}"])
    hid = w[f"w1{d}"].shape[-1] // 2
    sizes = [min(P, hid - i) for i in range(0, hid, P)]
    gate = s.take(COLS)
    for i, n in enumerate(sizes):
        ca, cg = i * P, hid + i * P
        s.end(s.pe().matmul(s.a[0:n, :], w[f"w1{d}"][:, cg:cg + n], h, start=True, stop=True)); yield
        s.end(s.act().activation(gate[0:n, :], s.a[0:n, :], ACT.Gelu, bias=w[f"b1g{d}"][0:n, i:i + 1])); yield
        s.end(s.pe().matmul(s.a[0:n, :], w[f"w1{d}"][:, ca:ca + n], h, start=True, stop=True)); yield
        s.end(s.dve().scalar_tensor_tensor(gate[0:n, :], s.a[0:n, :], w[f"b1a{d}"][0:n, i:i + 1], gate[0:n, :],
                                           ALU.add, ALU.mult)); yield
        s.end(s.pe().matmul(s.b, w[f"w2{d}"][0:n, i * P:(i + 1) * P], gate[0:n, :], start=(i == 0),
                            stop=(i == len(sizes) - 1))); yield
    s.end(s.dve().scalar_tensor_tensor(x, s.b, w[f"b2{d}"], x, ALU.add, ALU.add)); yield


def local_transformer(s, w):
    s.fresh()
    y = s.take(COLS)
    yield from layer_norm(s, s.x, y)
    for d in range(2):
        yield from local_layer(s, w, d, y)
    s.end(s.dve().tensor_tensor(s.x, s.x, y, ALU.add)); yield


def slot_memory(s, w):
    N, TOP = 64, 8
    B = PER_STREAM
    s.fresh()
    xn, alpha, x_tok, hT = s.take(COLS), s.take(TILES, N), s.take(TILES, P), s.take(COLS, parts=N)
    yield from layer_norm(s, s.x, xn)
    col = s.take(4)
    s.end(s.dve().tensor_reduce(col[:, 0:1], w["slots"], AX, ALU.add)); yield
    s.end(s.dve().tensor_scalar(col[:, 0:1], col[:, 0:1], 1.0 / N, None, ALU.mult)); yield
    s.end(s.pe().matmul(s.a[0:N, 0:1], w["w1s"], col[:, 0:1], start=True, stop=True)); yield
    s.end(s.dve().tensor_tensor(col[0:N, 1:2], w["b1"], s.a[0:N, 0:1], ALU.add)); yield
    s.end(s.dve().scalar_tensor_tensor(col[:, 2:3], w["tau"], -1.0, w["tau"], ALU.mult, ALU.max)); yield
    s.end(s.dve().tensor_scalar(col[:, 2:3], col[:, 2:3], 0.1, None, ALU.add)); yield
    s.end(s.dve().reciprocal(col[:, 2:3], col[:, 2:3])); yield
    s.end(s.pe().matmul(s.a[0:N, :], w["w1x"], xn, start=True, stop=True)); yield
    s.end(s.act().activation(hT, s.a[0:N, :], ACT.Gelu, bias=col[0:N, 1:2])); yield
    e = s.pe()
    for t in range(TILES):
        last = e.matmul(s.b[:, t * N:(t + 1) * N], hT[:, t * P:(t + 1) * P], w["w2"], start=True, stop=True)
    s.end(last); yield
    logits = s.take(TILES, N)
    s.end(s.dve().tensor_tensor(logits, over(w["b2"].unsqueeze(1), [P, TILES, N]), v2(s.b[:, 0:TILES * N], N), ALU.add)); yield
    s.end(s.dve().tensor_scalar(logits, logits, col[:, 2:3], None, ALU.mult)); yield
    top = yield from keep_top(s, logits, alpha, TOP, -1.5e38)
    s.end(s.dve().tensor_tensor(logits, logits, over(top[:, :, 0:1], [P, TILES, N]), ALU.subtract)); yield
    s.end(s.act().activation(logits, logits, ACT.Exp)); yield
    s.end(s.dve().tensor_tensor(alpha, alpha, logits, ALU.mult)); yield
    yield from row_scale(s, alpha, TILES, N)
    e = s.pe()
    for t in range(TILES):
        last = e.transpose(s.a[:, t * P:(t + 1) * P], xn[:, t * P:(t + 1) * P], s.c["ident"])
    s.end(last); yield
    s.end(s.act().activation(x_tok, v2(s.a, P), ACT.Copy)); yield
    e = s.pe()
    for bt in range(B):
        for i in range(2):
            last = e.matmul(s.a[:, bt * N:(bt + 1) * N], x_tok[:, 2 * bt + i, :], alpha[:, 2 * bt + i, :], start=(i == 0), stop=(i == 1))
    for bt in range(B):
        for i in range(2):
            last = e.matmul(s.b[:, bt * N:(bt + 1) * N], s.c["ones"], alpha[:, 2 * bt + i, :], start=(i == 0), stop=(i == 1))
    s.end(last); yield
    M = B * N
    si, gh, gi, new, tmp = s.take(M), s.take(3, N), s.take(3, M), s.take(M), s.take(M)
    s.end(s.dve().tensor_scalar(si, s.b[:, 0:M], 1e-8, None, ALU.add)); yield
    s.end(s.dve().reciprocal(si, si)); yield
    s.end(s.dve().tensor_tensor(si, si, s.a[:, 0:M], ALU.mult)); yield
    e = s.pe()
    for i in range(3):
        last = e.matmul(s.a[:, i * M:(i + 1) * M], w["Wih"][:, i * P:(i + 1) * P], si, start=True, stop=True)
    for i in range(3):
        last = e.matmul(s.b[:, i * N:(i + 1) * N], w["Whh"][:, i * P:(i + 1) * P], w["slots"], start=True, stop=True)
    s.end(last); yield
    e = s.dve()
    for i in range(3):
        e.tensor_scalar(gi[:, i, :], s.a[:, i * M:(i + 1) * M], w["bih"][:, i:i + 1], None, ALU.add)
        last = e.tensor_scalar(gh[:, i, :], s.b[:, i * N:(i + 1) * N], w["bhh"][:, i:i + 1], None, ALU.add)
    s.end(last); yield
    e = s.dve()
    for i in range(2):
        last = e.tensor_tensor(v2(gi[:, i, :], N), v2(gi[:, i, :], N), over(gh[:, i:i + 1, :], [P, B, N]), ALU.add)
    s.end(last); yield
    s.end(s.act().activation(gi[:, 0:2, :], gi[:, 0:2, :], ACT.Sigmoid)); yield
    s.end(s.dve().tensor_tensor(v2(tmp, N), v2(gi[:, 0, :], N), over(gh[:, 2:3, :], [P, B, N]), ALU.mult)); yield
    s.end(s.dve().tensor_tensor(tmp, tmp, gi[:, 2, :], ALU.add)); yield
    s.end(s.act().activation(new, tmp, ACT.Tanh)); yield
    s.end(s.dve().tensor_tensor(v2(tmp, N), over(w["slots"].unsqueeze(1), [P, B, N]), v2(new, N), ALU.subtract)); yield
    s.end(s.dve().tensor_tensor(tmp, tmp, gi[:, 1, :], ALU.mult)); yield
    s.end(s.dve().tensor_tensor(new, new, tmp, ALU.add)); yield
    DQ = w["wq"].shape[-1]
    qk, vt, pr, prT = s.take(2, M, parts=DQ), s.take(B, P, parts=N), s.take(B, N, parts=N), s.take(B, N, parts=N)
    m = s.take(B, parts=N)
    e = s.pe()
    e.matmul(s.a[0:DQ, 0:M], w["wq"], new, start=True, stop=True)
    e.matmul(s.a[0:DQ, M:2 * M], w["wk"], new, start=True, stop=True)
    for bt in range(B):
        last = e.matmul(s.b[0:N, bt * P:(bt + 1) * P], new[:, bt * N:(bt + 1) * N], w["wv"], start=True, stop=True)
    s.end(last); yield
    e = s.act()
    e.activation(qk[:, 0, :], s.a[0:DQ, 0:M], ACT.Identity, bias=w["bq"])
    s.end(e.activation(qk[:, 1, :], s.a[0:DQ, M:2 * M], ACT.Identity, bias=w["bk"])); yield
    s.end(s.dve().tensor_tensor(vt, over(w["bv"][0:N].unsqueeze(1), [N, B, P]), v2(s.b[0:N, 0:B * P], P), ALU.add)); yield
    e = s.pe()
    for bt in range(B):
        last = e.matmul(s.a[0:N, bt * N:(bt + 1) * N], qk[:, 0, bt * N:(bt + 1) * N], qk[:, 1, bt * N:(bt + 1) * N], start=True, stop=True)
    s.end(last); yield
    S = v2(s.a[0:N, 0:M], N)
    s.end(s.dve().tensor_reduce(m, S, AX, ALU.max)); yield
    s.end(s.dve().tensor_scalar(m, m, -DQ ** -0.5, None, ALU.mult)); yield
    e = s.act()
    for bt in range(B):
        last = e.activation(pr[:, bt, :], S[:, bt, :], ACT.Exp, bias=m[:, bt:bt + 1], scale=DQ ** -0.5)
    s.end(last); yield
    s.end(s.dve().tensor_reduce(m, pr, AX, ALU.add)); yield
    s.end(s.dve().reciprocal(m, m)); yield
    s.end(s.dve().tensor_tensor(pr, pr, over(m.unsqueeze(2), [N, B, N]), ALU.mult)); yield
    e = s.pe()
    for bt in range(B):
        last = e.transpose(s.b[0:N, bt * N:(bt + 1) * N], pr[:, bt, :], s.c["ident"][0:N, 0:N])
    s.end(last); yield
    s.end(s.act().activation(prT, v2(s.b[0:N, 0:M], N), ACT.Copy)); yield
    e = s.pe()
    for bt in range(B):
        last = e.matmul(s.a[:, bt * N:(bt + 1) * N], vt[:, bt, :], prT[:, bt, :], start=True, stop=True)
    s.end(last); yield
    s.end(s.dve().tensor_tensor(new, new, s.a[:, 0:M], ALU.add)); yield
    yield from layer_norm(s, new, new, w["ln_g"], w["ln_b"])
    e = s.pe()
    for bt in range(B):
        last = e.matmul(s.a[0:N, bt * P:(bt + 1) * P], new[:, bt * N:(bt + 1) * N], w["wvp"], start=True, stop=True)
    for t in range(TILES):
        last = e.transpose(s.b[0:N, t * P:(t + 1) * P], alpha[:, t, :], s.c["ident"])
    s.end(last); yield
    s.end(s.dve().tensor_tensor(vt, over(w["bvp"][0:N].unsqueeze(1), [N, B, P]), v2(s.a[0:N, 0:B * P], P), ALU.add)); yield
    s.end(s.act().activation(hT, s.b[0:N, :], ACT.Copy)); yield
    e = s.pe()
    for bt in range(B):
        c = slice(bt * TOKENS, (bt + 1) * TOKENS)
        last = e.matmul(s.a[:, c], vt[:, bt, :], hT[:, c], start=True, stop=True)
    s.end(last); yield
    s.end(s.act().activation(xn, s.a, ACT.Copy)); yield
    s.end(s.pe().matmul(s.b, w["wo"], xn, start=True, stop=True)); yield
    s.end(s.dve().scalar_tensor_tensor(s.x, s.b, w["bo"], s.x, ALU.add, ALU.add)); yield


NETWORK = [
    ("L0_scan", lambda s, w: scan_block(s, w, conv=False, a_is_exp=False, clip=(0.001, 0.1))),
    ("L0_experts", expert_mix),
    ("L0_linear", linear_attention),
    ("L0_experts", expert_mix),
    ("L1_gla", gated_linear_attention),
    ("L1_local", local_transformer),
    ("L1_attn", lambda s, w: attention(s, w, latent=True, masked=False)),
    ("L1_local", local_transformer),
    ("L2_scan", lambda s, w: scan_block(s, w, conv=True, a_is_exp=True, clip=None)),
    ("L2_experts", expert_swiglu),
    ("L2_attn", lambda s, w: attention(s, w, latent=False, masked=True)),
    ("L2_experts", expert_swiglu),
    ("L3_blocks", block_attention),
    ("L3_slots", slot_memory),
    ("L3_gqa", grouped_query_attention),
    ("L3_slots", slot_memory),
]
SUCCESSORS = {"L0_experts": ("L2_experts",), "L1_local": ("L2_attn", "L3_blocks", "L3_slots", "L3_gqa")}


def build(nc, x_dram, out_dram, packed_dram, where, network):
    with ExitStack() as ctx:
        core = Core(nc, ctx)
        engines = core.engines
        groups = ["constants"] + [g for i, (g, _) in enumerate(network) if g not in [n for n, _ in network[:i]]]
        for g in groups + ["x"]:
            core.sems[f"load_{g}"] = ctx.enter_context(nc.semaphore(f"load_{g}"))
        stored = ctx.enter_context(nc.semaphore("stored"))
        width = {g: packed_dram[g].shape[1] for g in groups}
        weights = {}
        after = {g: first for first, later in SUCCESSORS.items() for g in later if first in groups and g in groups}
        for g in groups:
            if g not in after:
                followers = [f for f in groups if after.get(f) == g]
                buf = ctx.enter_context(nc.sbuf_tensor(f"w_{g}", [P, max(width[g], sum(width[f] for f in followers))], F32))
                weights[g] = Weights(buf[:, 0:width[g]], where[g])
                at = 0
                for f in followers:
                    weights[f] = Weights(buf[:, at:at + width[f]], where[f])
                    at += width[f]
        x = ctx.enter_context(nc.sbuf_tensor("x", [P, BATCHES * TOKENS], F32))
        scratch = ctx.enter_context(nc.sbuf_tensor("scratch", [P, N_STREAMS * SCRATCH], F32))
        psum = ctx.enter_context(nc.psum_tensor("psum", [P, N_STREAMS * 2 * BANK], F32))

        def load(g):
            nc.sync.dma_start(weights[g].buf, packed_dram[g]).then_inc(core.sems[f"load_{g}"], 16)

        n = packed_dram["masks"].shape[1]
        core.sems["load_masks"] = ctx.enter_context(nc.semaphore("load_masks"))
        bf16_masks = Weights(ctx.enter_context(nc.sbuf_tensor("bf16_masks", [P, n], BF16)), where["masks"])
        load("constants")
        nc.sync.dma_start(x[:, :], x_dram).then_inc(core.sems["load_x"], 16)
        staged = scratch[:, (N_STREAMS - 1) * SCRATCH:][:, 0:n]
        nc.sync.dma_start(staged, packed_dram["masks"]).then_inc(core.sems["load_masks"], 16)
        for g in groups[1:]:
            if g not in after:
                load(g)

        streams = [Stream(core, i, x[:, i * COLS:(i + 1) * COLS], scratch[:, i * SCRATCH:(i + 1) * SCRATCH],
                          psum[:, i * 2 * BANK:(i + 1) * 2 * BANK], weights["constants"], bf16_masks) for i in range(N_STREAMS)]
        streams[0].needs("constants")
        streams[0].needs("x")
        streams[0].needs("masks")
        streams[-1].end(streams[-1].act().activation(bf16_masks.buf[:, :], staged, ACT.Copy))
        core.wait("pe", *streams[-1].last[0])
        local = weights.get("L1_local")
        if local:
            local.extra = ctx.enter_context(nc.sbuf_tensor("xpos", [P, 8 * TOKENS // P * 64], F32))
        last_use = {g: i for i, (g, _) in enumerate(network)}
        passed = dict.fromkeys(SUCCESSORS, 0)

        def through(s):
            for i, (g, block) in enumerate(network):
                s.needs(g)
                if local and g == "L1_local" and not local.prepared:
                    prepare_xpos(s, local)
                    local.prepared = s.last
                if g == "L1_local":
                    s.wait_all(*local.prepared[0])
                yield from block(s, weights[g])
                if g in SUCCESSORS and i == last_use[g]:
                    core.wait("sp", *s.last[0])
                    passed[g] += 1
                    if passed[g] == N_STREAMS:
                        for f in SUCCESSORS[g]:
                            if after.get(f) == g:
                                load(f)

        running = [(i * SKEW, through(s)) for i, s in enumerate(streams)]
        while running:
            for r in list(running):
                behind, steps = r
                at = running.index(r)
                if behind:
                    running[at] = (behind - 1, steps)
                    continue
                try:
                    next(steps)
                except StopIteration:
                    running.remove(r)
        for i, s in enumerate(streams):
            core.wait("sp", *s.last[0])
            nc.sync.dma_start(out_dram[:, i * COLS:(i + 1) * COLS], s.x).then_inc(stored, 16)
        nc.sync.wait_ge(stored, 16 * N_STREAMS)


def kernel(**inputs):
    import concourse.bacc as bacc
    from concourse.bass_utils import run_bass_kernel_spmd

    p = {k: np.asarray(v) for k, v in inputs.items()}
    packs = {"constants": pack(constants()), "masks": pack(masks()), **{g: pack(parts) for g, parts in layouts(p).items()}}
    x = np.ascontiguousarray(p["L0_attn_a_x"].reshape(BATCHES * TOKENS, P).T)
    nc = bacc.Bacc("TRN2", target_bir_lowering=False, num_devices=1)
    arrays = {"x_dram": x, **{f"{g}_dram": a for g, (a, _) in packs.items()}}
    aps = {n: nc.dram_tensor(n, a.shape, F32, kind="ExternalInput").ap() for n, a in arrays.items()}
    out = nc.dram_tensor("out_dram", x.shape, F32, kind="ExternalOutput").ap()
    build(nc, aps["x_dram"], out, {g: aps[f"{g}_dram"] for g in packs}, {g: w for g, (_, w) in packs.items()}, NETWORK)
    r = run_bass_kernel_spmd(nc, [arrays], core_ids=[0])
    y = r.results[0]["out_dram"]
    return np.ascontiguousarray(y.T).reshape(BATCHES, TOKENS, P)
```

```python
from contextlib import ExitStack

import numpy as np

import concourse.bass as bass
from concourse import mybir

ALU = mybir.AluOpType
ACT = mybir.ActivationFunctionType
F32 = mybir.dt.float32
BF16 = mybir.dt.bfloat16
AX = mybir.AxisListType.X

P = 128
BATCHES, TOKENS = 8, 256
N_STREAMS = 4
PER_STREAM = BATCHES // N_STREAMS
COLS = PER_STREAM * TOKENS
TILES = COLS // P
BANK = 512
HEADS8, HD8 = 16, 8
NEG = -1.0e30


def k_tiles(w):
    k, n = w.shape
    nt = -(-k // P)
    out = np.zeros((nt * P, n), w.dtype)
    out[:k] = w
    return out.reshape(nt, P, n).transpose(1, 0, 2).reshape(P, nt * n)


def as_cols(v):
    return k_tiles(v.reshape(-1, 1))


def as_rows(v):
    return np.broadcast_to(v.reshape(1, -1), (P, v.size))


def pack(parts):
    where, at = {}, 0
    for name, a in parts.items():
        where[name] = (at, a.shape[0], a.shape[1])
        at += a.shape[1]
    out = np.zeros((P, at), np.float32)
    for name, a in parts.items():
        c, r, n = where[name]
        out[:r, c:c + n] = a
    return out, where


def constants():
    ch = np.arange(P)
    c = {"ident": np.eye(P), "mean": np.full((P, P), 1.0 / P), "center": np.eye(P) - 1.0 / P,
         "ones": np.ones((P, P))}
    g8 = (ch[:, None] // HD8 == ch[None] // HD8).astype(float)
    c["group8"] = g8
    c["mean8"] = g8 / HD8
    c["center8"] = np.eye(P) - g8 / HD8
    c["head_of_col_group"] = np.tile((ch[None] % 32 // HD8 == np.arange(4)[:, None]).astype(float).reshape(1, -1), (P, 1))
    c["channels_of_head"] = (np.arange(HEADS8)[None] == ch[:, None] // HD8).astype(float)
    c["expand16"] = (np.arange(HEADS8)[:, None] == ch[None] // HD8).astype(float)
    c["expand8"] = (np.arange(8)[:, None] == np.arange(4 * P)[None] // 64).astype(float)
    q, k = np.arange(P)[:, None], np.arange(P)[None]
    c["keys_up_to_query"] = (q <= k).astype(float)
    rot = np.zeros((P, P))
    for i in range(0, P, 2):
        rot[i + 1, i] = -1.0
        rot[i, i + 1] = 1.0
    c["pair_rotation"] = rot
    f = np.float32
    for name, base in (("global", 1000000.0), ("local", 10000.0)):
        inv = (f(1.0) / f(base) ** (np.arange(0, HD8, 2, dtype=f) / f(HD8))).astype(f)
        ang = (np.arange(TOKENS, dtype=f)[:, None] * inv[None]).astype(f)
        ang = ang[:, (ch % HD8) // 2].T
        c[f"cos_{name}"], c[f"sin_{name}"] = np.cos(ang), np.sin(ang)
    hd, window = 64, 64
    half = np.arange(0, hd, 2, dtype=f)
    inv = (f(1.0) / f(10000.0) ** (half / f(hd))).astype(f)
    t = np.arange(TOKENS, dtype=f)
    ang = (t[:, None] * inv[None]).astype(f)
    scale = ((half + f(0.4 * hd)) / f(1.4 * hd))[None] ** ((t - TOKENS // 2) / f(window // 2))[:, None]
    scale = scale.astype(f)
    for name, s in (("q", scale), ("k", (f(1.0) / scale).astype(f))):
        cs, sn = np.cos(ang) * s, np.sin(ang) * s
        c[f"xpos_cos_{name}"] = k_tiles(np.concatenate([cs, cs], 1))
        c[f"xpos_sin_{name}"] = k_tiles(np.concatenate([-sn, sn], 1))
    c["eps"] = np.tile(np.array([[1e-5, 1e-12, 1e-6, 12 * np.log(2.0)]]), (P, 1))
    c["half_of_pair"] = (ch[:, None] // hd == np.arange(2)[None]).astype(float)
    return {k: np.ascontiguousarray(v, np.float32) for k, v in c.items()}


def masks():
    out = {"ident": np.eye(P)}
    q, k = np.arange(P)[:, None], np.arange(TOKENS)[None]
    for name, band in (("causal", TOKENS), ("band32", 31), ("band64", 64)):
        for t in range(2):
            first = 64 if (name, t) == ("band64", 1) else 0
            d = (q + t * P) - k[:, first:(t + 1) * P]
            out[f"{name}_{t}"] = np.where((d >= 0) & (d <= band), 0.0, NEG)
    for t in range(2):
        out[f"block32_{t}"] = ((q + t * P) // 32 >= k // 32).astype(float)
    out["row_of_32"] = np.tile(np.eye(32), (3, 1))
    out["row_of_8"] = np.tile(np.eye(8), (3, 1))
    out["spread"] = gla_spread()
    return {k: v.astype(np.float32) for k, v in out.items()}


def gla_spread(K=32):
    per = P // K
    row, p = np.arange(K)[:, None], np.arange(P)[None]
    tiles = [(row == per * i + p // K) for i in range(K // per)]
    return np.tile(np.concatenate(tiles, 1).astype(np.float32), (3, 1))


def scan_layout(p, w_in, w_xproj, w_dt, b_dt, a_log, d, w_out):
    return {"w_in": p[w_in], "w_rank": k_tiles(p[w_xproj][:, :p[w_dt].shape[0]]),
            "w_bc": k_tiles(np.tile(p[w_xproj][:, p[w_dt].shape[0]:], (1, 3))), "w_dt": p[w_dt], "b_dt": as_cols(p[b_dt]),
            "a_log": k_tiles(p[a_log]), "d": as_cols(p[d]), "w_out": k_tiles(p[w_out])}


def layouts(p):
    g = {}
    g["L0_scan"] = scan_layout(p, *(f"L0_attn_a_{n}" for n in
                                    ("W_in", "W_xproj", "W_dt", "b_dt", "A_log", "D", "W_out")))
    n = "L0_attn_b_"
    w0 = np.zeros((P, P), np.float32)
    for h in range(HEADS8):
        w0[h * HD8:(h + 1) * HD8, h * HD8:(h + 1) * HD8] = p[n + "W_init"][0, h]
    g["L0_linear"] = {**{w: p[n + w].T for w in ("Wq", "Wk", "Wv", "Wg", "Wo")},
                      **{w: p[n + w] for w in ("conv_q", "conv_k", "conv_v")}, "state0": w0,
                      "ln_gamma": as_cols(np.tile(p[n + "ln_gamma"], HEADS8)),
                      "ln_beta": as_cols(np.tile(p[n + "ln_beta"], HEADS8))}
    n = "L0_ffn_"
    e = p[n + "w1"].shape[0]
    g["L0_experts"] = {"w_route": np.concatenate([p[n + "lang_w"], p[n + "router_w"]]).T,
                       "b_route": as_rows(np.concatenate([p[n + "lang_b"], p[n + "router_b"]])),
                       "b1": as_cols(p[n + "b1"].reshape(-1)), "b2": np.tile(p[n + "b2"], (3, 1)),
                       "w1": p[n + "w1"].transpose(1, 0, 2).reshape(P, -1),
                       "w2": k_tiles(p[n + "w2"].reshape(-1, P))}
    n = "L1_attn_a_"
    g["L1_gla"] = {**{f"w{c}": np.tile(p[n + "W" + c], (1, 3)) for c in "qkg"},
                   **{f"b{c}": np.tile(p[n + "b" + c], 3).reshape(-1, 1) for c in "qkg"},
                   "wv": np.tile(p[n + "Wv"], (1, 4)), "bv": as_cols(np.tile(p[n + "bv"], 4)),
                   "Wo": np.tile(p[n + "Wo"], (4, 1)), "bo": as_cols(p[n + "bo"])}
    n = "L1_attn_b_"
    g["L1_attn"] = {**{w: p[n + w] for w in ("Wq", "Wl", "Wk", "Wv", "Wo")},
                    **{w: as_cols(p[n + w]) for w in ("bq", "bk", "bo")},
                    "bl": p[n + "bl"].reshape(-1, 1), "bv": as_rows(p[n + "bv"])}
    n = "L1_ffn_"
    g["L1_local"] = {}
    for d in range(p[n + "wqkv"].shape[0]):
        g["L1_local"].update({
            f"wqkv{d}": p[n + "wqkv"][d], f"q_scale{d}": as_rows(p[n + "q_scale"][d]),
            f"k_scale{d}": as_rows(p[n + "k_scale"][d]), f"wo{d}": k_tiles(p[n + "wo"][d]),
            f"ln_g{d}": as_cols(p[n + "ln_g"][d]), f"ln_b{d}": as_cols(p[n + "ln_b"][d]),
            f"w1{d}": p[n + "w1"][d], f"w2{d}": k_tiles(p[n + "w2"][d]), f"b2{d}": as_cols(p[n + "b2"][d]),
            f"b1a{d}": as_cols(np.split(p[n + "b1"][d], 2)[0]),
            f"b1g{d}": as_cols(np.split(p[n + "b1"][d], 2)[1])})
    n = "L2_attn_a_"
    g["L2_scan"] = scan_layout(p, *(n + w for w in ("in_proj_w", "x_proj_w", "dt_proj_w", "dt_proj_b",
                                                    "A_log", "D", "out_proj_w")))
    g["L2_scan"]["conv_w"] = k_tiles(p[n + "conv_w"][:, 0])
    g["L2_scan"]["conv_b"] = as_cols(p[n + "conv_b"])
    n = "L2_attn_b_"
    g["L2_attn"] = {**{w: p[n + w].T for w in ("Wq", "Wk", "Wv", "Wo")},
                    **{w: as_cols(p[n + w]) for w in ("bq", "bk", "bo")}, "bv": as_rows(p[n + "bv"])}
    n = "L2_ffn_"
    g["L2_experts"] = {"w_route": p[n + "gate_w"].T,
                       "w1": p[n + "w1"].transpose(1, 0, 2).reshape(P, -1),
                       "w3": p[n + "w3"].transpose(1, 0, 2).reshape(P, -1),
                       "w2": np.concatenate([k_tiles(p[n + "w2"][i]) for i in range(e)], 1)}
    n = "L3_attn_a_"
    g["L3_blocks"] = {"w_qkv": p[n + "qkv_w"].T, "Wo": p[n + "proj_w"].T, "bo": as_cols(p[n + "proj_b"])}
    n = "L3_attn_b_"

    def over_heads(w):
        return np.repeat(w.reshape(w.shape[0], -1, HD8), HEADS8 * HD8 // w.shape[1], axis=1).reshape(w.shape[0], P)

    g["L3_gqa"] = {"norm1": as_cols(p[n + "norm1_w"]), "norm2": as_cols(p[n + "norm2_w"]),
                   "g_wq": p[n + "g_wq"], "g_down": p[n + "g_kv_down"], "g_wk": over_heads(p[n + "g_k_up"]),
                   "g_wv": over_heads(p[n + "g_v_up"]), "g_wo": p[n + "g_wo"], "l_wq": p[n + "l_wq"],
                   "l_wk": over_heads(p[n + "l_wk"]), "l_wv": over_heads(p[n + "l_wv"]), "l_wo": p[n + "l_wo"]}
    n = "L3_ffn_"
    g["L3_slots"] = {"slots": p[n + "slot_init"].T, "w1x": p[n + "w1"][:P], "w1s": p[n + "w1"][P:],
                     "b1": p[n + "b1"].reshape(-1, 1), "w2": p[n + "w2"], "b2": as_rows(p[n + "b2"]),
                     "tau": as_rows(p[n + "tau"]), "Wih": p[n + "Wih"].T, "Whh": p[n + "Whh"].T,
                     "bih": as_cols(p[n + "bih"]), "bhh": as_cols(p[n + "bhh"]),
                     "wq": p[n + "wq"], "bq": p[n + "bq"].reshape(-1, 1), "wk": p[n + "wk"],
                     "bk": p[n + "bk"].reshape(-1, 1), "wv": p[n + "wv"], "bv": as_rows(p[n + "bv"]),
                     "ln_g": as_cols(p[n + "ln_g"]), "ln_b": as_cols(p[n + "ln_b"]), "wvp": p[n + "wvp"],
                     "bvp": as_rows(p[n + "bvp"]), "wo": p[n + "wo"], "bo": as_cols(p[n + "bo"])}
    return g


def cols(ap):
    return int(np.prod(ap.shape[1:]))


class Queue:
    per_col, fixed = 1.0, 60

    def __init__(self, engine):
        self.engine, self.free = engine, 0.0

    def wait_ge(self, sem, value):
        self.engine.wait_ge(sem, value)

    def spend(self, out, factor=1.0):
        self.free += self.fixed + factor * self.per_col * cols(out)


class TensorQueue(Queue):
    per_col, fixed = 1 / 2.4, 3

    def matmul(self, out, lhsT, rhs, **kw):
        self.spend(out, 4 if rhs.dtype == F32 else 1)
        return self.engine.matmul(out, lhsT, rhs, **kw)

    def transpose(self, out, src, ident):
        self.spend(out, 2)
        return self.engine.transpose(out, src, ident)


class ActQueue(Queue):
    per_col, fixed, per_channel_operands = 1 / 1.2, 51, 93
    table = None
    LN_EXP, LN_EXP_TABLE = (ACT.Ln, ACT.Exp), 6
    IN_EVERY_TABLE = (ACT.Copy, ACT.Identity, ACT.Square)

    def table_of(self, function):
        return self.LN_EXP if function in self.LN_EXP else function

    def activation(self, out, src, function, **kw):
        if function not in self.IN_EVERY_TABLE:
            table = self.table_of(function)
            if table != self.table:
                self.table = table
                self.free += 1280
                if table == self.LN_EXP:
                    self.engine.add_instruction(mybir.InstLoadActFuncSet(
                        name=self.nc.get_next_instruction_name(), act_func_set_id=self.LN_EXP_TABLE))
        self.spend(out)
        if "bias" in kw or "scale" in kw:
            self.free += self.per_channel_operands
        return self.engine.activation(out, src, function, **kw)


class VectorQueue(Queue):
    per_col, fixed = 1 / 0.96, 68

    def tensor_tensor(self, out, a, b, op):
        self.spend(out)
        return self.engine.tensor_tensor(out, a, b, op)

    def tensor_scalar(self, out, src, *args):
        self.spend(out)
        return self.engine.tensor_scalar(out, src, *args)

    def scalar_tensor_tensor(self, out, *args):
        self.spend(out)
        return self.engine.scalar_tensor_tensor(out, *args)

    def tensor_tensor_scan(self, out, *args):
        self.spend(out)
        return self.engine.tensor_tensor_scan(out, *args)

    def tensor_copy(self, out, src):
        self.spend(out)
        return self.engine.tensor_copy(out, src)

    def tensor_reduce(self, out, src, axis, op):
        self.spend(src)
        return self.engine.tensor_reduce(out, src, axis, op)

    def reciprocal(self, out, src):
        self.spend(out, 6)
        return self.engine.reciprocal(out, src)

    def memset(self, out, value):
        self.spend(out, 0.5)
        return self.engine.memset(out, value)

    def max(self, out, src):
        self.spend(src)
        return self.engine.max(out, src)

    def match_replace(self, out, *args, **kw):
        self.spend(out)
        return self.engine.match_replace(out, *args, **kw)


class PoolQueue(VectorQueue):
    per_col, fixed = 2.4, 0


class Core:

    def __init__(self, nc, ctx):
        self.nc = nc
        self.engines = {"pe": TensorQueue(nc.tensor), "act": ActQueue(nc.scalar), "dve": VectorQueue(nc.vector),
                        "pool": PoolQueue(nc.gpsimd), "sp": Queue(nc.sync)}
        self.engines["act"].nc = nc
        self.sems = {e: ctx.enter_context(nc.semaphore(f"steps_{e}")) for e in ("pe", "act", "dve", "pool")}
        self.count = dict.fromkeys(self.sems, 0)
        self.waited = {}
        self.ends = {}

    def wait(self, engine, sem_name, value):
        if self.waited.get((engine, sem_name), 0) < value:
            self.waited[engine, sem_name] = value
            self.engines[engine].wait_ge(self.sems[sem_name], value)

    def count_up(self, engine, instruction):
        self.count[engine] += 1
        instruction.then_inc(self.sems[engine], 1)
        self.ends[engine, self.count[engine]] = self.engines[engine].free + STEP_LATENCY
        return engine, self.count[engine]


class Weights:

    def __init__(self, buf, where):
        self.buf, self.where, self.extra = buf, where, None
        self.prepared = None

    def __getitem__(self, name):
        c, r, n = self.where[name]
        return self.buf[0:r, c:c + n]


class Stream:

    def __init__(self, core, index, x, scratch, psum, const, masks):
        self.core, self.index, self.x, self.scratch, self.psum = core, index, x, scratch, psum
        self.c, self.m = const, masks
        if psum is not None:
            self.a, self.b = psum[:, 0:BANK], psum[:, BANK:2 * BANK]
        self.last, self.engine, self.used = (), None, 0
        self.parts = ()
        self.wants = None


    def _on(self, engine):
        for step in self.last:
            self.core.wait(engine, *step)
        self.engine = engine
        queue = self.core.engines[engine]
        queue.free = max([queue.free] + [self.core.ends[step] for step in self.last])
        return queue

    def copy(self, out, src):
        begin = max(self.core.ends[step] for step in self.last)
        act, dve = (max(self.core.engines[e].free, begin) for e in ("act", "dve"))
        if act <= dve:
            self.end(self.act().activation(out, src, ACT.Copy))
        else:
            self.end(self.dve().tensor_copy(out, src))

    def ready(self):
        if self.parts:
            return min(p.ready() for p in self.parts)
        begin = max([self.core.ends[step] for step in self.last], default=0.0)
        act = self.core.engines["act"]
        if self.wants and act.table_of(self.wants) != act.table:
            begin += TABLE_PATIENCE
        return begin

    def pe(self):
        return self._on("pe")

    def act(self):
        return self._on("act")

    def dve(self):
        return self._on("dve")

    def pool(self):
        return self._on("pool")

    def end(self, instruction):
        self.last = (self.core.count_up(self.engine, instruction),)

    def needs(self, group):
        for e in ("pe", "act", "dve", "pool"):
            self.core.wait(e, f"load_{group}", 16)

    def wait_all(self, engine, value):
        for e in ("dve", "pool"):
            self.core.wait(e, engine, value)

    def branch(self, i, scratch):
        base = self.used
        self.take(scratch)
        b = Stream(self.core, self.index, self.x, self.scratch[:, base:base + scratch], None, self.c, self.m)
        b.a, b.last = (self.a, self.b)[i], self.last
        return b

    def twin(self):
        t = Stream(self.core, self.index, self.x, self.scratch, self.psum, self.c, self.m)
        t.last, t.used = self.last, self.used
        return t

    def join(self, branches, chains):
        going = dict(zip(branches, chains))
        while going:
            b = min(going, key=Stream.ready)
            self.parts = tuple(going)
            yield
            try:
                b.wants = next(going[b])
            except StopIteration:
                del going[b]
        self.parts = ()
        self.last = tuple(step for b in branches for step in b.last)

    def take_bf16(self, n, parts=P):
        return self.take(n // 2, parts=parts).bitcast(BF16)

    def fresh(self):
        self.used = 0

    def take(self, *shape, parts=P):
        n = int(np.prod(shape))
        ap = self.scratch[0:parts, self.used:self.used + n]
        self.used += n
        assert self.used <= self.scratch.shape[1], (self.used, shape)
        if len(shape) == 2:
            ap = ap.rearrange("p (a b) -> p a b", b=shape[1])
        if len(shape) == 3:
            ap = ap.rearrange("p (a b c) -> p a b c", b=shape[1], c=shape[2])
        return ap


SCRATCH = 6212

TABLE_PATIENCE = 500
STEP_LATENCY = 100


def v2(ap, n):
    return ap.rearrange("p (a b) -> p a b", b=n)


def over(ap, shape):
    return ap.broadcast_to(shape)


def normalise(s, src, out, center, mean, eps, gain=None, shift=None):
    n = src.shape[-1]
    mark = s.used
    sq = s.take(n)
    a, b = s.a[:, 0:n], s.b[:, 0:n]
    centred = src
    if center is not None:
        s.end(s.pe().matmul(a, center, src, start=True, stop=True)); yield
        centred = a
    s.end(s.act().activation(sq, centred, ACT.Square)); yield
    s.end(s.pe().matmul(b, mean, sq, start=True, stop=True)); yield
    yield ACT.Ln
    s.end(s.act().activation(sq, b, ACT.Ln, bias=eps)); yield
    yield ACT.Exp
    s.end(s.act().activation(sq, sq, ACT.Exp, scale=-0.5)); yield
    s.end(s.dve().tensor_tensor(out, centred, sq, ALU.mult)); yield
    if gain is not None:
        if shift is not None:
            s.end(s.dve().tensor_scalar(out, out, gain, shift, ALU.mult, ALU.add)); yield
        else:
            s.end(s.dve().tensor_scalar(out, out, gain, None, ALU.mult)); yield
    s.used = mark


def layer_norm(s, src, out, gain=None, shift=None):
    yield from normalise(s, src, out, s.c["center"], s.c["mean"], s.c["eps"][:, 0:1], gain, shift)


def to_channels(s, src, dst, bank):
    t = dst.shape[1]
    e = s.pe()
    for i in range(t):
        last = e.transpose(bank[:, i * P:(i + 1) * P], src[:, i * P:(i + 1) * P], s.c["ident"])
    s.end(last); yield
    s.copy(dst, v2(bank[:, 0:t * P], P)); yield


def split_rows(s, src, parts):
    mark = s.used
    n = src.shape[-1]
    rest = s.take(n)
    s.end(s.act().activation(parts, src, ACT.Copy)); yield
    s.end(s.dve().tensor_tensor(rest[0:64], src[0:64], parts[0:64], ALU.subtract)); yield
    s.end(s.dve().tensor_copy(parts[0:64], rest[0:64])); yield
    s.end(s.dve().tensor_tensor(rest[0:32], rest[0:32], parts[0:32], ALU.subtract)); yield
    s.end(s.dve().tensor_copy(parts[0:32], rest[0:32])); yield
    s.used = mark


def scan_block(s, w, conv, a_is_exp, clip):
    D, N = 2, 16
    rank = w["w_dt"].shape[0]
    T = TOKENS
    s.fresh()
    xn = s.take(COLS)
    yield from layer_norm(s, s.x, xn)
    xc, delta, dx = (s.take(D, T) for _ in range(3))
    mark = s.used
    padded = s.take(D, T + 3)
    s.used = mark
    bcn2, a2, b2 = ([s.take(D, T), s.take(D, T)] for _ in range(3))
    b = b2[0]
    low = s.take(T, parts=rank)
    bc = s.take_bf16(T, parts=3 * 2 * N)
    A = s.take(D, N)
    yield ACT.Exp
    s.end(s.act().activation(A, v2(w["a_log"], N), ACT.Exp)); yield
    s.end(s.dve().tensor_scalar(A, A, -1.0, None, ALU.mult)); yield
    for a in a2:
        s.end(s.dve().memset(a, 0.0)); yield
    A2, B2 = v2(s.a, T), v2(s.b, T)
    for bt in range(PER_STREAM):
        xb = xn[:, bt * T:(bt + 1) * T]
        e = s.pe()
        for d in range(D):
            last = e.matmul(A2[:, d, :], w["w_in"][:, d * P:(d + 1) * P], xb, start=True, stop=True)
        s.end(last); yield
        if conv:
            s.end(s.dve().memset(padded[:, :, 0:3], 0.0)); yield
            s.copy(padded[:, :, 3:3 + T], A2); yield
            taps = v2(w["conv_w"], 4)
            for k in range(4):
                e = s.dve()
                for d in range(D):
                    tap = taps[:, d, k:k + 1]
                    if k == 0:
                        last = e.tensor_scalar(b[:, d, :], padded[:, d, 0:T], tap, w["conv_b"][:, d:d + 1],
                                               ALU.mult, ALU.add)
                    else:
                        last = e.scalar_tensor_tensor(b[:, d, :], padded[:, d, k:k + T], tap, b[:, d, :],
                                                      ALU.mult, ALU.add)
                s.end(last); yield
            yield ACT.Silu
            s.end(s.act().activation(xc, b, ACT.Silu)); yield
        else:
            s.copy(xc, A2); yield
        e = s.pe()
        for d in range(D):
            last = e.matmul(s.a[0:rank, 0:T], w["w_rank"][:, d * rank:(d + 1) * rank], xc[:, d, :],
                            start=(d == 0), stop=(d == D - 1))
        for d in range(D):
            last = e.matmul(s.b[0:6 * N, 0:T], w["w_bc"][:, d * 6 * N:(d + 1) * 6 * N], xc[:, d, :],
                            start=(d == 0), stop=(d == D - 1))
        s.end(last); yield
        s.copy(low, s.a[0:rank, 0:T]); yield
        yield from split_rows(s, s.b[0:6 * N, 0:T], bc)
        e = s.pe()
        for d in range(D):
            last = e.matmul(B2[:, d, :], w["w_dt"][:, d * P:(d + 1) * P], low, start=True, stop=True)
        s.end(last); yield
        e = s.act()
        for d in range(D):
            last = e.activation(delta[:, d, :], B2[:, d, :], ACT.Identity, bias=w["b_dt"][:, d:d + 1])
        s.end(last); yield
        s.end(s.dve().scalar_tensor_tensor(dx, delta, -1.0, delta, ALU.mult, ALU.max)); yield
        yield ACT.Exp
        s.end(s.act().activation(dx, dx, ACT.Exp, scale=-1.0)); yield
        yield ACT.Ln
        s.end(s.act().activation(dx, dx, ACT.Ln, bias=1.0)); yield
        s.end(s.dve().scalar_tensor_tensor(delta, delta, 0.0, dx, ALU.max, ALU.add)); yield
        if clip:
            s.end(s.dve().tensor_scalar(delta, delta, clip[0], clip[1], ALU.max, ALU.min)); yield
        s.end(s.dve().tensor_tensor(dx, delta, xc, ALU.mult)); yield

        make, use = s.twin(), s.twin()
        made, used = {}, {-2: s.last, -1: s.last}

        def make_state(n):
            a, b, bcn = a2[n % 2], b2[n % 2], bcn2[n % 2]
            e = make.pe()
            for i in range(2):
                row = i * N + n
                last = e.matmul(B2[:, i, :], over(s.m["row_of_32"][:, row:row + 1], [6 * N, P]), bc, start=True, stop=True)
            make.end(last); yield
            make.end(make.act().activation(bcn, B2, ACT.Copy)); yield
            make.end(make.pool().tensor_tensor(b, dx, over(bcn[:, 0:1, :], [P, D, T]), ALU.mult))
            b_done = make.last
            e = core_act
            for d in range(D):
                last = e.activation(a[:, d, 1:T], delta[:, d, 1:T], ACT.Exp if a_is_exp else ACT.Identity,
                                    scale=A[:, d, n:n + 1], bias=0.0 if a_is_exp else 1.0)
            make.last = (s.core.count_up("act", last),)
            made[n] = make.last + b_done; yield

        def use_state(n):
            a, b, bcn = (x.rearrange("p a b -> p (a b)") for x in (a2[n % 2], b2[n % 2], bcn2[n % 2]))
            use.end(use.dve().tensor_tensor_scan(b, a, b, 0.0, ALU.mult, ALU.add)); yield
            use.end(use.dve().tensor_tensor(b2[n % 2], b2[n % 2], over(bcn2[n % 2][:, 1:2, :], [P, D, T]), ALU.mult)); yield
            use.end(use.pe().matmul(s.a, s.c["ident"], b, start=(n == 0), stop=(n == N - 1)))
            used[n] = use.last; yield

        core_act = s.core.engines["act"]
        chains = {make: (make_state, used, 2), use: (use_state, made, 0)}
        begun, going = {make: 0, use: 0}, {}
        while going or begun[use] < N:
            for c, (state, needed, before) in chains.items():
                n = begun[c]
                if c not in going and n < N and n - before in needed:
                    c.last += needed[n - before]
                    going[c], begun[c] = state(n), n + 1
            s.parts = tuple(going)
            yield
            c = min(going, key=Stream.ready)
            try:
                c.wants = next(going[c])
            except StopIteration:
                del going[c]
        s.parts, s.last = (), use.last
        a, b = a2[0], b2[0]
        z = b2[1]
        e = s.pe()
        for d in range(D):
            last = e.matmul(B2[:, d, :], w["w_in"][:, (D + d) * P:(D + d + 1) * P], xb, start=True, stop=True)
        s.end(last); yield
        yield ACT.Silu
        s.end(s.act().activation(z, B2, ACT.Silu)); yield
        e = s.dve()
        for d in range(D):
            last = e.scalar_tensor_tensor(b[:, d, :], xc[:, d, :], w["d"][:, d:d + 1], A2[:, d, :], ALU.mult, ALU.add)
        s.end(last); yield
        s.end(s.dve().tensor_tensor(b, b, z, ALU.mult)); yield
        e = s.pe()
        for d in range(D):
            last = e.matmul(s.b[:, 0:T], w["w_out"][:, d * P:(d + 1) * P], b[:, d, :], start=(d == 0), stop=(d == D - 1))
        s.end(last); yield
        xs = s.x[:, bt * T:(bt + 1) * T]
        s.end(s.dve().tensor_tensor(xs, xs, s.b[:, 0:T], ALU.add)); yield


def linear_attention(s, w):
    s.fresh()
    T = TOKENS
    xn = s.take(COLS)
    yield from layer_norm(s, s.x, xn)
    padded = s.take(PER_STREAM, T + 3)
    s.end(s.dve().memset(padded[:, :, 0:3], 0.0)); yield
    q, k, v = (s.take(COLS) for _ in range(3))
    for name, dst in (("q", q), ("k", k), ("v", v)):
        s.end(s.pe().matmul(s.a, w[f"W{name}"], xn, start=True, stop=True)); yield
        s.copy(padded[:, :, 3:], v2(s.a, T)); yield
        taps, y = w[f"conv_{name}"], v2(dst, T)
        for j in range(4):
            s.end(s.dve().scalar_tensor_tensor(y, padded[:, :, j:j + T], taps[:, j:j + 1],
                                               padded[:, :, 3:] if j == 0 else y, ALU.mult, ALU.add)); yield
        yield ACT.Silu
        s.end(s.act().activation(dst, dst, ACT.Silu)); yield
        if name != "v":
            yield from normalise(s, dst, dst, None, s.c["group8"], s.c["eps"][:, 1:2])
    v_tok, k_tok = s.take(TILES, P), s.take(PER_STREAM, P)
    e = s.pe()
    for t in range(TILES):
        last = e.transpose(s.a[:, t * P:(t + 1) * P], v[:, t * P:(t + 1) * P], s.c["ident"])
    for bt in range(PER_STREAM):
        last = e.transpose(s.b[:, bt * P:(bt + 1) * P], k[:, bt * T:bt * T + P], s.c["ident"])
    s.end(last); yield
    s.copy(v_tok, v2(s.a, P)); yield
    s.copy(k_tok, v2(s.b[:, 0:PER_STREAM * P], P)); yield
    state = s.take(P)
    o = v
    qm2, st, vm = [s.take(4, P), s.take(4, P)], s.take(4, P), s.take(4, P)

    def one_head_each(t, g):
        ahead = s.twin()
        ahead.end(ahead.pool().tensor_tensor(qm2[g % 2], over(q[:, t * P:(t + 1) * P].unsqueeze(1), [P, 4, P]),
                                             over(s.c["channels_of_head"][:, 4 * g:4 * g + 4].unsqueeze(2), [P, 4, P]), ALU.mult))
        return ahead.last

    made = one_head_each(0, 0)
    for t in range(TILES):
        bt, chunk = divmod(t, T // P)
        cols = slice(t * P, (t + 1) * P)
        if chunk == 0:
            carried = w["state0"]
        else:
            s.end(s.pe().matmul(s.a[:, 0:P], k_tok[:, bt, :], v_tok[:, t - 1, :], start=True, stop=True)); yield
            s.end(s.dve().tensor_tensor(state, s.c["group8"], s.a[:, 0:P], ALU.mult)); yield
            s.end(s.dve().tensor_tensor(state, state, w["state0"], ALU.add)); yield
            carried = state
        s.end(s.pool().tensor_tensor(vm, over(v_tok[:, t:t + 1, :], [P, 4, P]), v2(s.c["head_of_col_group"], P), ALU.mult)); yield
        s.end(s.pe().matmul(s.b[:, 0:P], carried, q[:, cols], start=True, stop=True, skip_group_check=True)); yield
        for g in range(4):
            rows = slice(32 * g, 32 * g + 32)
            s.last += made
            s.end(s.pe().matmul(s.a, k[:, cols], qm2[g % 2].rearrange("p a b -> p (a b)"), start=True, stop=True))
            if (t, g) != (TILES - 1, 3):
                made = one_head_each(t + (g + 1) // 4, (g + 1) % 4)
            yield
            s.end(s.dve().tensor_tensor(st, v2(s.a, P), over(s.c["keys_up_to_query"].unsqueeze(1), [P, 4, P]), ALU.mult)); yield
            e = s.pe()
            for j in range(4):
                last = e.matmul(s.b[rows, 0:P], vm[:, j, rows], st[:, j, :], start=False, stop=True, skip_group_check=True)
            s.end(last); yield
        s.copy(o[:, cols], s.b[:, 0:P]); yield
    yield from normalise(s, o, o, s.c["center8"], s.c["mean8"], s.c["eps"][:, 0:1], w["ln_gamma"], w["ln_beta"])
    s.end(s.pe().matmul(s.a, w["Wg"], xn, start=True, stop=True)); yield
    s.end(s.dve().tensor_tensor(o, o, s.a, ALU.mult)); yield
    s.end(s.pe().matmul(s.b, w["Wo"], o, start=True, stop=True)); yield
    s.end(s.dve().tensor_tensor(s.x, s.x, s.b, ALU.add)); yield


def keep_top(s, values, kept, n_top, fill):
    rows, n = values.shape[1], values.shape[2]
    top = s.take(rows, 8)
    e = s.dve()
    for r in range(rows):
        last = e.max(top[:, r, :], values[:, r, :])
    s.end(last); yield
    if n_top < 8:
        s.end(s.dve().memset(top[:, :, n_top:8], fill)); yield
    for r in range(rows):
        s.end(s.dve().match_replace(kept[:, r, :], top[:, r, :], values[:, r, :], 2 * fill)); yield
    s.end(s.dve().tensor_tensor(kept, kept, values, ALU.not_equal)); yield
    return top


def row_exp(s, logits, out, rows, n):
    m = s.take(rows)
    s.end(s.dve().tensor_reduce(m, logits, AX, ALU.max)); yield
    s.end(s.dve().tensor_tensor(out, logits, over(m.unsqueeze(2), [P, rows, n]), ALU.subtract)); yield
    yield ACT.Exp
    s.end(s.act().activation(out, out, ACT.Exp)); yield


def row_scale(s, values, rows, n):
    m = s.take(rows)
    s.end(s.dve().tensor_reduce(m, values, AX, ALU.add)); yield
    s.end(s.dve().reciprocal(m, m)); yield
    s.end(s.dve().tensor_tensor(values, values, over(m.unsqueeze(2), [P, rows, n]), ALU.mult)); yield


def gates_to_rows(s, gates, rows_bf16, rows):
    n = gates.shape[2]
    mark = s.used
    part, rest = s.take_bf16(TILES * n).rearrange("p (t n) -> p t n", n=n), s.take(TILES, n)
    by_token = s.take(TILES, 3, n)
    s.copy(part, gates); yield
    s.copy(by_token[:, :, 0, :], part); yield
    s.end(s.dve().tensor_tensor(rest, gates, part, ALU.subtract)); yield
    s.copy(part, rest); yield
    s.copy(by_token[:, :, 1, :], part); yield
    s.end(s.dve().tensor_tensor(by_token[:, :, 2, :], rest, part, ALU.subtract)); yield
    e = s.pe()
    for t in range(TILES):
        last = e.transpose(s.a[0:3 * n, t * P:(t + 1) * P], by_token[:, t].rearrange("p a n -> p (a n)"), s.c["ident"])
    s.end(last); yield
    s.copy(rows_bf16, s.a[0:3 * n, :]); yield
    if rows is not None:
        s.copy(rows, s.a[0:3 * n, :]); yield
    s.used = mark


def expert_mix(s, w):
    E, L = 8, 4
    s.fresh()
    xn = s.take(COLS)
    yield from layer_norm(s, s.x, xn)
    mark = s.used
    e = s.pe()
    for t in range(TILES):
        last = e.matmul(s.a[:, t * 16:t * 16 + L + E], xn[:, t * P:(t + 1) * P], w["w_route"], start=True, stop=True)
    s.end(last); yield
    logits = s.take(TILES, L + E)
    s.end(s.dve().tensor_tensor(logits, over(w["b_route"].unsqueeze(1), [P, TILES, L + E]),
                                v2(s.a[:, 0:16 * TILES], 16)[:, :, 0:L + E], ALU.add)); yield
    lang = s.take(TILES, L + 1)
    s.end(s.dve().memset(lang, 0.0)); yield
    yield from row_exp(s, logits[:, :, 0:L], lang[:, :, 0:L], TILES, L)
    yield from row_scale(s, lang[:, :, 0:L], TILES, L)
    pair = s.take(TILES, L)
    s.end(s.dve().tensor_tensor(pair, lang[:, :, 0:L], lang[:, :, 1:L + 1], ALU.add)); yield
    route, gates = s.take(TILES, E), s.take(TILES, E)
    e = s.dve()
    for i in range(E // L):
        last = e.scalar_tensor_tensor(route[:, :, i * L:(i + 1) * L], pair, 0.1,
                                      logits[:, :, L + i * L:L + (i + 1) * L], ALU.mult, ALU.add)
    s.end(last); yield
    yield from row_exp(s, route, route, TILES, E)
    yield from row_scale(s, route, TILES, E)
    yield from keep_top(s, route, gates, 2, -1.0)
    s.end(s.dve().tensor_tensor(gates, gates, route, ALU.mult)); yield
    yield from row_scale(s, gates, TILES, E)
    gates_t, gates_16 = s.take(COLS, parts=3 * E), s.take_bf16(COLS, parts=3 * E)
    yield from gates_to_rows(s, gates, gates_16, gates_t)
    s.end(s.pe().matmul(s.b, w["b2"], gates_t, start=True, stop=True)); yield
    s.end(s.dve().tensor_tensor(s.x, s.x, s.b, ALU.add)); yield
    h, gate = s.take(COLS), s.take(COLS)
    H = w["w1"].shape[-1] // E // P
    for x in range(E):
        s.end(s.pe().matmul(s.a, over(s.m["row_of_8"][:, x:x + 1], [3 * E, P]), gates_16, start=True, stop=True)); yield
        s.copy(gate, s.a); yield
        for t in range(H):
            i = x * H + t
            s.end(s.pe().matmul(s.a, w["w1"][:, i * P:(i + 1) * P], xn, start=True, stop=True)); yield
            yield ACT.Gelu
            s.end(s.act().activation(h, s.a, ACT.Gelu, bias=w["b1"][:, i:i + 1])); yield
            s.end(s.pe().matmul(s.b, w["w2"][:, i * P:(i + 1) * P], h, start=(t == 0), stop=(t == H - 1))); yield
        s.end(s.dve().tensor_tensor(gate, gate, s.b, ALU.mult)); yield
        s.end(s.pool().tensor_tensor(s.x, s.x, gate, ALU.add)); yield


def expert_swiglu(s, w):
    E = 8
    s.fresh()
    xn = s.take(COLS)
    yield from layer_norm(s, s.x, xn)
    e = s.pe()
    for t in range(TILES):
        last = e.matmul(s.a[:, t * E:(t + 1) * E], xn[:, t * P:(t + 1) * P], w["w_route"], start=True, stop=True)
    s.end(last); yield
    scores, gates = s.take(TILES, E), s.take(TILES, E)
    s.copy(scores, v2(s.a[:, 0:TILES * E], E)); yield
    yield from row_exp(s, scores, scores, TILES, E)
    yield from row_scale(s, scores, TILES, E)
    yield from keep_top(s, scores, gates, 2, -1.0)
    s.end(s.dve().tensor_tensor(gates, gates, scores, ALU.mult)); yield
    gates_16 = s.take_bf16(COLS, parts=3 * E)
    yield from gates_to_rows(s, gates, gates_16, None)
    hidden = w["w1"].shape[-1] // E
    sizes = [min(P, hidden - i) for i in range(0, hidden, P)]
    xe, h = s.take(COLS), s.take(COLS)
    for x in range(E):
        s.end(s.pe().matmul(s.a, over(s.m["row_of_8"][:, x:x + 1], [3 * E, P]), gates_16, start=True, stop=True)); yield
        s.end(s.dve().tensor_tensor(xe, xn, s.a, ALU.mult)); yield
        for t, m in enumerate(sizes):
            c = x * hidden + t * P
            s.end(s.pe().matmul(s.a[0:m, :], w["w1"][:, c:c + m], xe, start=True, stop=True)); yield
            yield ACT.Silu
            s.end(s.act().activation(h[0:m, :], s.a[0:m, :], ACT.Silu)); yield
            s.end(s.pe().matmul(s.a[0:m, :], w["w3"][:, c:c + m], xe, start=True, stop=True)); yield
            s.end(s.dve().tensor_tensor(h[0:m, :], h[0:m, :], s.a[0:m, :], ALU.mult)); yield
            i = (x * len(sizes) + t) * P
            s.end(s.pe().matmul(s.b, w["w2"][0:m, i:i + P], h[0:m, :], start=(x == 0 and t == 0),
                                stop=(x == E - 1 and t == len(sizes) - 1))); yield
    s.end(s.dve().tensor_tensor(s.x, s.x, s.b, ALU.add)); yield


def gated_linear_attention(s, w):
    K = 32
    per = P // K
    s.fresh()
    xn = s.take(COLS)
    yield from layer_norm(s, s.x, xn)
    rows = {}
    for c, f in (("q", ACT.Identity), ("k", ACT.Sigmoid), ("g", ACT.Sigmoid)):
        mark = s.used
        rows[c] = s.take_bf16(COLS, parts=3 * K)
        full = s.take(COLS, parts=3 * K)
        s.end(s.pe().matmul(s.a[0:3 * K, :], w[f"w{c}"], xn, start=True, stop=True)); yield
        s.end(s.act().activation(full, s.a[0:3 * K, :], f, bias=w[f"b{c}"])); yield
        yield from split_rows(s, full, rows[c])
        s.used = mark + COLS // 2
    v_all, b, h = s.take(COLS), s.take(COLS), s.take(COLS)

    def spread(c, i):
        return s.pe().matmul(s.a, s.m["spread"][:, i * P:(i + 1) * P], rows[c], start=True, stop=True)

    s.end(s.pe().matmul(s.a, w["wv"], xn, start=True, stop=True)); yield
    s.end(s.act().activation(v_all, s.a, ACT.Identity, bias=w["bv"])); yield
    for i in range(K // per):
        s.end(spread("k", i)); yield
        s.end(s.dve().tensor_tensor(b, v_all, s.a, ALU.mult)); yield
        s.end(spread("g", i)); yield
        e = s.dve()
        for bt in range(PER_STREAM):
            c = slice(bt * TOKENS, (bt + 1) * TOKENS)
            last = e.tensor_tensor_scan(h[:, c], s.a[:, c], b[:, c], 0.0, ALU.mult, ALU.add)
        s.end(last); yield
        s.end(spread("q", i)); yield
        s.end(s.dve().tensor_tensor(h, h, s.a, ALU.mult)); yield
        s.end(s.pe().matmul(s.b, w["Wo"], h, start=(i == 0), stop=(i == K // per - 1))); yield
    s.end(s.dve().scalar_tensor_tensor(s.x, s.b, w["bo"], s.x, ALU.add, ALU.add)); yield


def attend8(s, q, keys, vm, n_tiles, o, sums, scale, add_mask=None, zero_mask=None):
    nk = n_tiles * P
    mark = s.used
    qm2, p, m = [s.take(2, P), s.take(2, P)], s.take(2, nk), s.take(2)
    pt = p
    S = s.a[:, 0:2 * nk].rearrange("p (i k) -> p i k", k=nk)
    steps = [(half, g) for half in range(2) for g in range(4)]

    def one_head_each(n, after):
        half, g = steps[n]
        h = 4 * g + 2 * half
        ahead = s.twin()
        ahead.last = after
        ahead.end(ahead.pool().tensor_tensor(qm2[n % 2], over(q.unsqueeze(1), [P, 2, P]),
                                             over(s.c["channels_of_head"][:, h:h + 2].unsqueeze(2), [P, 2, P]), ALU.mult))
        return ahead.last

    made = one_head_each(0, s.last)
    for n, (half, g) in enumerate(steps):
        js = (2 * half, 2 * half + 1)
        rows = slice(32 * g, 32 * g + 32)
        if add_mask is not None:
            s.end(s.pe().matmul(S, s.m["ident"], over(add_mask.unsqueeze(1), [P, 2, nk]), start=True, stop=True)); yield
        s.last += made
        e = s.pe()
        for i in range(2):
            last = e.matmul(S[:, i, :], qm2[n % 2][:, i, :], keys[:, 0:nk], start=(add_mask is None),
                            stop=True, skip_group_check=True)
        s.end(last)
        if n + 1 < len(steps):
            made = one_head_each(n + 1, s.last)
        yield
        scores = S
        if zero_mask is not None:
            scores = p
            s.end(s.dve().tensor_tensor(scores, S, over(zero_mask[:, 0:nk].unsqueeze(1), [P, 2, nk]), ALU.mult)); yield
        s.end(s.dve().tensor_reduce(m, scores, AX, ALU.max)); yield
        s.end(s.dve().tensor_scalar(m, m, -scale, None, ALU.mult)); yield
        yield ACT.Exp
        e = s.act()
        for i, j in enumerate(js):
            last = e.activation(p[:, i, :], scores[:, i, :], ACT.Exp, bias=m[:, i:i + 1], scale=scale,
                                accum_out=sums[:, 4 * g + j:4 * g + j + 1])
        s.end(last); yield
        e = s.pe()
        for i in range(2):
            for c in range(n_tiles):
                last = e.transpose(S[:, i, c * P:(c + 1) * P], p[:, i, c * P:(c + 1) * P], s.c["ident"])
        s.end(last); yield
        s.copy(pt, S); yield
        e = s.pe()
        for i, j in enumerate(js):
            for c in range(n_tiles):
                last = e.matmul(s.a[rows, 0:P], vm[:, c, j, rows], pt[:, i, c * P:(c + 1) * P],
                                start=(i + c == 0), stop=(i + c == n_tiles))
        s.end(last); yield
        if half == 0:
            s.copy(o[rows, :], s.a[rows, 0:P]); yield
        else:
            s.end(s.dve().tensor_tensor(o[rows, :], o[rows, :], s.a[rows, 0:P], ALU.add)); yield
    s.used = mark


def divide_by_sums(s, o, sums):
    mark = s.used
    n = sums.shape[1]
    by_head = s.take(n * P, parts=HEADS8)
    s.end(s.dve().reciprocal(sums, sums)); yield
    e = s.pe()
    for t in range(n):
        last = e.transpose(s.a[0:HEADS8, t * P:(t + 1) * P], sums[:, t, :], s.c["ident"])
    s.end(last); yield
    s.copy(by_head, s.a[0:HEADS8, 0:n * P]); yield
    s.end(s.pe().matmul(s.a[:, 0:n * P], s.c["expand16"], by_head, start=True, stop=True)); yield
    s.end(s.dve().tensor_tensor(o, o, s.a[:, 0:n * P], ALU.mult)); yield
    s.used = mark


BRANCH8 = 2 * 2 * P + 2 * 2 * P + 2 + 2 * HEADS8


def attend_batches(s, q, k, vm, o, n_tiles, **masks):
    mark = s.used
    branches = [s.branch(i, BRANCH8) for i in range(PER_STREAM)]

    def chain(b, bt):
        sums = b.take(2, HEADS8)
        for qt in range(2):
            cols = slice((2 * bt + qt) * P, (2 * bt + qt + 1) * P)
            yield from attend8(b, q[:, cols], k[:, bt * TOKENS:(bt + 1) * TOKENS], vm[:, 2 * bt:2 * bt + 2],
                               n_tiles[qt], o[:, cols], sums[:, qt, :], HD8 ** -0.5,
                               **{n: m[qt] for n, m in masks.items()})
        yield from divide_by_sums(b, o[:, bt * TOKENS:(bt + 1) * TOKENS], sums)

    yield from s.join(branches, [chain(b, i) for i, b in enumerate(branches)])
    s.used = mark


def spread_values(s, v_tok, vm):
    n = v_tok.shape[1]
    mask = v2(s.c["head_of_col_group"], P)
    e = s.dve()
    for j in range(4):
        last = e.tensor_tensor(vm[:, :, j, :], v_tok, over(mask[:, j:j + 1, :], [P, n, P]), ALU.mult)
    s.end(last); yield


def values_by_token(s, src, wv, vm, bias=None):
    mark = s.used
    v_tok = s.take(TILES, P)
    e = s.pe()
    for t in range(TILES):
        last = e.matmul(s.a[:, t * P:(t + 1) * P], src[:, t * P:(t + 1) * P], wv, start=True, stop=True)
    s.end(last); yield
    if bias is None:
        s.copy(v_tok, v2(s.a, P)); yield
    else:
        s.end(s.dve().tensor_tensor(v_tok, over(bias.unsqueeze(1), [P, TILES, P]), v2(s.a, P), ALU.add)); yield
    yield from spread_values(s, v_tok, vm)
    s.used = mark


def project(s, w, src, dst, bias=None):
    m = w.shape[-1]
    s.end(s.pe().matmul(s.a[0:m, :], w, src, start=True, stop=True)); yield
    if bias is None:
        s.copy(dst, s.a[0:m, :]); yield
    else:
        s.end(s.act().activation(dst, s.a[0:m, :], ACT.Identity, bias=bias)); yield


def attention(s, w, latent, masked):
    s.fresh()
    xn = s.take(COLS)
    yield from layer_norm(s, s.x, xn)
    q, k, vm = s.take(COLS), s.take(COLS), s.take(TILES, 4, P)
    mark = s.used
    yield from project(s, w["Wq"], xn, q, w["bq"])
    src = xn
    if latent:
        m = w["Wl"].shape[-1]
        src = s.take(COLS, parts=m)
        yield from project(s, w["Wl"], xn, src, w["bl"])
    yield from project(s, w["Wk"], src, k, w["bk"])
    yield from values_by_token(s, src, w["Wv"], vm, w["bv"])
    s.used = mark
    o = xn
    zero = {"zero_mask": [s.m["block32_0"], s.m["block32_1"]]} if masked else {}
    yield from attend_batches(s, q, k, vm, o, (2, 2), **zero)
    s.end(s.pe().matmul(s.a, w["Wo"], o, start=True, stop=True)); yield
    s.end(s.dve().scalar_tensor_tensor(s.x, s.a, w["bo"], s.x, ALU.add, ALU.add)); yield


def block_attention(s, w):
    s.fresh()
    xn = s.take(COLS)
    yield from layer_norm(s, s.x, xn)
    q, k, v = (s.take(COLS) for _ in range(3))
    for i, dst in enumerate((q, k, v)):
        yield from project(s, w["w_qkv"][:, i * P:(i + 1) * P], xn, dst)
    qs, ks, prod = s.take(TILES), s.take(TILES), s.take(TILES, 2)
    s.end(s.dve().tensor_reduce(qs, v2(q, P), AX, ALU.add)); yield
    s.end(s.dve().tensor_reduce(ks, v2(k, P), AX, ALU.add)); yield
    s.end(s.dve().tensor_scalar(qs, qs, 1.0 / P, None, ALU.mult)); yield
    s.end(s.dve().tensor_scalar(ks, ks, 1.0 / P, None, ALU.mult)); yield
    e = s.dve()
    for bt in range(PER_STREAM):
        two = slice(2 * bt, 2 * bt + 2)
        last = e.tensor_tensor(prod[:, two, :], over(qs[:, two].unsqueeze(2), [P, 2, 2]),
                               over(ks[:, two].unsqueeze(1), [P, 2, 2]), ALU.mult)
    s.end(last); yield
    n = TILES * 2
    s.end(s.pe().matmul(s.a[:, 0:n], s.c["group8"], prod.rearrange("p a b -> p (a b)"), start=True, stop=True)); yield
    s.copy(prod, v2(s.a[:, 0:n], 2)); yield
    second, first = s.take(TILES), s.take(TILES)
    s.end(s.dve().tensor_tensor(second, prod[:, :, 1], prod[:, :, 0], ALU.is_gt)); yield
    s.end(s.dve().tensor_scalar(first, second, -1.0, 1.0, ALU.mult, ALU.add)); yield
    o = xn
    branches = [s.branch(i, BRANCH8 - 2 * P + 7 * P) for i in range(PER_STREAM)]

    def chain(b, bt):
        kc, vc, v_tok, vm = b.take(P), b.take(P), b.take(1, P), b.take(1, 4, P)
        sums = b.take(2, HEADS8)
        lo = bt * TOKENS
        for t in (2 * bt, 2 * bt + 1):
            for src, dst in ((k, kc), (v, vc)):
                b.end(b.dve().tensor_scalar(dst, src[:, lo:lo + P], first[:, t:t + 1], None, ALU.mult)); yield
                b.end(b.dve().scalar_tensor_tensor(dst, src[:, lo + P:lo + 2 * P], second[:, t:t + 1], dst, ALU.mult, ALU.add)); yield
            yield from to_channels(b, vc, v_tok, b.a)
            yield from spread_values(b, v_tok, vm)
            cols = slice(t * P, (t + 1) * P)
            yield from attend8(b, q[:, cols], kc, vm, 1, o[:, cols], sums[:, t - 2 * bt, :], HD8 ** -0.5)
        yield from divide_by_sums(b, o[:, lo:lo + TOKENS], sums)

    yield from s.join(branches, [chain(b, i) for i, b in enumerate(branches)])
    s.end(s.pe().matmul(s.a, w["Wo"], o, start=True, stop=True)); yield
    s.end(s.dve().scalar_tensor_tensor(s.x, s.a, w["bo"], s.x, ALU.add, ALU.add)); yield


def grouped_query_attention(s, w):
    s.fresh()
    y, xn, q, k = (s.take(COLS) for _ in range(4))
    vm = s.take(TILES, 4, P)
    yield from layer_norm(s, s.x, y)

    def rotate_and_norm(dst, kind):
        tmp = s.take(COLS)
        s.end(s.pe().matmul(s.a, s.c["pair_rotation"], dst, start=True, stop=True)); yield
        sin = over(s.c[f"sin_{kind}"].unsqueeze(1), [P, PER_STREAM, TOKENS])
        cos = over(s.c[f"cos_{kind}"].unsqueeze(1), [P, PER_STREAM, TOKENS])
        s.end(s.dve().tensor_tensor(v2(tmp, TOKENS), sin, v2(s.a, TOKENS), ALU.mult)); yield
        s.end(s.dve().tensor_tensor(v2(dst, TOKENS), v2(dst, TOKENS), cos, ALU.mult)); yield
        s.end(s.dve().tensor_tensor(dst, dst, tmp, ALU.add)); yield
        s.used -= COLS
        yield from normalise(s, dst, dst, None, s.c["mean8"], s.c["eps"][:, 2:3])

    for kind, gain in (("global", "norm1"), ("local", "norm2")):
        yield from normalise(s, y, xn, None, s.c["mean"], s.c["eps"][:, 2:3], w[gain])
        p = kind[0] + "_"
        yield from project(s, w[p + "wq"], xn, q)
        src = xn
        mark = s.used
        if kind == "global":
            src = s.take(COLS, parts=w["g_down"].shape[-1])
            yield from project(s, w["g_down"], xn, src)
        yield from project(s, w[p + "wk"], src, k)
        yield from values_by_token(s, src, w[p + "wv"], vm)
        s.used = mark
        for dst in (q, k):
            yield from rotate_and_norm(dst, kind)
        mask = "causal" if kind == "global" else "band32"
        yield from attend_batches(s, q, k, vm, xn, (1, 2), add_mask=[s.m[f"{mask}_0"], s.m[f"{mask}_1"]])
        s.end(s.pe().matmul(s.a, w[p + "wo"], xn, start=True, stop=True)); yield
        s.end(s.dve().tensor_tensor(y, y, s.a, ALU.add)); yield
    s.end(s.dve().tensor_tensor(s.x, s.x, y, ALU.add)); yield


def shift_tokens(s, src, out):
    src, out = v2(src, TOKENS), v2(out, TOKENS)
    half = P // 2
    e = s.dve()
    e.tensor_copy(out[0:half], src[0:half])
    e.memset(out[half:P, :, 0:1], 0.0)
    s.end(e.tensor_copy(out[half:P, :, 1:TOKENS], src[half:P, :, 0:TOKENS - 1])); yield


def xpos_tables(w, d):
    T2, HD = TOKENS // P, 64
    n = T2 * HD
    at = [v2(w.extra[:, (4 * d + i) * n:(4 * d + i + 1) * n], HD) for i in range(4)]
    return {"q": at[0], "k": at[1]}, {"q": at[2], "k": at[3]}


def prepare_xpos(s, w):
    T2, HD = TOKENS // P, 64
    half = HD // 2
    e = s.dve()
    for d in range(2):
        cos_t, sin_t = xpos_tables(w, d)
        for n in "qk":
            g = w[f"{n}_scale{d}"]
            e.tensor_tensor(cos_t[n], v2(s.c[f"xpos_cos_{n}"], HD), over(g.unsqueeze(1), [P, T2, HD]), ALU.mult)
            for i in range(2):
                o, p = slice(half * i, half * i + half), slice(half - half * i, 2 * half - half * i)
                last = e.tensor_tensor(sin_t[n][:, :, o], v2(s.c[f"xpos_sin_{n}"], HD)[:, :, o],
                                       over(g[:, p].unsqueeze(1), [P, T2, half]), ALU.mult)
    s.end(last)


def local_layer(s, w, d, x):
    H, HD = 8, 64
    T2 = TOKENS // P
    inner = H * HD
    s.used = COLS
    h = s.take(COLS)
    yield from shift_tokens(s, x, h)
    mark = s.used
    half = HD // 2
    cos_t, sin_t = xpos_tables(w, d)
    chunks = {0: [(0, P)], 1: [(1, P), (2, 64)]}
    first_token = (0, 64, 192)
    q, k, v = s.take(inner // P, 2, P), s.take(inner // P, TOKENS), s.take(len(first_token), inner)
    tmp, tok = s.take(inner), s.take(inner)
    p, sums = s.take(2 * 2 * P), s.take(H)
    heads = lambda ap: v2(ap, HD)

    def rotated(s, bt, n, t, tmp, tok):
        col = 0 if n == "q" else inner
        mark = s.used
        ss = s.take(H)
        first = bt * TOKENS + t * P
        s.end(s.pe().matmul(s.a, h[:, first:first + P], w[f"wqkv{d}"][:, col:col + inner], start=True, stop=True)); yield
        s.end(s.act().activation(tmp, s.a, ACT.Square)); yield
        s.end(s.dve().tensor_reduce(ss, heads(tmp), AX, ALU.add)); yield
        s.end(s.dve().tensor_scalar(ss, ss, 1e-24, None, ALU.max)); yield
        yield ACT.Ln
        s.end(s.act().activation(ss, ss, ACT.Ln, scale=2.0 ** 24)); yield
        yield ACT.Exp
        s.end(s.act().activation(ss, ss, ACT.Exp, scale=-0.5, bias=s.c["eps"][:, 3:4])); yield
        s.end(s.dve().tensor_tensor(heads(tmp), heads(s.a), over(ss.unsqueeze(2), [P, H, HD]), ALU.mult)); yield
        e = s.dve()
        for i in range(2):
            o, pa = slice(half * i, half * i + half), slice(half - half * i, 2 * half - half * i)
            last = e.tensor_tensor(heads(tok)[:, :, o], heads(tmp)[:, :, pa],
                                   over(sin_t[n][:, t:t + 1, o], [P, H, half]), ALU.mult)
        s.end(last); yield
        s.end(s.pool().tensor_tensor(heads(tmp), heads(tmp), over(cos_t[n][:, t:t + 1, :], [P, H, HD]), ALU.mult)); yield
        s.end(s.pool().tensor_tensor(tok, tok, tmp, ALU.add)); yield
        e = s.pe()
        for i in range(inner // P):
            last = e.transpose(s.a[:, i * P:(i + 1) * P], tok[:, i * P:(i + 1) * P], s.c["ident"])
        s.end(last); yield
        s.used = mark

    def keys(b, bt, t, work):
        yield from rotated(b, bt, "k", t, *work)
        b.copy(k[:, :, t * P:(t + 1) * P], v2(b.a, P)); yield

    def values(b, bt, i, first):
        n = min(P, TOKENS - first)
        t0 = bt * TOKENS + first
        b.end(b.pe().matmul(b.a[0:n, :], h[:, t0:t0 + n], w[f"wqkv{d}"][:, 2 * inner:3 * inner], start=True, stop=True)); yield
        b.copy(v[0:n, i, :], b.a[0:n, :]); yield

    def pairs(b, t, mine, p, o):
        lo = 64 * t
        nk = P + 64 * t
        mask = s.m[f"band64_{t}"]
        m = b.take(2)
        S = b.a[:, 0:2 * nk].rearrange("p (i k) -> p i k", k=nk)
        for pair in mine:
            scores = v2(p[:, 0:2 * nk], nk)
            b.end(b.pe().matmul(S, s.m["ident"], over(mask.unsqueeze(1), [P, 2, nk]), start=True, stop=True)); yield
            e = b.pe()
            for i in range(2):
                last = e.matmul(S[:, i, :], q[:, pair, i, :], k[:, pair, lo:lo + nk], start=False, stop=True,
                                skip_group_check=True)
            b.end(last); yield
            b.end(b.dve().tensor_reduce(m, S, AX, ALU.max)); yield
            b.end(b.dve().tensor_scalar(m, m, -8.0, None, ALU.mult)); yield
            yield ACT.Exp
            e = b.act()
            for i in range(2):
                hh = 2 * pair + i
                last = e.activation(scores[:, i, :], S[:, i, :], ACT.Exp, bias=m[:, i:i + 1], scale=8.0,
                                    accum_out=sums[:, hh:hh + 1])
            b.end(last); yield
            width = len(chunks[t]) * P
            turned, pt = v2(b.a[:, 0:2 * width], width), v2(p[:, 0:2 * width], width)
            e = b.pe()
            at = list(reversed(range(len(chunks[t]))))
            for i in range(2):
                for c, (_, n) in enumerate(chunks[t]):
                    last = e.transpose(turned[0:n, i, at[c] * P:(at[c] + 1) * P], scores[:, i, c * P:c * P + n], s.c["ident"])
            b.end(last); yield
            b.copy(pt, turned); yield
            e = b.pe()
            for i in range(2):
                hc = slice((2 * pair + i) * HD, (2 * pair + i + 1) * HD)
                for c, (vc, n) in enumerate(chunks[t]):
                    last = e.matmul(b.a[i * HD:(i + 1) * HD, 0:P], v[0:n, vc, hc], pt[0:n, i, at[c] * P:(at[c] + 1) * P],
                                    start=(c == 0), stop=(c == len(chunks[t]) - 1), skip_group_check=True)
            b.end(last); yield
            b.copy(o[:, pair, :], b.a[:, 0:P]); yield

    def follow(*chains):
        for c in chains:
            yield from c

    for bt in range(PER_STREAM):
        at = s.used
        branches = [s.branch(i, H + 2) for i in range(2)]
        spare = q.rearrange("p a b c -> p (a b c)")
        works = [(tmp, tok), (spare[:, 0:inner], spare[:, inner:2 * inner])]
        yield from s.join(branches, [
            follow(keys(b, bt, i, works[i]), *[values(b, bt, c, first) for c, first in enumerate(first_token) if (c > 0) == i])
            for i, b in enumerate(branches)])
        s.used = at
        for t in range(T2):
            yield from rotated(s, bt, "q", t, tmp, tok)
            turned = v2(s.a, P)
            s.end(s.act().activation(q[:, :, 0, :], turned, ACT.Copy, scale=s.c["half_of_pair"][:, 0:1])); yield
            s.end(s.dve().tensor_scalar(q[:, :, 1, :], turned, s.c["half_of_pair"][:, 1:2], None, ALU.mult)); yield
            o = v2(tok, P)
            branches = [s.branch(i, H + 2) for i in range(2)]
            yield from s.join(branches, [pairs(b, t, range(i, H // 2, 2), (tmp, p)[i], o) for i, b in enumerate(branches)])
            s.used = at
            s.end(s.dve().reciprocal(sums, sums)); yield
            s.end(s.pe().transpose(s.a[0:H, 0:P], sums, s.c["ident"])); yield
            s.copy(tmp[0:H, 0:P], s.a[0:H, 0:P]); yield
            e = s.pe()
            for i in range(inner // P):
                last = e.matmul(s.a[:, i * P:(i + 1) * P], s.c["expand8"][:, i * P:(i + 1) * P], tmp[0:H, 0:P], start=True, stop=True)
            s.end(last); yield
            s.end(s.dve().tensor_tensor(tok, tok, s.a, ALU.mult)); yield
            e = s.pe()
            for i in range(inner // P):
                last = e.matmul(s.b[:, 0:P], w[f"wo{d}"][:, i * P:(i + 1) * P], o[:, i, :],
                                start=(i == 0), stop=(i == inner // P - 1))
            s.end(last); yield
            xs = x[:, bt * TOKENS + t * P:bt * TOKENS + (t + 1) * P]
            s.end(s.dve().tensor_tensor(xs, xs, s.b[:, 0:P], ALU.add)); yield
    s.used = mark
    yield from shift_tokens(s, x, h)
    yield from layer_norm(s, h, h, w[f"ln_g{d}"], w[f"ln_b{d}"])
    hid = w[f"w1{d}"].shape[-1] // 2
    sizes = [min(P, hid - i) for i in range(0, hid, P)]
    gate = s.take(COLS)
    for i, n in enumerate(sizes):
        ca, cg = i * P, hid + i * P
        s.end(s.pe().matmul(s.a[0:n, :], w[f"w1{d}"][:, cg:cg + n], h, start=True, stop=True)); yield
        yield ACT.Gelu
        s.end(s.act().activation(gate[0:n, :], s.a[0:n, :], ACT.Gelu, bias=w[f"b1g{d}"][0:n, i:i + 1])); yield
        s.end(s.pe().matmul(s.a[0:n, :], w[f"w1{d}"][:, ca:ca + n], h, start=True, stop=True)); yield
        s.end(s.dve().scalar_tensor_tensor(gate[0:n, :], s.a[0:n, :], w[f"b1a{d}"][0:n, i:i + 1], gate[0:n, :],
                                           ALU.add, ALU.mult)); yield
        s.end(s.pe().matmul(s.b, w[f"w2{d}"][0:n, i * P:(i + 1) * P], gate[0:n, :], start=(i == 0),
                            stop=(i == len(sizes) - 1))); yield
    s.end(s.dve().scalar_tensor_tensor(x, s.b, w[f"b2{d}"], x, ALU.add, ALU.add)); yield


def local_transformer(s, w):
    s.fresh()
    y = s.take(COLS)
    yield from layer_norm(s, s.x, y)
    for d in range(2):
        yield from local_layer(s, w, d, y)
    s.end(s.dve().tensor_tensor(s.x, s.x, y, ALU.add)); yield


def slot_memory(s, w):
    N, TOP = 64, 8
    B = PER_STREAM
    s.fresh()
    xn, alpha, x_tok, hT = s.take(COLS), s.take(TILES, N), s.take(TILES, P), s.take(COLS, parts=N)
    yield from layer_norm(s, s.x, xn)
    col = s.take(4)
    s.end(s.dve().tensor_reduce(col[:, 0:1], w["slots"], AX, ALU.add)); yield
    s.end(s.dve().tensor_scalar(col[:, 0:1], col[:, 0:1], 1.0 / N, None, ALU.mult)); yield
    s.end(s.pe().matmul(s.a[0:N, 0:1], w["w1s"], col[:, 0:1], start=True, stop=True)); yield
    s.end(s.dve().tensor_tensor(col[0:N, 1:2], w["b1"], s.a[0:N, 0:1], ALU.add)); yield
    s.end(s.dve().scalar_tensor_tensor(col[:, 2:3], w["tau"], -1.0, w["tau"], ALU.mult, ALU.max)); yield
    s.end(s.dve().tensor_scalar(col[:, 2:3], col[:, 2:3], 0.1, None, ALU.add)); yield
    s.end(s.dve().reciprocal(col[:, 2:3], col[:, 2:3])); yield
    s.end(s.pe().matmul(s.a[0:N, :], w["w1x"], xn, start=True, stop=True)); yield
    yield ACT.Gelu
    s.end(s.act().activation(hT, s.a[0:N, :], ACT.Gelu, bias=col[0:N, 1:2])); yield
    e = s.pe()
    for t in range(TILES):
        last = e.matmul(s.b[:, t * N:(t + 1) * N], hT[:, t * P:(t + 1) * P], w["w2"], start=True, stop=True)
    s.end(last); yield
    logits = s.take(TILES, N)
    s.end(s.dve().tensor_tensor(logits, over(w["b2"].unsqueeze(1), [P, TILES, N]), v2(s.b[:, 0:TILES * N], N), ALU.add)); yield
    s.end(s.dve().tensor_scalar(logits, logits, col[:, 2:3], None, ALU.mult)); yield
    top = yield from keep_top(s, logits, alpha, TOP, -1.5e38)
    s.end(s.dve().tensor_tensor(logits, logits, over(top[:, :, 0:1], [P, TILES, N]), ALU.subtract)); yield
    yield ACT.Exp
    s.end(s.act().activation(logits, logits, ACT.Exp)); yield
    s.end(s.dve().tensor_tensor(alpha, alpha, logits, ALU.mult)); yield
    yield from row_scale(s, alpha, TILES, N)
    e = s.pe()
    for t in range(TILES):
        last = e.transpose(s.a[:, t * P:(t + 1) * P], xn[:, t * P:(t + 1) * P], s.c["ident"])
    s.end(last); yield
    s.copy(x_tok, v2(s.a, P)); yield
    e = s.pe()
    for bt in range(B):
        for i in range(2):
            last = e.matmul(s.a[:, bt * N:(bt + 1) * N], x_tok[:, 2 * bt + i, :], alpha[:, 2 * bt + i, :], start=(i == 0), stop=(i == 1))
    for bt in range(B):
        for i in range(2):
            last = e.matmul(s.b[:, bt * N:(bt + 1) * N], s.c["ones"], alpha[:, 2 * bt + i, :], start=(i == 0), stop=(i == 1))
    s.end(last); yield
    M = B * N
    si, gh, gi, new, tmp = s.take(M), s.take(3, N), s.take(3, M), s.take(M), s.take(M)
    s.end(s.dve().tensor_scalar(si, s.b[:, 0:M], 1e-8, None, ALU.add)); yield
    s.end(s.dve().reciprocal(si, si)); yield
    s.end(s.dve().tensor_tensor(si, si, s.a[:, 0:M], ALU.mult)); yield
    e = s.pe()
    for i in range(3):
        last = e.matmul(s.a[:, i * M:(i + 1) * M], w["Wih"][:, i * P:(i + 1) * P], si, start=True, stop=True)
    for i in range(3):
        last = e.matmul(s.b[:, i * N:(i + 1) * N], w["Whh"][:, i * P:(i + 1) * P], w["slots"], start=True, stop=True)
    s.end(last); yield
    e = s.dve()
    for i in range(3):
        e.tensor_scalar(gi[:, i, :], s.a[:, i * M:(i + 1) * M], w["bih"][:, i:i + 1], None, ALU.add)
        last = e.tensor_scalar(gh[:, i, :], s.b[:, i * N:(i + 1) * N], w["bhh"][:, i:i + 1], None, ALU.add)
    s.end(last); yield
    e = s.dve()
    for i in range(2):
        last = e.tensor_tensor(v2(gi[:, i, :], N), v2(gi[:, i, :], N), over(gh[:, i:i + 1, :], [P, B, N]), ALU.add)
    s.end(last); yield
    yield ACT.Sigmoid
    s.end(s.act().activation(gi[:, 0:2, :], gi[:, 0:2, :], ACT.Sigmoid)); yield
    s.end(s.dve().tensor_tensor(v2(tmp, N), v2(gi[:, 0, :], N), over(gh[:, 2:3, :], [P, B, N]), ALU.mult)); yield
    s.end(s.dve().tensor_tensor(tmp, tmp, gi[:, 2, :], ALU.add)); yield
    yield ACT.Tanh
    s.end(s.act().activation(new, tmp, ACT.Tanh)); yield
    s.end(s.dve().tensor_tensor(v2(tmp, N), over(w["slots"].unsqueeze(1), [P, B, N]), v2(new, N), ALU.subtract)); yield
    s.end(s.dve().tensor_tensor(tmp, tmp, gi[:, 1, :], ALU.mult)); yield
    s.end(s.dve().tensor_tensor(new, new, tmp, ALU.add)); yield
    DQ = w["wq"].shape[-1]
    qk, vt, pr, prT = s.take(2, M, parts=DQ), s.take(B, P, parts=N), s.take(B, N, parts=N), s.take(B, N, parts=N)
    m = s.take(B, parts=N)
    e = s.pe()
    e.matmul(s.a[0:DQ, 0:M], w["wq"], new, start=True, stop=True)
    e.matmul(s.a[0:DQ, M:2 * M], w["wk"], new, start=True, stop=True)
    for bt in range(B):
        last = e.matmul(s.b[0:N, bt * P:(bt + 1) * P], new[:, bt * N:(bt + 1) * N], w["wv"], start=True, stop=True)
    s.end(last); yield
    e = s.act()
    e.activation(qk[:, 0, :], s.a[0:DQ, 0:M], ACT.Identity, bias=w["bq"])
    s.end(e.activation(qk[:, 1, :], s.a[0:DQ, M:2 * M], ACT.Identity, bias=w["bk"])); yield
    s.end(s.dve().tensor_tensor(vt, over(w["bv"][0:N].unsqueeze(1), [N, B, P]), v2(s.b[0:N, 0:B * P], P), ALU.add)); yield
    e = s.pe()
    for bt in range(B):
        last = e.matmul(s.a[0:N, bt * N:(bt + 1) * N], qk[:, 0, bt * N:(bt + 1) * N], qk[:, 1, bt * N:(bt + 1) * N], start=True, stop=True)
    s.end(last); yield
    S = v2(s.a[0:N, 0:M], N)
    s.end(s.dve().tensor_reduce(m, S, AX, ALU.max)); yield
    s.end(s.dve().tensor_scalar(m, m, -DQ ** -0.5, None, ALU.mult)); yield
    yield ACT.Exp
    e = s.act()
    for bt in range(B):
        last = e.activation(pr[:, bt, :], S[:, bt, :], ACT.Exp, bias=m[:, bt:bt + 1], scale=DQ ** -0.5)
    s.end(last); yield
    s.end(s.dve().tensor_reduce(m, pr, AX, ALU.add)); yield
    s.end(s.dve().reciprocal(m, m)); yield
    s.end(s.dve().tensor_tensor(pr, pr, over(m.unsqueeze(2), [N, B, N]), ALU.mult)); yield
    e = s.pe()
    for bt in range(B):
        last = e.transpose(s.b[0:N, bt * N:(bt + 1) * N], pr[:, bt, :], s.c["ident"][0:N, 0:N])
    s.end(last); yield
    s.copy(prT, v2(s.b[0:N, 0:M], N)); yield
    e = s.pe()
    for bt in range(B):
        last = e.matmul(s.a[:, bt * N:(bt + 1) * N], vt[:, bt, :], prT[:, bt, :], start=True, stop=True)
    s.end(last); yield
    s.end(s.dve().tensor_tensor(new, new, s.a[:, 0:M], ALU.add)); yield
    yield from layer_norm(s, new, new, w["ln_g"], w["ln_b"])
    e = s.pe()
    for bt in range(B):
        last = e.matmul(s.a[0:N, bt * P:(bt + 1) * P], new[:, bt * N:(bt + 1) * N], w["wvp"], start=True, stop=True)
    for t in range(TILES):
        last = e.transpose(s.b[0:N, t * P:(t + 1) * P], alpha[:, t, :], s.c["ident"])
    s.end(last); yield
    s.end(s.dve().tensor_tensor(vt, over(w["bvp"][0:N].unsqueeze(1), [N, B, P]), v2(s.a[0:N, 0:B * P], P), ALU.add)); yield
    s.copy(hT, s.b[0:N, :]); yield
    e = s.pe()
    for bt in range(B):
        c = slice(bt * TOKENS, (bt + 1) * TOKENS)
        last = e.matmul(s.a[:, c], vt[:, bt, :], hT[:, c], start=True, stop=True)
    s.end(last); yield
    s.copy(xn, s.a); yield
    s.end(s.pe().matmul(s.b, w["wo"], xn, start=True, stop=True)); yield
    s.end(s.dve().scalar_tensor_tensor(s.x, s.b, w["bo"], s.x, ALU.add, ALU.add)); yield


NETWORK = [
    ("L0_scan", lambda s, w: scan_block(s, w, conv=False, a_is_exp=False, clip=(0.001, 0.1))),
    ("L0_experts", expert_mix),
    ("L0_linear", linear_attention),
    ("L0_experts", expert_mix),
    ("L1_gla", gated_linear_attention),
    ("L1_local", local_transformer),
    ("L1_attn", lambda s, w: attention(s, w, latent=True, masked=False)),
    ("L1_local", local_transformer),
    ("L2_scan", lambda s, w: scan_block(s, w, conv=True, a_is_exp=True, clip=None)),
    ("L2_experts", expert_swiglu),
    ("L2_attn", lambda s, w: attention(s, w, latent=False, masked=True)),
    ("L2_experts", expert_swiglu),
    ("L3_blocks", block_attention),
    ("L3_slots", slot_memory),
    ("L3_gqa", grouped_query_attention),
    ("L3_slots", slot_memory),
]
SUCCESSORS = {"L0_experts": ("L2_experts",), "L1_local": ("L2_attn", "L3_blocks", "L3_slots", "L3_gqa")}


def build(nc, x_dram, out_dram, packed_dram, where, network):
    with ExitStack() as ctx:
        core = Core(nc, ctx)
        engines = core.engines
        groups = ["constants"] + [g for i, (g, _) in enumerate(network) if g not in [n for n, _ in network[:i]]]
        for g in groups + ["x"]:
            core.sems[f"load_{g}"] = ctx.enter_context(nc.semaphore(f"load_{g}"))
        stored = ctx.enter_context(nc.semaphore("stored"))
        width = {g: packed_dram[g].shape[1] for g in groups}
        weights = {}
        after = {g: first for first, later in SUCCESSORS.items() for g in later if first in groups and g in groups}
        for g in groups:
            if g not in after:
                followers = [f for f in groups if after.get(f) == g]
                buf = ctx.enter_context(nc.sbuf_tensor(f"w_{g}", [P, max(width[g], sum(width[f] for f in followers))], F32))
                weights[g] = Weights(buf[:, 0:width[g]], where[g])
                at = 0
                for f in followers:
                    weights[f] = Weights(buf[:, at:at + width[f]], where[f])
                    at += width[f]
        x = ctx.enter_context(nc.sbuf_tensor("x", [P, BATCHES * TOKENS], F32))
        scratch = ctx.enter_context(nc.sbuf_tensor("scratch", [P, N_STREAMS * SCRATCH], F32))
        psum = ctx.enter_context(nc.psum_tensor("psum", [P, N_STREAMS * 2 * BANK], F32))

        def load(g):
            nc.sync.dma_start(weights[g].buf, packed_dram[g]).then_inc(core.sems[f"load_{g}"], 16)

        n = packed_dram["masks"].shape[1]
        core.sems["load_masks"] = ctx.enter_context(nc.semaphore("load_masks"))
        bf16_masks = Weights(ctx.enter_context(nc.sbuf_tensor("bf16_masks", [P, n], BF16)), where["masks"])
        load("constants")
        nc.sync.dma_start(x[:, :], x_dram).then_inc(core.sems["load_x"], 16)
        staged = scratch[:, (N_STREAMS - 1) * SCRATCH:][:, 0:n]
        nc.sync.dma_start(staged, packed_dram["masks"]).then_inc(core.sems["load_masks"], 16)
        for g in groups[1:]:
            if g not in after:
                load(g)

        streams = [Stream(core, i, x[:, i * COLS:(i + 1) * COLS], scratch[:, i * SCRATCH:(i + 1) * SCRATCH],
                          psum[:, i * 2 * BANK:(i + 1) * 2 * BANK], weights["constants"], bf16_masks) for i in range(N_STREAMS)]
        streams[0].needs("constants")
        streams[0].needs("x")
        streams[0].needs("masks")
        streams[-1].end(streams[-1].act().activation(bf16_masks.buf[:, :], staged, ACT.Copy))
        core.wait("pe", *streams[-1].last[0])
        local = weights.get("L1_local")
        if local:
            local.extra = ctx.enter_context(nc.sbuf_tensor("xpos", [P, 8 * TOKENS // P * 64], F32))
        last_use = {g: i for i, (g, _) in enumerate(network)}
        passed = dict.fromkeys(SUCCESSORS, 0)

        def through(s):
            for i, (g, block) in enumerate(network):
                s.needs(g)
                if local and g == "L1_local" and not local.prepared:
                    prepare_xpos(s, local)
                    local.prepared = s.last
                if g == "L1_local":
                    s.wait_all(*local.prepared[0])
                yield from block(s, weights[g])
                if g in SUCCESSORS and i == last_use[g]:
                    core.wait("sp", *s.last[0])
                    passed[g] += 1
                    if passed[g] == N_STREAMS:
                        for f in SUCCESSORS[g]:
                            if after.get(f) == g:
                                load(f)

        running = {s: through(s) for s in streams}
        while running:
            s = min(running, key=Stream.ready)
            try:
                s.wants = next(running[s])
            except StopIteration:
                del running[s]
        for i, s in enumerate(streams):
            core.wait("sp", *s.last[0])
            nc.sync.dma_start(out_dram[:, i * COLS:(i + 1) * COLS], s.x).then_inc(stored, 16)
        nc.sync.wait_ge(stored, 16 * N_STREAMS)


def kernel(**inputs):
    import concourse.bacc as bacc
    from concourse.bass_utils import run_bass_kernel_spmd

    p = {k: np.asarray(v) for k, v in inputs.items()}
    packs = {"constants": pack(constants()), "masks": pack(masks()), **{g: pack(parts) for g, parts in layouts(p).items()}}
    x = np.ascontiguousarray(p["L0_attn_a_x"].reshape(BATCHES * TOKENS, P).T)
    nc = bacc.Bacc("TRN2", target_bir_lowering=False, num_devices=1)
    arrays = {"x_dram": x, **{f"{g}_dram": a for g, (a, _) in packs.items()}}
    aps = {n: nc.dram_tensor(n, a.shape, F32, kind="ExternalInput").ap() for n, a in arrays.items()}
    out = nc.dram_tensor("out_dram", x.shape, F32, kind="ExternalOutput").ap()
    build(nc, aps["x_dram"], out, {g: aps[f"{g}_dram"] for g in packs}, {g: w for g, (_, w) in packs.items()}, NETWORK)
    r = run_bass_kernel_spmd(nc, [arrays], core_ids=[0])
    y = r.results[0]["out_dram"]
    return np.ascontiguousarray(y.T).reshape(BATCHES, TOKENS, P)
```
